# Optimizing a Trainium2 kernel written in Bass

```python
import numpy as np
import jax
import jax.numpy as jnp

def _softmax(x, axis=-1):
    return jax.nn.softmax(x, axis=axis)

def _gelu(x):
    return jax.nn.gelu(x, approximate=True)

def _silu(x):
    return jax.nn.silu(x)

def _sigmoid(x):
    return jax.nn.sigmoid(x)

def _layernorm(x, axis=-1, eps=1e-05):
    m = jnp.mean(x, axis=axis, keepdims=True)
    v = jnp.var(x, axis=axis, keepdims=True)
    return (x - m) / jnp.sqrt(v + eps)

def _scatter_add(tgt, idx, src, axis=0):
    return tgt.at[idx].add(src)

def _segment_sum(src, seg, n):
    return jax.ops.segment_sum(src, seg, n)
kernel_name = 'mk_seq_postln_d2_jaxref_r8_fa47ae'

def setup_inputs(seed: int=0):
    np.random.seed(seed)
    _w = jnp.asarray

    def _L0_attn_setup():
        import jax, jax.numpy as jnp
        import numpy as np
        B, L, H, I, K, G = (2, 512, 128, 256, 4, 8)
        EPS = 1e-05

        def _layernorm(x, g, b):
            m = x.mean(-1, keepdims=True)
            v = jnp.var(x, axis=-1, keepdims=True)
            return (x - m) * jax.lax.rsqrt(v + EPS) * g + b
        key = jax.random.key(seed)
        ks = jax.random.split(key, 8)
        s = 0.02
        return {'hidden_states': jax.random.normal(ks[0], (B, L, H), jnp.float32), 'in_proj_w': jax.random.normal(ks[1], (2 * I, H), jnp.float32) * s, 'conv_w': jax.random.normal(ks[2], (I, I // G, K), jnp.float32) * s, 'conv_b': jax.random.normal(ks[3], (I,), jnp.float32) * s, 'ln_g': jnp.ones((I,), jnp.float32), 'ln_b': jnp.zeros((I,), jnp.float32), 'fc_w': jax.random.normal(ks[4], (H, I), jnp.float32) * s, 'fc_b': jnp.zeros((H,), jnp.float32), 'cproj_w': jax.random.normal(ks[5], (I, H), jnp.float32) * s, 'cproj_b': jnp.zeros((I,), jnp.float32), 'out_w': jax.random.normal(ks[6], (H, I), jnp.float32) * s}
    _L0_attn_in = _L0_attn_setup()

    def _L0_ffn_setup():
        import jax, jax.numpy as jnp
        import numpy as np
        TOP_K = 2

        def _route(x2d, gate_w, num_experts, top_k):
            scores = jax.nn.softmax((x2d @ gate_w.T).astype(jnp.float32), axis=1)
            top_scores, sel = jax.lax.top_k(scores, top_k)
            sel_flat = sel.reshape(-1)
            counts = jnp.bincount(sel_flat, length=num_experts)
            order = jnp.argsort(sel_flat, stable=True)
            top_scores_sorted = top_scores.reshape(-1)[order]
            token_idx = order // top_k
            return (top_scores_sorted, token_idx, counts)

        def _grouped_swiglu(xr, w1, w2, w3, eid):
            out = jnp.zeros((xr.shape[0], w2.shape[-1]), dtype=xr.dtype)
            for e in range(w1.shape[0]):
                xe = jnp.where((eid == e)[:, None], xr, 0.0)
                h = jax.nn.silu(xe @ w1[e]) * (xe @ w3[e])
                out = out + h @ w2[e]
            return out
        key = jax.random.key(seed)
        ks = jax.random.split(key, 5)
        bs, slen, dim, hidden, E = (2, 256, 128, 352, 8)
        x = jax.random.normal(ks[0], (bs, slen, dim), dtype=jnp.float32)
        gate_w = jax.random.normal(ks[1], (E, dim), dtype=jnp.float32) * 0.02
        w1 = jax.random.normal(ks[2], (E, dim, hidden), dtype=jnp.float32) * 0.02
        w2 = jax.random.normal(ks[3], (E, hidden, dim), dtype=jnp.float32) * 0.02
        w3 = jax.random.normal(ks[4], (E, dim, hidden), dtype=jnp.float32) * 0.02
        return {'x': x, 'gate_w': gate_w, 'w1': w1, 'w2': w2, 'w3': w3}
    _L0_ffn_in = _L0_ffn_setup()

    def _L1_attn_setup():
        import jax, jax.numpy as jnp
        import numpy as np
        B, N, D = (4, 512, 128)
        H, M = (16, 32)
        DH = D // H

        def _feature_map(t, omega):
            t_omega = jnp.einsum('bhnd,dm->bhnm', t, omega)
            norm_sq = 0.5 * jnp.sum(t * t, axis=-1, keepdims=True)
            return jnp.exp(t_omega - norm_sq)
        key = jax.random.key(seed)
        ks = jax.random.split(key, 6)
        x = jax.random.normal(ks[0], (B, N, D), dtype=jnp.float32)
        Wqkv = jax.random.normal(ks[1], (D, 3 * D), dtype=jnp.float32) * 0.02
        bqkv = jnp.zeros((3 * D,), dtype=jnp.float32)
        Wout = jax.random.normal(ks[2], (D, D), dtype=jnp.float32) * 0.02
        bout = jnp.zeros((D,), dtype=jnp.float32)
        omega = jax.random.normal(ks[3], (DH, M), dtype=jnp.float32)
        return {'x': x, 'Wqkv': Wqkv, 'bqkv': bqkv, 'Wout': Wout, 'bout': bout, 'omega': omega}
    _L1_attn_in = _L1_attn_setup()

    def _L1_ffn_setup():
        import jax, jax.numpy as jnp
        import numpy as np
        D_IN, D_HID = (128, 512)

        def _ternary(key, shape):
            return jax.random.randint(key, shape, -1, 2).astype(jnp.float32)

        def _tlin(x, w, s):
            return jnp.einsum('bsi,oi->bso', x, w) * s
        key = jax.random.key(seed)
        ks = jax.random.split(key, 12)
        inv = lambda fan: 1.0 / np.sqrt(fan).astype(np.float32)
        return {'x': jax.random.normal(ks[0], (4, 256, D_IN), dtype=jnp.float32), 'w1_w': _ternary(ks[1], (D_HID, D_IN)), 'w1_s': jax.random.uniform(ks[2], (D_HID,), dtype=jnp.float32) * inv(D_IN), 'w2_w': _ternary(ks[3], (D_HID, D_IN)), 'w2_s': jax.random.uniform(ks[4], (D_HID,), dtype=jnp.float32) * inv(D_IN), 'h1_w': _ternary(ks[5], (D_HID, D_HID)), 'h1_s': jax.random.uniform(ks[6], (D_HID,), dtype=jnp.float32) * inv(D_HID), 'h2_w': _ternary(ks[7], (D_HID, D_HID)), 'h2_s': jax.random.uniform(ks[8], (D_HID,), dtype=jnp.float32) * inv(D_HID), 'w3_w': _ternary(ks[9], (D_IN, D_HID)), 'w3_s': jax.random.uniform(ks[10], (D_IN,), dtype=jnp.float32) * inv(D_HID)}
    _L1_ffn_in = _L1_ffn_setup()
    _d = {'L0_attn_hidden_states': _L0_attn_in['hidden_states'], 'L0_attn_in_proj_w': _L0_attn_in['in_proj_w'], 'L0_attn_conv_w': _L0_attn_in['conv_w'], 'L0_attn_conv_b': _L0_attn_in['conv_b'], 'L0_attn_ln_g': _L0_attn_in['ln_g'], 'L0_attn_ln_b': _L0_attn_in['ln_b'], 'L0_attn_fc_w': _L0_attn_in['fc_w'], 'L0_attn_fc_b': _L0_attn_in['fc_b'], 'L0_attn_cproj_w': _L0_attn_in['cproj_w'], 'L0_attn_cproj_b': _L0_attn_in['cproj_b'], 'L0_attn_out_w': _L0_attn_in['out_w'], 'L0_ffn_gate_w': _L0_ffn_in['gate_w'], 'L0_ffn_w1': _L0_ffn_in['w1'], 'L0_ffn_w2': _L0_ffn_in['w2'], 'L0_ffn_w3': _L0_ffn_in['w3'], 'L1_attn_Wqkv': _L1_attn_in['Wqkv'], 'L1_attn_bqkv': _L1_attn_in['bqkv'], 'L1_attn_Wout': _L1_attn_in['Wout'], 'L1_attn_bout': _L1_attn_in['bout'], 'L1_attn_omega': _L1_attn_in['omega'], 'L1_ffn_w1_w': _L1_ffn_in['w1_w'], 'L1_ffn_w1_s': _L1_ffn_in['w1_s'], 'L1_ffn_w2_w': _L1_ffn_in['w2_w'], 'L1_ffn_w2_s': _L1_ffn_in['w2_s'], 'L1_ffn_h1_w': _L1_ffn_in['h1_w'], 'L1_ffn_h1_s': _L1_ffn_in['h1_s'], 'L1_ffn_h2_w': _L1_ffn_in['h2_w'], 'L1_ffn_h2_s': _L1_ffn_in['h2_s'], 'L1_ffn_w3_w': _L1_ffn_in['w3_w'], 'L1_ffn_w3_s': _L1_ffn_in['w3_s']}
    _x0 = _d['L0_attn_hidden_states']
    _d['L0_attn_hidden_states'] = jax.random.normal(jax.random.fold_in(jax.random.key(seed), 1), (8, 256, 128), dtype=_x0.dtype)
    del _x0
    return _d

def reference(L0_attn_hidden_states, L0_attn_in_proj_w, L0_attn_conv_w, L0_attn_conv_b, L0_attn_ln_g, L0_attn_ln_b, L0_attn_fc_w, L0_attn_fc_b, L0_attn_cproj_w, L0_attn_cproj_b, L0_attn_out_w, L0_ffn_gate_w, L0_ffn_w1, L0_ffn_w2, L0_ffn_w3, L1_attn_Wqkv, L1_attn_bqkv, L1_attn_Wout, L1_attn_bout, L1_attn_omega, L1_ffn_w1_w, L1_ffn_w1_s, L1_ffn_w2_w, L1_ffn_w2_s, L1_ffn_h1_w, L1_ffn_h1_s, L1_ffn_h2_w, L1_ffn_h2_s, L1_ffn_w3_w, L1_ffn_w3_s):

    def _L0_attn_ref(hidden_states, in_proj_w, conv_w, conv_b, ln_g, ln_b, fc_w, fc_b, cproj_w, cproj_b, out_w):
        import jax, jax.numpy as jnp
        import numpy as np
        B, L, H, I, K, G = (2, 512, 128, 256, 4, 8)
        EPS = 1e-05

        def _layernorm(x, g, b):
            m = x.mean(-1, keepdims=True)
            v = jnp.var(x, axis=-1, keepdims=True)
            return (x - m) * jax.lax.rsqrt(v + EPS) * g + b
        p = hidden_states @ in_proj_w.T
        h, gate = (p[..., :I], p[..., I:])
        gate = jax.nn.silu(gate)
        hc = jnp.transpose(h, (0, 2, 1))
        conv = jax.lax.conv_general_dilated(hc, conv_w, window_strides=(1,), padding=[(K - 1, 0)], feature_group_count=G, dimension_numbers=('NCH', 'OIH', 'NCH'))
        conv = conv + conv_b[None, :, None]
        h = jnp.transpose(conv, (0, 2, 1)) * gate
        residual = h
        hn = _layernorm(h, ln_g, ln_b)
        m = jax.nn.silu(hn @ fc_w.T + fc_b) @ cproj_w.T + cproj_b
        h = m + residual
        return h @ out_w.T

    def _L0_ffn_ref(x, gate_w, w1, w2, w3):
        import jax, jax.numpy as jnp
        import numpy as np
        TOP_K = 2

        def _route(x2d, gate_w, num_experts, top_k):
            scores = jax.nn.softmax((x2d @ gate_w.T).astype(jnp.float32), axis=1)
            top_scores, sel = jax.lax.top_k(scores, top_k)
            sel_flat = sel.reshape(-1)
            counts = jnp.bincount(sel_flat, length=num_experts)
            order = jnp.argsort(sel_flat, stable=True)
            top_scores_sorted = top_scores.reshape(-1)[order]
            token_idx = order // top_k
            return (top_scores_sorted, token_idx, counts)

        def _grouped_swiglu(xr, w1, w2, w3, eid):
            out = jnp.zeros((xr.shape[0], w2.shape[-1]), dtype=xr.dtype)
            for e in range(w1.shape[0]):
                xe = jnp.where((eid == e)[:, None], xr, 0.0)
                h = jax.nn.silu(xe @ w1[e]) * (xe @ w3[e])
                out = out + h @ w2[e]
            return out
        bs, slen, dim = x.shape
        E, top_k = (gate_w.shape[0], TOP_K)
        x2d = x.reshape(bs * slen, dim)
        top_scores, token_idx, counts = _route(x2d, gate_w, E, top_k)
        routed_in = (x2d[token_idx].astype(jnp.float32) * top_scores[:, None]).astype(x.dtype)
        Tr = bs * slen * top_k
        eid = jnp.repeat(jnp.arange(E), counts, total_repeat_length=Tr)
        routed_out = _grouped_swiglu(routed_in, w1, w2, w3, eid)
        out = jnp.zeros((bs * slen, dim), dtype=x.dtype).at[token_idx].add(routed_out)
        return out.reshape(bs, slen, dim)

    def _L1_attn_ref(x, Wqkv, bqkv, Wout, bout, omega):
        import jax, jax.numpy as jnp
        import numpy as np
        B, N, D = (4, 512, 128)
        H, M = (16, 32)
        DH = D // H

        def _feature_map(t, omega):
            t_omega = jnp.einsum('bhnd,dm->bhnm', t, omega)
            norm_sq = 0.5 * jnp.sum(t * t, axis=-1, keepdims=True)
            return jnp.exp(t_omega - norm_sq)
        b, n, d = x.shape
        qkv = x @ Wqkv + bqkv
        q, k, v = jnp.split(qkv, 3, axis=-1)

        def to_heads(t):
            return t.reshape(b, n, H, DH).transpose(0, 2, 1, 3)
        q, k, v = (to_heads(q), to_heads(k), to_heads(v))
        q_prime = _feature_map(q, omega)
        k_prime = _feature_map(k, omega)
        k_sum = jnp.sum(k_prime, axis=2)
        denominator = jnp.einsum('bhnm,bhm->bhn', q_prime, k_sum)[..., None]
        k_v = jnp.einsum('bhnm,bhnd->bhmd', k_prime, v)
        numerator = jnp.einsum('bhnm,bhmd->bhnd', q_prime, k_v)
        out = numerator / (denominator + 1e-06)
        out = out.transpose(0, 2, 1, 3).reshape(b, n, d)
        return out @ Wout + bout

    def _L1_ffn_ref(x, w1_w, w1_s, w2_w, w2_s, h1_w, h1_s, h2_w, h2_s, w3_w, w3_s):
        import jax, jax.numpy as jnp
        import numpy as np
        D_IN, D_HID = (128, 512)

        def _ternary(key, shape):
            return jax.random.randint(key, shape, -1, 2).astype(jnp.float32)

        def _tlin(x, w, s):
            return jnp.einsum('bsi,oi->bso', x, w) * s
        h = jax.nn.silu(_tlin(x, w1_w, w1_s)) * _tlin(x, w2_w, w2_s)
        h = jax.nn.gelu(_tlin(h, h1_w, h1_s), approximate=False)
        h = jax.nn.gelu(_tlin(h, h2_w, h2_s), approximate=False)
        return _tlin(h, w3_w, w3_s)
    x = L0_attn_hidden_states
    x = _layernorm(x + _L0_attn_ref(x, L0_attn_in_proj_w, L0_attn_conv_w, L0_attn_conv_b, L0_attn_ln_g, L0_attn_ln_b, L0_attn_fc_w, L0_attn_fc_b, L0_attn_cproj_w, L0_attn_cproj_b, L0_attn_out_w), axis=-1)
    x = _layernorm(x + _L0_ffn_ref(x, L0_ffn_gate_w, L0_ffn_w1, L0_ffn_w2, L0_ffn_w3), axis=-1)
    x = _layernorm(x + _L1_attn_ref(x, L1_attn_Wqkv, L1_attn_bqkv, L1_attn_Wout, L1_attn_bout, L1_attn_omega), axis=-1)
    x = _layernorm(x + _L1_ffn_ref(x, L1_ffn_w1_w, L1_ffn_w1_s, L1_ffn_w2_w, L1_ffn_w2_s, L1_ffn_h1_w, L1_ffn_h1_s, L1_ffn_h2_w, L1_ffn_h2_s, L1_ffn_w3_w, L1_ffn_w3_s), axis=-1)
    return x

_drawn_inputs = setup_inputs


def setup_inputs(seed=0):
    import zlib

    import numpy as np

    out = dict(_drawn_inputs(seed))
    spreads = {'L0_attn_ln_g': (1.0, 0.2),
     'L0_attn_ln_b': (0.0, 0.1),
     'L0_attn_fc_b': (0.0, 0.1),
     'L0_attn_cproj_b': (0.0, 0.1),
     'L1_attn_bqkv': (0.0, 0.1),
     'L1_attn_bout': (0.0, 0.1)}
    factors = {}
    for name, (base, spread) in spreads.items():
        noise = np.random.default_rng([zlib.crc32(name.encode()), seed]).standard_normal(out[name].shape)
        drawn = base * np.exp(spread * noise) if base else spread * noise
        out[name] = jnp.asarray(drawn.astype(out[name].dtype))
    for name, factor in factors.items():
        out[name] = (out[name] * factor).astype(out[name].dtype)
    return out
```

```python
import numpy as np
import concourse.bass as bass
from concourse import mybir
from contextlib import ExitStack

P = 128
BATCHES, SEQ, D = 8, 256, 128
TOKENS = BATCHES * SEQ
TILES = SEQ // P
INNER, TAPS, GROUPS = 256, 4, 8
PAD = TAPS - 1
EXPERTS, TOP_K, HIDDEN = 8, 2, 352
HIDDEN_TILES = -(-HIDDEN // P)
SLOT_TILES = TOKENS * TOP_K // P + EXPERTS - 1
DUMMY_TILES = EXPERTS - 1
REGION = TOKENS
ROWS = EXPERTS * REGION + DUMMY_TILES * P
HEADS, FEATS = 16, 32
HEAD_DIM = D // HEADS
GROUP_HEADS = P // FEATS
HEAD_GROUPS = HEADS // GROUP_HEADS
FF = 512
FF_TILES = FF // P
CHUNK = 512
CHUNKS = TOKENS // CHUNK
CHUNK_TILES = CHUNK // P
FLY = 3
STORE_LAG = 5
EPS = 1e-5

C_IDENT, C_BEFORE, C_KVMASK = 0, P, 2 * P
C_IOTA = 3 * P
C_BASE = C_IOTA + EXPERTS
C_UPTO = C_BASE + EXPERTS
C_TILE = C_UPTO + EXPERTS * EXPERTS
C_ROW = C_TILE + SLOT_TILES
C_ALL = C_ROW + SLOT_TILES


def steps(engine, count, lag, step):
    for i in range(lag + 1):
        step(i)
    with engine.Fori(lag + 1, count) as i:
        step(i)
    for i in range(count, count + lag):
        step(i)


def alone(engine, carrier):
    engine.sem_inc(carrier, 1)


def live(n, count):
    return not isinstance(n, int) or 0 <= n < count


def wait(engine, semaphore, value):
    if not isinstance(value, int) or value > 0:
        engine.wait_ge(semaphore, value)


def build(nc, A, out):
    fp32, f32r, bf16 = mybir.dt.float32, mybir.dt.float32r, mybir.dt.bfloat16
    u32, i32 = mybir.dt.uint32, mybir.dt.int32
    ALU, ACT, AX = mybir.AluOpType, mybir.ActivationFunctionType, mybir.AxisListType

    ctx = ExitStack()
    with ctx:
        def sb(name, shape, dt=fp32):
            return ctx.enter_context(nc.sbuf_tensor("sb_" + name, shape, dt))

        def sems(prefix, names):
            return {n: ctx.enter_context(nc.semaphore(f"{prefix}_{n}")) for n in names.split()}

        routed = nc.dram_tensor("routed", [ROWS, D], fp32).ap()
        answers = nc.dram_tensor("answers", [SLOT_TILES * P, D], fp32).ap()

        const = sb("const", [P, C_ALL])
        ident = const[:, C_IDENT:C_IDENT + P]
        x_kept = sb("x_kept", [P, BATCHES, TILES * D])
        x_in = sb("x_in", [P, BATCHES, TILES * D])
        xT_in = sb("xT_in", [P, BATCHES, PAD + SEQ])
        w_h = sb("w_h", [P, 2, D])
        w_gate = sb("w_gate", [P, INNER])
        conv_bd = sb("conv_bd", [P, 2, TAPS * P])
        conv_b = sb("conv_b", [P, INNER])
        fc_wT = sb("fc_wT", [P, 2, D])
        ln_gb = sb("ln_gb", [P, 4])
        fc_b = sb("fc_b", [P, 1])
        cproj = sb("cproj", [P, 2, D])
        cproj_b = sb("cproj_b", [P, 2])
        out_wT = sb("out_wT", [P, 2, D])
        gate_wT = sb("gate_wT", [P, EXPERTS])
        w13 = sb("w13", [P, 2, 2 * HIDDEN])
        w2 = sb("w2", [P, EXPERTS, HIDDEN_TILES, D])
        qk_w = sb("qk_w", [P, 4, P])
        qk_b = sb("qk_b", [P, 4])
        wv = sb("wv", [P, D])
        bv = sb("bv", [P, D])
        omega = sb("omega", [P, 2 * P])
        wout = sb("wout", [P, D])
        bout = sb("bout", [P, D])
        ff_in = conv_bd[:, :, :]
        ff_s = sb("ff_s", [P, 4, FF_TILES])
        ff_out = sb("ff_out", [P, FF_TILES, D])
        ff_out_s = sb("ff_out_s", [P, D])

        def room(tile):
            flat = tile[:, :, :].rearrange("p b t -> p (b t)")
            return flat[:, 0:FF_TILES * CHUNK].rearrange("p (m t) -> p m t", t=CHUNK)
        ff_h = [room(x_in), room(xT_in)]

        before = sb("before", [P, P], bf16)
        ones_bf = sb("ones_bf", [P, P], bf16)
        ones = sb("ones", [P, FEATS])
        zeros = sb("zeros", [P, D])
        minus_half = sb("minus_half", [P, TILES])
        eps = sb("eps", [P, CHUNK_TILES])
        euler = sb("euler", [P, TILES * EXPERTS])
        front_hi = sb("front_hi", [P, TAPS + 1, INNER], f32r)
        front_lo = sb("front_lo", [P, TAPS + 1, INNER], f32r)
        fc_g = sb("fc_g", [P, 2, D])
        fc_bias = sb("fc_bias", [P, 1])
        cproj_bb = sb("cproj_bb", [P, 2, P])
        mid_out = sb("mid_out", [P, D])
        out_bias = sb("out_bias", [P, D])
        w13_hi = sb("w13_hi", [P, EXPERTS, 2 * HIDDEN], f32r)
        w13_lo = sb("w13_lo", [P, EXPERTS, 2 * HIDDEN], f32r)
        qk_hi, qk_lo = sb("qk_hi", [P, 4, P], f32r), sb("qk_lo", [P, 4, P], f32r)
        om_hi, om_lo = sb("om_hi", [P, 2 * P], f32r), sb("om_lo", [P, 2 * P], f32r)
        fh_hi, fh_lo = sb("fh_hi", [P, 2 * FF_TILES, FF], f32r), sb("fh_lo", [P, 2 * FF_TILES, FF], f32r)
        ff_out_w = sb("ff_out_w", [P, FF_TILES, D])

        xT_hi, xT_lo = sb("xT_hi", [P, PAD + SEQ], f32r), sb("xT_lo", [P, PAD + SEQ], f32r)
        work = sb("work", [P, 4, TILES * INNER])
        gate, conv, h, hn = (work[:, n, :].rearrange("p (t f) -> p t f", f=INNER) for n in range(4))
        hT = sb("hT", [P, TILES, 2 * P])
        hnT = sb("hnT", [P, 2, SEQ])
        mid = sb("mid", [P, SEQ])
        res = sb("res", [P, TILES * D])
        x1 = sb("x1", [P, TILES * D])
        x1T = sb("x1T", [P, SEQ])
        stats = sb("stats", [P, CHUNK_TILES, 6])
        mv = sb("mv", [P, CHUNK_TILES, 2])
        veps = sb("veps", [P, CHUNK_TILES])
        rstd = sb("rstd", [P, CHUNK_TILES])
        stats_h = sb("stats_h", [P, TILES, 6])
        mv_h = sb("mv_h", [P, TILES, 2])
        veps_h = sb("veps_h", [P, TILES])
        rstd_h = sb("rstd_h", [P, TILES])
        top = sb("top", [P, TILES, EXPERTS])
        top_at = sb("top_at", [P, TILES, EXPERTS], u32)
        below = sb("below", [P, TILES, EXPERTS])
        exps = sb("exps", [P, TILES, EXPERTS])
        denom = sb("denom", [P, TILES])
        rdenom = sb("rdenom", [P, TILES])
        score = sb("score", [P, TILES, TOP_K])
        chosen_at = sb("chosen_at", [P, TILES, TOP_K])
        chosen = sb("chosen", [P, BATCHES, TILES * TOP_K, EXPERTS])
        either = sb("either", [P, TILES, EXPERTS], bf16)
        earlier = sb("earlier", [P, TILES, EXPERTS], bf16)
        rank = sb("rank", [P, TILES, EXPERTS])
        rank_of = sb("rank_of", [P, TILES * TOP_K, EXPERTS])
        row_f = sb("row_f", [P, TILES * TOP_K])
        rows_f = sb("rows_f", [P, BATCHES, TILES * TOP_K])
        row = sb("row", [P, TILES * TOP_K], u32)
        row_all = sb("row_all", [P, BATCHES, TILES * TOP_K], u32)
        xs = sb("xs", [P, TILES * TOP_K, D])

        n_tiles_f = sb("n_tiles_f", [P, EXPERTS])
        n_tiles_i = sb("n_tiles_i", [P, EXPERTS], i32)
        n_tiles_s = sb("n_tiles_s", [P, EXPERTS], i32)
        n_tiles = sb("n_tiles", [P, EXPERTS])
        upto_p = sb("upto_p", [P, EXPERTS, EXPERTS])
        upto = sb("upto", [P, EXPERTS])
        skip_rows = sb("skip_rows", [P, EXPERTS])
        past = sb("past", [P, SLOT_TILES, EXPERTS])
        past_rows = sb("past_rows", [P, SLOT_TILES, EXPERTS])
        shift_r = sb("shift_r", [P, EXPERTS])
        shift = sb("shift", [P, EXPERTS])
        shift_of = sb("shift_of", [P, BATCHES * TILES * TOP_K])
        expert_f = sb("expert_f", [P, SLOT_TILES])
        start_f = sb("start_f", [P, SLOT_TILES])
        start_f2 = sb("start_f2", [P, SLOT_TILES])
        expert_t = sb("expert_t", [P, SLOT_TILES], i32)
        start_t = sb("start_t", [P, SLOT_TILES], i32)

        rows_in = sb("rows_in", [P, FLY, D])
        rT_hi, rT_lo = sb("rT_hi", [P, FLY, P], f32r), sb("rT_lo", [P, FLY, P], f32r)
        hid_room, hidT_room, act1_room = (sb(n, [P, FLY * HIDDEN_TILES * P]) for n in ("hid_room", "hidT_room", "act1_room"))
        hid, hidT = (r[:, :].rearrange("p (j f) -> p j f", j=FLY) for r in (hid_room, hidT_room))
        act1 = act1_room[:, 0:FLY * HIDDEN].rearrange("p (j f) -> p j f", j=FLY)
        rows_out = sb("rows_out", [P, FLY, D])

        row_now = sb("row_now", [P, TILES * TOP_K], u32)
        got = hT[:, :, :].rearrange("p t (k d) -> p t k d", d=D)
        kv, kvT = (hnT[:, n, :].rearrange("p (a f) -> p a f", f=P) for n in range(2))
        sum1, v_tok = (work[:, n, 0:SEQ].rearrange("p (t d) -> p t d", d=D) for n in range(2))
        x2, x2T = work[:, 0, SEQ:], work[:, 1, SEQ:]
        den, rden = work[:, 2, 0:SEQ], work[:, 2, SEQ:]
        att, x3 = work[:, 3, 0:SEQ], work[:, 3, SEQ:]
        x2T_hi, x2T_lo = xT_hi[:, 0:SEQ], xT_lo[:, 0:SEQ]
        st = hid_room[:, 0:4 * SEQ].rearrange("p (s t) -> p s t", t=SEQ)
        st_hi, st_lo = front_hi[:, 0:4, :], front_lo[:, 0:4, :]
        kp = hidT_room[:, 0:TILES * HEADS * FEATS].rearrange("p (t f) -> p t f", t=TILES)
        qp = act1_room[:, 0:HEAD_GROUPS * SEQ].rearrange("p (g t) -> p g t", t=SEQ)
        def over(parts, first, n, k):
            return parts[:, :, :].rearrange("p e c -> p (e c)")[:, first:first + n * k].rearrange("p (n k) -> p n k", k=k)
        x3T_hi, x3T_lo = (over(w, 0, BATCHES, SEQ) for w in (w13_hi, w13_lo))
        f_hi, f_lo = (over(w, TOKENS, FF_TILES, CHUNK) for w in (w13_hi, w13_lo))
        fi_hi, fi_lo = (over(w, TOKENS + FF_TILES * CHUNK, 2, FF) for w in (w13_hi, w13_lo))

        f_silu = work[:, 0:2, :]
        f_act = room(x_in)
        f_last = room(xT_in)
        f_res = sb("f_res", [P, CHUNK_TILES * D])
        f_out = work[:, 2, :]

        ps = ctx.enter_context(nc.psum_tensor("ps", [P, 8, 512], fp32))

        ld = sems("ld", "const x conv w2 att ff")
        moe_loaded = [ctx.enter_context(nc.semaphore(f"ld_moe{j}")) for j in range(2)]
        wt = sems("wt", "before memset conv_mm front_hi front_lo fc_g cproj_bb small_mm small x_bias zero_rows moe_hi moe_lo att_hi att_lo ff_hi ff_lo fi_hi fi_lo ff_out")
        g0 = sems("g0", "x_hi x_lo front gate conv h mv rstd hn tr hT hnT fc mid out res"
                  " mv1 rstd1 x1 kept x1_tr x1T logits top top_at below exps denom rdenom score"
                  " at_f chosen either rank_mm added rank rank_of row_f row carry xs sent")
        carrier = sems("carrier", "dve pool")
        tb = sems("tb", "count step ready place placed")
        mo = sems("mo", "rows tr hi lo up act1 hid hid_tr hidT down out")
        mo_out = [ctx.enter_context(nc.semaphore(f"mo_stored{j}")) for j in range(FLY)]
        mo_in = [ctx.enter_context(nc.semaphore(f"mo_loaded{j}")) for j in range(FLY)]
        at = sems("at", "row got sum1 res mv rstd x2 kept tr x2T hi lo qk st sq st_hi st_lo v_mm v_tok"
                  " kf kp qf qp kv_mm kv kv_tr kvT nd den rden att out"
                  " res3 mv3 rstd3 x3 kept3 tr3 x3_hi x3_lo")
        ff = sems("ff", "in_mm silu act g1 g2 hi lo h1_mm h2_mm out_mm res mv rstd out stored")

        block = ctx.enter_context(nc.Block())

        @block.sync
        def _(sp):
            for tile, src in ((xT_in, "xT"), (x_in, "x_tok")):
                sp.dma_start(tile[:, :, :], A[src]).then_inc(ld["x"], 16)
            for tile, src in ((w_h, "w_h"), (conv_bd, "conv_bd"), (fc_wT, "fc_wT"), (cproj, "cproj"), (out_wT, "out_wT")):
                sp.dma_start(tile[:, :, :], A[src]).then_inc(ld["conv"], 16)
            sp.wait_ge(wt["memset"], 7)
            zero_src = zeros[:, :].unsqueeze(1).to_broadcast([P, REGION // P, D])
            for e in range(EXPERTS):
                sp.dma_start(routed[e * REGION:(e + 1) * REGION, :].rearrange("(t p) d -> p t d", p=P),
                             zero_src).then_inc(wt["zero_rows"], 16)
            sp.dma_start(routed[EXPERTS * REGION:ROWS, :].rearrange("(t p) d -> p t d", p=P),
                         zeros[:, :].unsqueeze(1).to_broadcast([P, DUMMY_TILES, D])).then_inc(wt["zero_rows"], 16)
            for tile, src in ((qk_w, "qk_w"),):
                sp.dma_start(tile[:, :, :], A[src]).then_inc(ld["att"], 16)
            for tile, src in ((qk_b, "qk_b"), (wv, "wv"), (bv, "bv"), (omega, "omega"), (wout, "wout"), (bout, "bout")):
                sp.dma_start(tile[:, :], A[src]).then_inc(ld["att"], 16)
            for tile, src in ((ff_s, "ff_s"), (ff_out, "ff_out")):
                sp.dma_start(tile[:, :, :], A[src]).then_inc(ld["ff"], 16)
            sp.dma_start(ff_out_s[:, :], A["ff_out_s"]).then_inc(ld["ff"], 16)
            sp.wait_ge(wt["conv_mm"], 2)
            sp.dma_start(ff_in[:, :, :], A["ff_in"]).then_inc(ld["ff"], 16)
            sp.dma_start(w2[:, :, :, :], A["w2"]).then_inc(ld["w2"], 16)
            for j in range(2):
                sp.dma_start(w13[:, j, :], A["w13"][:, j, :]).then_inc(moe_loaded[j], 16)
            with sp.Fori(1, EXPERTS // 2) as n:
                for j in range(2):
                    sp.wait_ge(wt["moe_lo"], 2 * n + j - 1)
                    sp.dma_start(w13[:, j, :], A["w13"][:, 2 * n + j, :]).then_inc(moe_loaded[j], 16)

            sp.wait_ge(tb["ready"], 1)
            sp.wait_ge(g0["sent"], 64 * BATCHES)
            for k, tile in enumerate(ff_h):
                sp.dma_start(tile, A["ff_h"][:, k * FF_TILES:(k + 1) * FF_TILES, :]).then_inc(ld["ff"], 16)

            def rows_step(i):
                for j in range(FLY):
                    t = FLY * i + j
                    if live(i, SLOT_TILES // FLY):
                        start = sp.value_load(start_t[0:1, bass.ds(t, 1)], min_val=0, max_val=ROWS - P)
                        wait(sp, mo["tr"], t - FLY + 1)
                        sp.dma_start(rows_in[:, j, :], routed[bass.ds(start, P), :]).then_inc(mo_in[j], 16)
                    t = t - STORE_LAG
                    if live(t, SLOT_TILES):
                        sp.wait_ge(mo["out"], t + 1)
                        sp.dma_start(answers.rearrange("(t p) d -> t p d", p=P)[t],
                                     rows_out[:, (j - STORE_LAG) % FLY, :]).then_inc(mo_out[(j - STORE_LAG) % FLY], 16)
            steps(sp, SLOT_TILES // FLY, 2, rows_step)

            def store(c):
                sp.wait_ge(ff["out"], c + 1)
                sp.dma_start(out.rearrange("(c t p) d -> c p t d", t=CHUNK_TILES, p=P)[c],
                             f_out[:, :].rearrange("p (t d) -> p t d", d=D)).then_inc(ff["stored"], 16)
            store(0)
            with sp.Fori(1, CHUNKS) as c:
                store(c)
            sp.wait_ge(ff["stored"], 16 * CHUNKS)

        @block.gpsimd
        def _(pool):
            pool.memset(zeros[:, :], 0.0).then_inc(wt["memset"], 1)
            pool.memset(ones[:, :], 1.0).then_inc(wt["memset"], 1)
            pool.memset(ones_bf[:, :], 1.0).then_inc(wt["memset"], 1)
            pool.memset(minus_half[:, :], -0.5).then_inc(wt["memset"], 1)
            pool.memset(eps[:, :], EPS).then_inc(wt["memset"], 1)
            pool.memset(euler[:, :], float(np.e)).then_inc(wt["memset"], 1)
            pool.memset(hid[:, :, :], 0.0).then_inc(wt["memset"], 1)

            def inverse_root(sem_mv, sem, n, mv_, veps_, rstd_, tiles):
                pool.wait_ge(sem_mv, 2 * n)
                nc.gpsimd.tensor_tensor(veps_[:, 0:tiles], mv_[:, 0:tiles, 1], eps[:, 0:tiles], ALU.add).then_inc(sem, 1)
                pool.wait_ge(sem, 2 * n - 1)
                for t in range(0, tiles, TILES):
                    last = nc.gpsimd.tensor_tensor(rstd_[:, t:t + TILES], veps_[:, t:t + TILES], minus_half[:, :], ALU.pow)
                last.then_inc(sem, 1)

            pool.wait_ge(wt["memset"], 7)
            with pool.Fori(0, EXPERTS // 2) as n:
                for j in range(2):
                    e = 2 * n + j
                    pool.wait_ge(moe_loaded[j], 16 * n + 16)
                    nc.gpsimd.tensor_copy(w13_hi[:, e, :], w13[:, j, :]).then_inc(wt["moe_hi"], 1)
                    pool.wait_ge(wt["moe_hi"], e + 1)
                    nc.gpsimd.tensor_tensor(w13_lo[:, e, :], w13[:, j, :], w13_hi[:, e, :].bitcast(fp32),
                                            ALU.subtract).then_inc(wt["moe_lo"], 1)

            def route_step(i):
                b = i - 3
                if live(b, BATCHES):
                    pool.wait_ge(g0["below"], b + 1)
                    nc.gpsimd.tensor_tensor(exps[:, :, :].rearrange("p t e -> p (t e)"), euler[:, :],
                                            below[:, :, :].rearrange("p t e -> p (t e)"), ALU.pow).then_inc(g0["exps"], 1)
                b = i - 2
                if live(b, BATCHES):
                    inverse_root(g0["mv1"], g0["rstd1"], b + 1, mv, veps, rstd, TILES)
                    pool.wait_ge(g0["x1"], b + 1)
                    nc.gpsimd.tensor_copy(x_kept[:, b, :], x1[:, :]).then_inc(g0["kept"], 1)
                b = i - 3
                if live(b, BATCHES):
                    pool.wait_ge(g0["xs"], b + 1)
                    pool.wait_ge(g0["row"], b + 1)
                    if isinstance(b, int) and b == 0:
                        pool.wait_ge(wt["zero_rows"], 16 * (EXPERTS + 1))
                    alone(pool, carrier["pool"])
                    for r in range(TILES * TOP_K):
                        nc.gpsimd.indirect_dma_start(
                            routed[:, :], bass.IndirectOffsetOnAxis(ap=row[:, r:r + 1], axis=0),
                            xs[:, r, :], None).then_inc(g0["sent"], 16)
                if live(i, BATCHES):
                    inverse_root(g0["mv"], g0["rstd"], i + 1, mv_h, veps_h, rstd_h, TILES)
            steps(pool, BATCHES, 3, route_step)

            pool.wait_ge(ld["att"], 16 * 7)
            nc.gpsimd.tensor_copy(qk_hi[:, :, :], qk_w[:, :, :]).then_inc(wt["att_hi"], 1)
            nc.gpsimd.tensor_copy(om_hi[:, :], omega[:, :]).then_inc(wt["att_hi"], 1)
            pool.wait_ge(wt["att_hi"], 2)
            nc.gpsimd.tensor_tensor(qk_lo[:, :, :], qk_w[:, :, :], qk_hi[:, :, :].bitcast(fp32), ALU.subtract).then_inc(wt["att_lo"], 1)
            nc.gpsimd.tensor_tensor(om_lo[:, :], omega[:, :], om_hi[:, :].bitcast(fp32), ALU.subtract).then_inc(wt["att_lo"], 1)
            pool.wait_ge(ld["ff"], 16 * 6)
            for half, stage in enumerate(ff_h):
                with pool.Fori(0, FF_TILES) as k:
                    r = half * FF_TILES + k
                    nc.gpsimd.tensor_copy(fh_hi[:, r, :], stage[:, k, :]).then_inc(wt["ff_hi"], 1)
                    pool.wait_ge(wt["ff_hi"], r + 1)
                    nc.gpsimd.tensor_tensor(fh_lo[:, r, :], stage[:, k, :], fh_hi[:, r, :].bitcast(fp32), ALU.subtract).then_inc(wt["ff_lo"], 1)
            nc.gpsimd.tensor_tensor(ff_out_w[:, :, :], ff_out[:, :, :],
                                    ff_out_s[:, :].unsqueeze(1).to_broadcast([P, FF_TILES, D]), ALU.mult).then_inc(wt["ff_out"], 1)

            pool.wait_ge(tb["placed"], 1)
            for j in range(FLY):
                pool.wait_ge(mo_out[j], 16 * (SLOT_TILES // FLY))
            nc.gpsimd.tensor_copy(fi_hi, ff_in).then_inc(wt["fi_hi"], 1)
            pool.wait_ge(wt["fi_hi"], 1)
            nc.gpsimd.tensor_tensor(fi_lo, ff_in, fi_hi.bitcast(fp32), ALU.subtract).then_inc(wt["fi_lo"], 1)

            def attention_step(i):
                if live(i, BATCHES):
                    wait(pool, at["got"], 64 * i)
                    nc.gpsimd.tensor_copy(row_now[:, :], row_all[:, i, :]).then_inc(at["row"], 1)
                    pool.wait_ge(at["row"], i + 1)
                    wait(pool, at["res"], i)
                    alone(pool, carrier["pool"])
                    for r in range(TILES * TOP_K):
                        nc.gpsimd.indirect_dma_start(
                            got[:, r // TOP_K, r % TOP_K, :], None,
                            answers[:, :], bass.IndirectOffsetOnAxis(ap=row_now[:, r:r + 1], axis=0)).then_inc(at["got"], 16)
                b = i - 1
                if live(b, BATCHES):
                    inverse_root(at["mv"], at["rstd"], b + 1, mv, veps, rstd, TILES)
                    pool.wait_ge(at["x2"], b + 1)
                    nc.gpsimd.tensor_tensor(x_kept[:, b, :].rearrange("p (t d) -> p t d", d=D),
                                            x2[:, :].rearrange("p (t d) -> p t d", d=D),
                                            bout[:, :].unsqueeze(1).to_broadcast([P, TILES, D]), ALU.add).then_inc(at["kept"], 1)
                b = i - 4
                if live(b, BATCHES):
                    inverse_root(at["mv3"], at["rstd3"], b + 1, mv_h, veps_h, rstd_h, TILES)
                    pool.wait_ge(at["x3"], b + 1)
                    nc.gpsimd.tensor_copy(x_kept[:, b, :], x3[:, :]).then_inc(at["kept3"], 1)
                b = i - 2
                if live(b, BATCHES):
                    pool.wait_ge(at["st_hi"], b + 1)
                    wait(pool, at["qf"], b)
                    nc.gpsimd.tensor_tensor(st_lo[:, :, :], st[:, :, :], st_hi[:, :, :].bitcast(fp32), ALU.subtract).then_inc(at["st_lo"], 1)
            steps(pool, BATCHES, 4, attention_step)

            def mlp_norm(c):
                inverse_root(ff["mv"], ff["rstd"], c + 1, mv, veps, rstd, CHUNK_TILES)
            with pool.Fori(0, CHUNKS) as c:
                mlp_norm(c)

        @block.scalar
        def _(act):
            act.dma_start(const[:, :], A["const"]).then_inc(ld["const"], 16)
            for tile, src in ((w_gate, "w_gate"), (conv_b, "conv_b"), (ln_gb, "ln_gb"), (fc_b, "fc_b"),
                              (cproj_b, "cproj_b"), (gate_wT, "gate_wT")):
                act.dma_start(tile[:, :], A[src]).then_inc(ld["conv"], 16)

            act.wait_ge(ld["conv"], 16 * 11)
            nc.scalar.activation(front_hi[:, TAPS, :], w_gate[:, :], ACT.Copy).then_inc(wt["front_hi"], 1)
            for t in range(2):
                act.wait_ge(wt["conv_mm"], t + 1)
                nc.scalar.activation(front_hi[:, 0:TAPS, t * P:(t + 1) * P],
                                     ps[:, t, :].rearrange("p (k o) -> p k o", o=P), ACT.Copy).then_inc(wt["front_hi"], 1)
            act.wait_ge(ld["x"], 32)

            def conv_step(i):
                if live(i, BATCHES):
                    wait(act, g0["front"], i)
                    nc.scalar.activation(xT_hi[:, :], xT_in[:, i, :], ACT.Copy).then_inc(g0["x_hi"], 1)
                b = i - 3
                if live(b, BATCHES):
                    act.wait_ge(g0["score"], b + 1)
                    act.wait_ge(g0["kept"], b + 1)
                    wait(act, g0["sent"], 64 * b)
                    for t in range(TILES):
                        for k in range(TOP_K):
                            last = nc.scalar.activation(xs[:, TOP_K * t + k, :], x_kept[:, b, t * D:(t + 1) * D],
                                                        ACT.Copy, scale=score[:, t, k:k + 1])
                    last.then_inc(g0["xs"], 1)
                if live(i, BATCHES):
                    act.wait_ge(g0["front"], i + 1)
                    wait(act, g0["h"], i)
                    nc.scalar.activation(gate[:, :, :], ps[:, 0:2, INNER:], ACT.Silu).then_inc(g0["gate"], 1)
                b = i - 1
                if live(b, BATCHES):
                    act.wait_ge(g0["tr"], b + 1)
                    wait(act, g0["out"], b)
                    nc.scalar.activation(hT[:, :, :].rearrange("p t f -> p (t f)"), ps[:, 2, :], ACT.Copy).then_inc(g0["hT"], 1)
                b = i - 2
                if live(b, BATCHES):
                    act.wait_ge(g0["x1_tr"], b + 1)
                    wait(act, g0["logits"], b)
                    nc.scalar.activation(x1T[:, :], ps[:, 6, 0:SEQ], ACT.Copy).then_inc(g0["x1T"], 1)
                b = i - 1
                if live(b, BATCHES):
                    act.wait_ge(g0["fc"], b + 1)
                    act.wait_ge(wt["small"], 2)
                    nc.scalar.activation(mid[:, :], ps[:, 4, 0:SEQ], ACT.Silu, bias=fc_bias[:, 0:1]).then_inc(g0["mid"], 1)
            steps(act, BATCHES, 3, conv_step)

            def expert_step(i):
                for j in range(FLY):
                    t = FLY * i + j
                    if live(i, SLOT_TILES // FLY):
                        act.wait_ge(mo["tr"], t + 1)
                        wait(act, mo["up"], t - FLY + 1)
                        nc.scalar.activation(rT_hi[:, j, :], ps[:, 0, 0:P], ACT.Copy).then_inc(mo["hi"], 1)
                    u, ju = t - 1, (j - 1) % FLY
                    if live(u, SLOT_TILES):
                        act.wait_ge(mo["up"], u + 1)
                        wait(act, mo["hid"], u - FLY + 1)
                        nc.scalar.activation(act1[:, ju, :], ps[:, 2, 0:HIDDEN], ACT.Silu).then_inc(mo["act1"], 1)
                    u, ju = t - 3, j
                    if live(u, SLOT_TILES):
                        act.wait_ge(mo["down"], u + 1)
                        n = u // FLY if isinstance(u, int) else i - 1
                        wait(act, mo_out[j], 16 * n)
                        nc.scalar.activation(rows_out[:, j, :], ps[:, 6, 0:D], ACT.Copy).then_inc(mo["out"], 1)
            steps(act, SLOT_TILES // FLY, 1, expert_step)

            def attention_step(i):
                b = i - 1
                if live(b, BATCHES):
                    act.wait_ge(at["tr"], b + 1)
                    wait(act, at["v_mm"], b)
                    wait(act, at["lo"], b)
                    nc.scalar.activation(x2T[:, :], ps[:, 0, 0:SEQ], ACT.Copy).then_inc(at["x2T"], 1)
                b = i - 3
                if live(b, BATCHES):
                    act.wait_ge(at["kv_tr"], b + 1)
                    wait(act, at["nd"], b)
                    nc.scalar.activation(kvT[:, :, :].rearrange("p a f -> p (a f)"), ps[:, 6, 256:512], ACT.Copy).then_inc(at["kvT"], 1)
                b = i - 2
                if live(b, BATCHES):
                    act.wait_ge(at["kf"], b + 1)
                    wait(act, at["kv_mm"], b)
                    nc.scalar.activation(kp[:, :, :], ps[:, 4:6, :], ACT.Exp).then_inc(at["kp"], 1)
                b = i - 4
                if live(b, BATCHES):
                    act.wait_ge(at["tr3"], b + 1)
                    nc.scalar.activation(x3T_hi[:, b, :], ps[:, 0, SEQ:], ACT.Copy).then_inc(at["x3_hi"], 1)
                b = i - 2
                if live(b, BATCHES):
                    act.wait_ge(at["qf"], b + 1)
                    wait(act, at["nd"], b)
                    nc.scalar.activation(qp[:, :, :].rearrange("p g t -> p (g t)"),
                                         ps[:, 4:6, :].rearrange("p a t -> p (a t)"), ACT.Exp).then_inc(at["qp"], 1)
                b = i - 1
                if live(b, BATCHES):
                    act.wait_ge(at["st"], b + 1)
                    nc.scalar.activation(st[64:128, :, :], st[64:128, :, :], ACT.Square).then_inc(at["sq"], 1)
            steps(act, BATCHES, 4, attention_step)

            def mlp_step(c):
                if live(c, CHUNKS):
                    for m in range(FF_TILES):
                        n = FF_TILES * c + m
                        act.wait_ge(ff["in_mm"], n + 1)
                        wait(act, ff["act"], n - 1)
                        nc.scalar.activation(f_silu[:, m % 2, :], ps[:, 2 * (m % 2), :], ACT.Silu,
                                             scale=ff_s[:, 0, m:m + 1]).then_inc(ff["silu"], 1)
                    for m in range(FF_TILES):
                        n = FF_TILES * c + m
                        act.wait_ge(ff["h1_mm"], n + 1)
                        act.wait_ge(ff["lo"], 2 * FF_TILES * c + m + 1)
                        nc.scalar.activation(f_act[:, m, :], ps[:, 4 + m, :], ACT.Gelu,
                                             scale=ff_s[:, 2, m:m + 1]).then_inc(ff["g1"], 1)
                    for m in range(FF_TILES):
                        n = FF_TILES * c + m
                        act.wait_ge(ff["h2_mm"], n + 1)
                        wait(act, ff["out_mm"], c)
                        nc.scalar.activation(f_last[:, m, :], ps[:, m, :], ACT.Gelu,
                                             scale=ff_s[:, 3, m:m + 1]).then_inc(ff["g2"], 1)
            act.wait_ge(ld["ff"], 16 * 6)
            act.wait_ge(wt["ff_lo"], 2 * FF_TILES)
            steps(act, CHUNKS, 0, mlp_step)

        @block.vector
        def _(dve):
            V = nc.vector

            def split(hi, lo, src, sem_hi, sem_lo, n):
                V.tensor_copy(hi, src).then_inc(sem_hi, 1)
                dve.wait_ge(sem_hi, n)
                V.tensor_tensor(lo, src, hi.bitcast(fp32), ALU.subtract).then_inc(sem_lo, 1)

            def moments(src, stats_, mv_, tiles, width, sem, n):
                for t in range(tiles):
                    last = V.bn_stats(stats_[:, t, :], src[:, t * width:(t + 1) * width])
                last.then_inc(sem, 1)
                dve.wait_ge(sem, 2 * n - 1)
                alone(dve, carrier["dve"])
                for t in range(tiles):
                    last = V.bn_aggr(mv_[:, t, :], stats_[:, t, :])
                last.then_inc(sem, 1)

            def normalise(dst, src, mv_, rstd_, tiles, width, sem):
                for t in range(tiles):
                    cols = slice(t * width, (t + 1) * width)
                    last = V.tensor_scalar(dst[:, cols], src[:, cols], mv_[:, t, 0:1], rstd_[:, t:t + 1],
                                           ALU.subtract, ALU.mult)
                last.then_inc(sem, 1)

            V.memset(earlier[:, :, :], 0.0).then_inc(wt["before"], 1)
            dve.wait_ge(ld["const"], 16)
            V.tensor_copy(before[:, :], const[:, C_BEFORE:C_BEFORE + P]).then_inc(wt["before"], 1)
            dve.wait_ge(ld["conv"], 16 * 11)
            for t in range(2):
                V.tensor_copy(cproj_bb[:, t, :], cproj_b[:, t:t + 1].to_broadcast([P, P])).then_inc(wt["cproj_bb"], 1)
                V.tensor_scalar(fc_g[:, t, :], fc_wT[:, t, :], ln_gb[:, t:t + 1], None, ALU.mult).then_inc(wt["fc_g"], 1)
            dve.wait_ge(wt["front_hi"], 1)
            V.tensor_tensor(front_lo[:, TAPS, :], w_gate[:, :], front_hi[:, TAPS, :].bitcast(fp32), ALU.subtract).then_inc(wt["front_lo"], 1)
            for t in range(2):
                dve.wait_ge(wt["front_hi"], t + 2)
                V.tensor_tensor(front_lo[:, 0:TAPS, t * P:(t + 1) * P], ps[:, t, :].rearrange("p (k o) -> p k o", o=P),
                                front_hi[:, 0:TAPS, t * P:(t + 1) * P].bitcast(fp32), ALU.subtract).then_inc(wt["front_lo"], 1)
            dve.wait_ge(wt["small_mm"], 1)
            V.tensor_copy(mid_out[:, :], ps[:, 4, 0:D]).then_inc(wt["small"], 1)
            dve.wait_ge(wt["small_mm"], 2)
            V.tensor_tensor(fc_bias[:, :], ps[:, 6, 0:1], fc_b[:, :], ALU.add).then_inc(wt["small"], 1)
            dve.wait_ge(wt["small_mm"], 3)
            V.tensor_copy(out_bias[:, :], ps[:, 5, 0:D]).then_inc(wt["small"], 1)
            dve.wait_ge(ld["x"], 32)
            dve.wait_ge(wt["small"], 3)
            x_tiles = x_in[:, :, :].rearrange("p b (t d) -> p (b t) d", d=D)
            V.tensor_tensor(x_tiles, x_tiles, out_bias[:, :].unsqueeze(1).to_broadcast([P, BATCHES * TILES, D]),
                            ALU.add).then_inc(wt["x_bias"], 1)

            iota = const[:, C_IOTA:C_IOTA + EXPERTS]
            base = const[:, C_BASE:C_BASE + EXPERTS]
            logits = ps[:, 7, 0:TILES * EXPERTS].rearrange("p (t e) -> p t e", e=EXPERTS)
            rank_ps = ps[:, 7, 32:32 + TILES * EXPERTS].rearrange("p (t e) -> p t e", e=EXPERTS)

            def choose(b):
                dve.wait_ge(g0["logits"], b + 1)
                alone(dve, carrier["dve"])
                for t in range(TILES):
                    last = V.max(top[:, t, :], logits[:, t, :])
                last.then_inc(g0["top"], 1)
                dve.wait_ge(g0["top"], b + 1)
                alone(dve, carrier["dve"])
                for t in range(TILES):
                    last = V.max_index(top_at[:, t, :], top[:, t, :], logits[:, t, :])
                last.then_inc(g0["top_at"], 1)
                V.tensor_tensor(below[:, :, :], top[:, :, :], top[:, :, 0:1].to_broadcast([P, TILES, EXPERTS]),
                                ALU.subtract).then_inc(g0["below"], 1)
                dve.wait_ge(g0["top_at"], b + 1)
                V.tensor_copy(chosen_at[:, :, :], top_at[:, :, 0:TOP_K]).then_inc(g0["at_f"], 1)
                dve.wait_ge(g0["at_f"], b + 1)
                V.tensor_tensor(chosen[:, b, :, :].rearrange("p (t k) e -> p t k e", k=TOP_K),
                                iota.unsqueeze(1).unsqueeze(1).to_broadcast([P, TILES, TOP_K, EXPERTS]),
                                chosen_at[:, :, :].unsqueeze(3).to_broadcast([P, TILES, TOP_K, EXPERTS]),
                                ALU.is_equal).then_inc(g0["chosen"], 1)
                dve.wait_ge(g0["chosen"], b + 1)
                wait(dve, g0["rank_mm"], b)
                of_tile = chosen[:, b, :, :].rearrange("p (t k) e -> p t k e", k=TOP_K)
                V.tensor_tensor(either[:, :, :], of_tile[:, :, 0, :], of_tile[:, :, 1, :], ALU.add).then_inc(g0["either"], 1)
                dve.wait_ge(g0["either"], b + 1)
                V.tensor_tensor(earlier[:, 1, :], earlier[:, 0, :], either[:, 0, :], ALU.add).then_inc(g0["added"], 1)
                dve.wait_ge(g0["exps"], b + 1)
                V.reduce_sum(denom[:, :], exps[:, :, :], axis=AX.X).then_inc(g0["denom"], 1)
                dve.wait_ge(g0["denom"], b + 1)
                V.reciprocal(rdenom[:, :], denom[:, :]).then_inc(g0["rdenom"], 1)
                dve.wait_ge(g0["rdenom"], b + 1)
                wait(dve, g0["xs"], b)
                V.tensor_tensor(score[:, :, :], exps[:, :, 0:TOP_K],
                                rdenom[:, :].unsqueeze(2).to_broadcast([P, TILES, TOP_K]), ALU.mult).then_inc(g0["score"], 1)

            def place(b):
                dve.wait_ge(g0["rank_mm"], b + 1)
                V.tensor_tensor(rank[:, :, :], rank_ps, base.unsqueeze(1).to_broadcast([P, TILES, EXPERTS]),
                                ALU.add).then_inc(g0["rank"], 1)
                V.tensor_tensor(earlier[:, 0, :], earlier[:, 1, :], either[:, 1, :], ALU.add).then_inc(g0["carry"], 1)
                dve.wait_ge(g0["rank"], b + 1)
                V.tensor_tensor(rank_of[:, :, :].rearrange("p (t k) e -> p t k e", k=TOP_K),
                                chosen[:, b, :, :].rearrange("p (t k) e -> p t k e", k=TOP_K),
                                rank[:, :, :].unsqueeze(2).to_broadcast([P, TILES, TOP_K, EXPERTS]),
                                ALU.mult).then_inc(g0["rank_of"], 1)
                dve.wait_ge(g0["rank_of"], b + 1)
                V.reduce_sum(row_f[:, :], rank_of[:, :, :], axis=AX.X).then_inc(g0["row_f"], 1)
                dve.wait_ge(g0["row_f"], b + 1)
                wait(dve, g0["sent"], 64 * b)
                V.tensor_copy(row[:, :], row_f[:, :])
                V.tensor_copy(rows_f[:, b, :], row_f[:, :]).then_inc(g0["row"], 1)

            def conv_step(i):
                if live(i, BATCHES):
                    dve.wait_ge(g0["x_hi"], i + 1)
                    V.tensor_tensor(xT_lo[:, :], xT_in[:, i, :], xT_hi[:, :].bitcast(fp32), ALU.subtract).then_inc(g0["x_lo"], 1)
                if live(i - 3, BATCHES):
                    choose(i - 3)
                b = i - 2
                if live(b, BATCHES):
                    dve.wait_ge(g0["out"], b + 1)
                    wait(dve, g0["x1"], b)
                    V.tensor_tensor(res[:, :], ps[:, 5, 0:SEQ], x_in[:, b, :], ALU.add).then_inc(g0["res"], 1)
                    dve.wait_ge(g0["res"], b + 1)
                    moments(res, stats, mv, TILES, D, g0["mv1"], b + 1)
                    dve.wait_ge(g0["rstd1"], 2 * b + 2)
                    wait(dve, g0["kept"], b)
                    wait(dve, g0["x1_tr"], b)
                    normalise(x1, res, mv, rstd, TILES, D, g0["x1"])
                b = i - 1
                if live(b, BATCHES):
                    dve.wait_ge(g0["tr"], b + 1)
                    wait(dve, g0["fc"], b)
                    V.tensor_copy(hnT[:, :, :].rearrange("p k (t q) -> p t k q", q=P),
                                  ps[:, 3, :].rearrange("p (t k q) -> p t k q", k=2, q=P)).then_inc(g0["hnT"], 1)
                if live(i - 3, BATCHES):
                    place(i - 3)
                if live(i, BATCHES):
                    dve.wait_ge(g0["gate"], i + 1)
                    V.tensor_tensor(conv[:, :, :], ps[:, 0:2, 0:INNER],
                                    conv_b[:, :].unsqueeze(1).to_broadcast([P, TILES, INNER]), ALU.add).then_inc(g0["conv"], 1)
                    dve.wait_ge(g0["conv"], i + 1)
                    wait(dve, g0["tr"], i)
                    V.tensor_tensor(h[:, :, :], conv[:, :, :], gate[:, :, :], ALU.mult).then_inc(g0["h"], 1)
                    dve.wait_ge(g0["h"], i + 1)
                    hf = h[:, :, :].rearrange("p t f -> p (t f)")
                    moments(hf, stats_h, mv_h, TILES, INNER, g0["mv"], i + 1)
                    dve.wait_ge(g0["rstd"], 2 * i + 2)
                    normalise(hn[:, :, :].rearrange("p t f -> p (t f)"), hf, mv_h, rstd_h, TILES, INNER, g0["hn"])
            steps(dve, BATCHES, 3, conv_step)

            dve.wait_ge(tb["count"], 1)
            V.tensor_scalar(n_tiles_f[:, :], ps[:, 7, 64:64 + EXPERTS], float(P - 1), None, ALU.add).then_inc(tb["step"], 1)
            dve.wait_ge(tb["step"], 1)
            V.tensor_copy(n_tiles_i[:, :], n_tiles_f[:, :]).then_inc(tb["step"], 1)
            dve.wait_ge(tb["step"], 2)
            V.tensor_scalar(n_tiles_s[:, :], n_tiles_i[:, :], P.bit_length() - 1, None, ALU.logical_shift_right).then_inc(tb["step"], 1)
            dve.wait_ge(tb["step"], 3)
            V.tensor_copy(n_tiles[:, :], n_tiles_s[:, :]).then_inc(tb["step"], 1)
            dve.wait_ge(tb["step"], 4)
            V.tensor_tensor(upto_p[:, :, :], const[:, C_UPTO:C_UPTO + EXPERTS * EXPERTS].rearrange("p (a b) -> p a b", b=EXPERTS),
                            n_tiles[:, :].unsqueeze(1).to_broadcast([P, EXPERTS, EXPERTS]), ALU.mult).then_inc(tb["step"], 1)
            V.tensor_scalar(skip_rows[:, :], n_tiles[:, :], -float(P), float(REGION), ALU.mult, ALU.add).then_inc(tb["step"], 1)
            dve.wait_ge(tb["step"], 5)
            V.reduce_sum(upto[:, :], upto_p[:, :, :], axis=AX.X).then_inc(tb["step"], 1)
            dve.wait_ge(tb["step"], 7)
            V.tensor_tensor(past[:, :, :], upto[:, :].unsqueeze(1).to_broadcast([P, SLOT_TILES, EXPERTS]),
                            const[:, C_TILE:C_TILE + SLOT_TILES].unsqueeze(2).to_broadcast([P, SLOT_TILES, EXPERTS]),
                            ALU.is_le).then_inc(tb["step"], 1)
            dve.wait_ge(tb["step"], 8)
            dve.wait_ge(tb["step"], 6)
            V.tensor_tensor(past_rows[:, :, :], past[:, :, :],
                            skip_rows[:, :].unsqueeze(1).to_broadcast([P, SLOT_TILES, EXPERTS]), ALU.mult).then_inc(tb["step"], 1)
            V.reduce_sum(expert_f[:, :], past[:, :, :], axis=AX.X).then_inc(tb["step"], 1)
            dve.wait_ge(tb["step"], 9)
            V.reduce_sum(start_f[:, :], past_rows[:, :, :], axis=AX.X).then_inc(tb["step"], 1)
            dve.wait_ge(tb["step"], 11)
            V.tensor_tensor(start_f2[:, :], start_f[:, :], const[:, C_ROW:C_ROW + SLOT_TILES], ALU.add).then_inc(tb["step"], 1)
            dve.wait_ge(tb["step"], 10)
            V.tensor_scalar(expert_t[:, :], expert_f[:, :], float(EXPERTS - 1), None, ALU.min)
            dve.wait_ge(tb["step"], 12)
            V.tensor_copy(start_t[:, :], start_f2[:, :]).then_inc(tb["ready"], 1)
            V.scalar_tensor_tensor(shift_r[:, :], upto[:, :], float(P), skip_rows[:, :], ALU.mult, ALU.add).then_inc(tb["place"], 1)
            dve.wait_ge(tb["place"], 1)
            V.scalar_tensor_tensor(shift[:, :], shift_r[:, :], float(REGION), base, ALU.subtract, ALU.subtract).then_inc(tb["place"], 1)
            dve.wait_ge(tb["place"], 2)
            chosen_rows = chosen[:, :, :, :].rearrange("p b r e -> p (b r) e")
            V.tensor_tensor(chosen_rows, chosen_rows, shift[:, :].unsqueeze(1).to_broadcast([P, BATCHES * TILES * TOP_K, EXPERTS]),
                            ALU.mult).then_inc(tb["place"], 1)
            dve.wait_ge(tb["place"], 3)
            V.reduce_sum(shift_of[:, :], chosen_rows, axis=AX.X).then_inc(tb["place"], 1)
            dve.wait_ge(tb["place"], 4)
            V.tensor_tensor(row_all[:, :, :].rearrange("p b r -> p (b r)"), rows_f[:, :, :].rearrange("p b r -> p (b r)"),
                            shift_of[:, :], ALU.add).then_inc(tb["placed"], 1)

            def expert_step(i):
                for j in range(FLY):
                    t = FLY * i + j
                    if live(i, SLOT_TILES // FLY):
                        dve.wait_ge(mo["hi"], t + 1)
                        wait(dve, mo["up"], t - FLY + 1)
                        V.tensor_tensor(rT_lo[:, j, :], ps[:, 0, 0:P], rT_hi[:, j, :].bitcast(fp32),
                                        ALU.subtract).then_inc(mo["lo"], 1)
                    u, ju = t - 2, (j - 2) % FLY
                    if live(u, SLOT_TILES):
                        dve.wait_ge(mo["hid_tr"], u + 1)
                        wait(dve, mo["down"], u - FLY + 1)
                        V.tensor_copy(hidT[:, ju, :], ps[:, 1, 0:HIDDEN_TILES * P]).then_inc(mo["hidT"], 1)
                    u, ju = t - 1, (j - 1) % FLY
                    if live(u, SLOT_TILES):
                        dve.wait_ge(mo["act1"], u + 1)
                        wait(dve, mo["hid_tr"], u - FLY + 1)
                        V.tensor_tensor(hid[:, ju, 0:HIDDEN], act1[:, ju, :], ps[:, 3 + ju, 0:HIDDEN],
                                        ALU.mult).then_inc(mo["hid"], 1)
            steps(dve, SLOT_TILES // FLY, 1, expert_step)

            def attention_step(i):
                b = i - 1
                if live(b, BATCHES):
                    dve.wait_ge(at["x2T"], b + 1)
                    wait(dve, at["qk"], b)
                    split(x2T_hi[:, :], x2T_lo[:, :], x2T[:, :], at["hi"], at["lo"], b + 1)
                b = i - 4
                if live(b, BATCHES):
                    dve.wait_ge(at["x3_hi"], b + 1)
                    V.tensor_tensor(x3T_lo[:, b, :], ps[:, 0, SEQ:], x3T_hi[:, b, :].bitcast(fp32), ALU.subtract).then_inc(at["x3_lo"], 1)
                b = i - 3
                if live(b, BATCHES):
                    dve.wait_ge(at["nd"], b + 1)
                    wait(dve, at["out"], b)
                    V.tensor_scalar(den[:, :], ps[:, 7, SEQ:], 1e-6, None, ALU.add).then_inc(at["den"], 1)
                    dve.wait_ge(at["den"], b + 1)
                    V.reciprocal(rden[:, :], den[:, :]).then_inc(at["rden"], 1)
                    dve.wait_ge(at["rden"], b + 1)
                    V.tensor_tensor(att[:, :], ps[:, 7, 0:SEQ], rden[:, :], ALU.mult).then_inc(at["att"], 1)
                if live(i, BATCHES):
                    dve.wait_ge(at["got"], 64 * (i + 1))
                    wait(dve, at["x2"], i)
                    V.tensor_tensor(sum1[:, :, :], got[:, :, 0, :], got[:, :, 1, :], ALU.add).then_inc(at["sum1"], 1)
                    dve.wait_ge(at["sum1"], i + 1)
                    V.tensor_tensor(res[:, :], sum1[:, :, :].rearrange("p t d -> p (t d)"), x_kept[:, i, :], ALU.add).then_inc(at["res"], 1)
                    dve.wait_ge(at["res"], i + 1)
                    moments(res, stats, mv, TILES, D, at["mv"], i + 1)
                    dve.wait_ge(at["rstd"], 2 * i + 2)
                    wait(dve, at["kept"], i)
                    wait(dve, at["tr"], i)
                    normalise(x2, res, mv, rstd, TILES, D, at["x2"])
                b = i - 3
                if live(b, BATCHES):
                    dve.wait_ge(at["out"], b + 1)
                    dve.wait_ge(at["kept"], b + 1)
                    wait(dve, at["x3"], b)
                    V.tensor_tensor(f_res[:, 0:SEQ], ps[:, 7, 0:SEQ], x_kept[:, b, :], ALU.add).then_inc(at["res3"], 1)
                    dve.wait_ge(at["res3"], b + 1)
                    moments(f_res, stats_h, mv_h, TILES, D, at["mv3"], b + 1)
                    dve.wait_ge(at["rstd3"], 2 * b + 2)
                    wait(dve, at["kept3"], b)
                    wait(dve, at["tr3"], b)
                    normalise(x3, f_res, mv_h, rstd_h, TILES, D, at["x3"])
                b = i - 1
                if live(b, BATCHES):
                    dve.wait_ge(at["qk"], b + 1)
                    wait(dve, at["st_lo"], b)
                    V.tensor_tensor(st[:, :, :], ps[:, 1:3, :].rearrange("p a (s t) -> p (a s) t", t=SEQ),
                                    qk_b[:, :].unsqueeze(2).to_broadcast([P, 4, SEQ]), ALU.add).then_inc(at["st"], 1)
                    dve.wait_ge(at["sq"], b + 1)
                    wait(dve, at["qf"], b)
                    V.tensor_copy(st_hi[:, :, :], st[:, :, :]).then_inc(at["st_hi"], 1)
                    dve.wait_ge(at["v_mm"], b + 1)
                    wait(dve, at["kv_mm"], b)
                    V.tensor_tensor(v_tok[:, :, :], ps[:, 3, 0:SEQ].rearrange("p (t d) -> p t d", d=D),
                                    bv[:, :].unsqueeze(1).to_broadcast([P, TILES, D]), ALU.add).then_inc(at["v_tok"], 1)
                b = i - 2
                if live(b, BATCHES):
                    dve.wait_ge(at["kv_mm"], b + 1)
                    wait(dve, at["kv_tr"], b)
                    V.tensor_tensor(kv[:, :, :], ps[:, 6, 0:2 * P].rearrange("p (a f) -> p a f", f=P),
                                    const[:, C_KVMASK:C_KVMASK + P].unsqueeze(1).to_broadcast([P, 2, P]), ALU.mult).then_inc(at["kv"], 1)
            steps(dve, BATCHES, 4, attention_step)

            def mlp_step(c):
                if live(c, CHUNKS):
                    for m in range(FF_TILES):
                        n = FF_TILES * c + m
                        dve.wait_ge(ff["silu"], n + 1)
                        wait(dve, ff["lo"], 2 * FF_TILES * c + m - FF_TILES + 1)
                        V.scalar_tensor_tensor(f_act[:, m, :], ps[:, 2 * (m % 2) + 1, :], ff_s[:, 1, m:m + 1],
                                               f_silu[:, m % 2, :], ALU.mult, ALU.mult).then_inc(ff["act"], 1)
                        dve.wait_ge(ff["act"], n + 1)
                        wait(dve, ff["h2_mm"], FF_TILES * c)
                        split(f_hi[:, m, :], f_lo[:, m, :], f_act[:, m, :], ff["hi"], ff["lo"], 2 * FF_TILES * c + m + 1)
                b = c - 1
                if live(b, CHUNKS):
                    dve.wait_ge(ff["out_mm"], b + 1)
                    wait(dve, ff["out"], b)
                    V.tensor_tensor(f_res[:, :], ps[:, 4, :],
                                    x_kept[:, :, :].rearrange("p (c a) d -> p c (a d)", a=BATCHES // CHUNKS)[:, b, :],
                                    ALU.add).then_inc(ff["res"], 1)
                if live(c, CHUNKS):
                    for m in range(FF_TILES):
                        n = FF_TILES * c + m
                        dve.wait_ge(ff["g1"], n + 1)
                        dve.wait_ge(ff["h1_mm"], FF_TILES * (c + 1))
                        split(f_hi[:, m, :], f_lo[:, m, :], f_act[:, m, :], ff["hi"], ff["lo"], 2 * FF_TILES * c + FF_TILES + m + 1)
                if live(b, CHUNKS):
                    dve.wait_ge(ff["res"], b + 1)
                    moments(f_res, stats, mv, CHUNK_TILES, D, ff["mv"], b + 1)
                    dve.wait_ge(ff["rstd"], 2 * b + 2)
                    wait(dve, ff["stored"], 16 * b)
                    normalise(f_out, f_res, mv, rstd, CHUNK_TILES, D, ff["out"])
            steps(dve, CHUNKS, 1, mlp_step)

        @block.tensor
        def _(pe):
            mm, transpose = nc.tensor.matmul, nc.tensor.transpose

            def mm3(dst, lhs, rhs, start, stop):
                mm(dst, lhs[0], rhs[0], start=start, stop=False)
                mm(dst, lhs[0], rhs[1], start=False, stop=False)
                return mm(dst, lhs[1], rhs[0], start=False, stop=stop)

            pe.wait_ge(ld["conv"], 16 * 11)
            for t in range(2):
                mm(ps[:, t, :], w_h[:, t, :], conv_bd[:, t, :], start=True, stop=True).then_inc(wt["conv_mm"], 1)
            for t in range(2):
                last = mm(ps[:, 4, 0:D], cproj[:, t, :], out_wT[:, t, :], start=t == 0, stop=t == 1)
            last.then_inc(wt["small_mm"], 1)
            for t in range(2):
                last = mm(ps[:, 6, 0:1], fc_wT[:, t, :], ln_gb[:, 2 + t:3 + t], start=t == 0, stop=t == 1)
            last.then_inc(wt["small_mm"], 1)
            pe.wait_ge(wt["cproj_bb"], 2)
            for t in range(2):
                last = mm(ps[:, 5, 0:D], cproj_bb[:, t, :], out_wT[:, t, :], start=t == 0, stop=t == 1)
            last.then_inc(wt["small_mm"], 1)
            pe.wait_ge(ld["const"], 16)
            pe.wait_ge(wt["before"], 2)
            pe.wait_ge(wt["memset"], 7)
            pe.wait_ge(wt["front_hi"], 3)
            pe.wait_ge(wt["front_lo"], 3)
            pe.wait_ge(wt["small"], 3)
            pe.wait_ge(wt["fc_g"], 2)

            def conv_step(i):
                if live(i, BATCHES):
                    pe.wait_ge(g0["x_lo"], i + 1)
                    wait(pe, g0["gate"], i)
                    wait(pe, g0["conv"], i)
                    for t in range(TILES):
                        def x_at(tap):
                            cols = slice(t * P + tap, t * P + tap + P)
                            return xT_hi[:, cols], xT_lo[:, cols]
                        both = [w[:, PAD:, :].rearrange("p k o -> p (k o)") for w in (front_hi, front_lo)]
                        mm3(ps[:, t, :], x_at(PAD), both, True, False)
                        for tap in range(PAD):
                            last = mm3(ps[:, t, 0:INNER], x_at(tap), (front_hi[:, tap, :], front_lo[:, tap, :]),
                                       False, tap == PAD - 1)
                    last.then_inc(g0["front"], 1)
                b = i - 3
                if live(b, BATCHES):
                    pe.wait_ge(g0["added"], b + 1)
                    wait(pe, g0["rank"], b)
                    dst = ps[:, 7, 32:32 + TILES * EXPERTS]
                    mm(dst, before[:, :], either[:, :, :].rearrange("p t e -> p (t e)"), start=True, stop=False)
                    mm(dst, ones_bf[:, :], earlier[:, :, :].rearrange("p t e -> p (t e)"), start=False, stop=True)\
                        .then_inc(g0["rank_mm"], 1)
                b = i - 1
                if live(b, BATCHES):
                    pe.wait_ge(g0["hn"], b + 1)
                    wait(pe, g0["hT"], b)
                    wait(pe, g0["hnT"], b)
                    for t in range(TILES):
                        for k in range(2):
                            cols = slice((2 * t + k) * P, (2 * t + k + 1) * P)
                            transpose(ps[:, 2, cols], h[:, t, k * P:(k + 1) * P], ident)
                            last = transpose(ps[:, 3, cols], hn[:, t, k * P:(k + 1) * P], ident)
                    last.then_inc(g0["tr"], 1)
                b = i - 2
                if live(b, BATCHES):
                    pe.wait_ge(g0["x1"], b + 1)
                    wait(pe, g0["x1T"], b)
                    for t in range(TILES):
                        last = transpose(ps[:, 6, t * P:(t + 1) * P], x1[:, t * D:(t + 1) * D], ident)
                    last.then_inc(g0["x1_tr"], 1)
                b = i - 1
                if live(b, BATCHES):
                    pe.wait_ge(g0["hnT"], b + 1)
                    wait(pe, g0["mid"], b)
                    for k in range(2):
                        last = mm(ps[:, 4, 0:SEQ], fc_g[:, k, :], hnT[:, k, :], start=k == 0, stop=k == 1)
                    last.then_inc(g0["fc"], 1)
                b = i - 2
                if live(b, BATCHES):
                    pe.wait_ge(g0["x1T"], b + 1)
                    wait(pe, g0["rank"], b)
                    for t in range(TILES):
                        last = mm(ps[:, 7, t * EXPERTS:(t + 1) * EXPERTS], x1T[:, t * P:(t + 1) * P], gate_wT[:, :],
                                  start=True, stop=True)
                    last.then_inc(g0["logits"], 1)
                b = i - 1
                if live(b, BATCHES):
                    pe.wait_ge(g0["mid"], b + 1)
                    pe.wait_ge(g0["hT"], b + 1)
                    wait(pe, g0["res"], b)
                    for t in range(TILES):
                        dst = ps[:, 5, t * D:(t + 1) * D]
                        mm(dst, mid[:, t * P:(t + 1) * P], mid_out[:, :], start=True, stop=False)
                        for k in range(2):
                            last = mm(dst, hT[:, t, k * P:(k + 1) * P], out_wT[:, k, :], start=False, stop=k == 1)
                    last.then_inc(g0["out"], 1)
            steps(pe, BATCHES, 3, conv_step)

            pe.wait_ge(g0["carry"], BATCHES)
            mm(ps[:, 7, 64:64 + EXPERTS], ones_bf[:, :], earlier[:, 0, :], start=True, stop=True).then_inc(tb["count"], 1)

            pe.wait_ge(tb["ready"], 1)
            pe.wait_ge(wt["moe_lo"], EXPERTS)
            pe.wait_ge(ld["w2"], 16)

            def expert_step(i):
                for j in range(FLY):
                    t = FLY * i + j
                    if live(i, SLOT_TILES // FLY):
                        pe.wait_ge(mo_in[j], 16 * (i + 1))
                        wait(pe, mo["lo"], t)
                        transpose(ps[:, 0, 0:P], rows_in[:, j, :], ident).then_inc(mo["tr"], 1)
                    u, ju = t - 1, (j - 1) % FLY
                    if live(u, SLOT_TILES):
                        e = pe.value_load(expert_t[0:1, bass.ds(u, 1)], min_val=0, max_val=EXPERTS - 1)
                        pe.wait_ge(mo["lo"], u + 1)
                        wait(pe, mo["act1"], u)
                        wait(pe, mo["hid"], u - FLY + 1)
                        for w in range(2):
                            cols = slice(w * HIDDEN, (w + 1) * HIDDEN)
                            last = mm3(ps[:, 3 + ju if w else 2, 0:HIDDEN], (rT_hi[:, ju, :], rT_lo[:, ju, :]),
                                       (w13_hi[:, e, cols], w13_lo[:, e, cols]), True, True)
                        last.then_inc(mo["up"], 1)
                    u, ju = t - 2, (j - 2) % FLY
                    if live(u, SLOT_TILES):
                        pe.wait_ge(mo["hid"], u + 1)
                        wait(pe, mo["hidT"], u)
                        for k in range(HIDDEN_TILES):
                            last = transpose(ps[:, 1, k * P:(k + 1) * P], hid[:, ju, k * P:(k + 1) * P], ident)
                        last.then_inc(mo["hid_tr"], 1)
                    u, ju = t - 3, j
                    if live(u, SLOT_TILES):
                        e = pe.value_load(expert_t[0:1, bass.ds(u, 1)], min_val=0, max_val=EXPERTS - 1)
                        pe.wait_ge(mo["hidT"], u + 1)
                        wait(pe, mo["out"], u)
                        for k in range(HIDDEN_TILES):
                            last = mm(ps[:, 6, 0:D], hidT[:, ju, k * P:(k + 1) * P], w2[:, e, k, :],
                                      start=k == 0, stop=k == HIDDEN_TILES - 1)
                        last.then_inc(mo["down"], 1)
            steps(pe, SLOT_TILES // FLY, 1, expert_step)

            pe.wait_ge(wt["att_lo"], 2)
            pe.wait_ge(mo["out"], SLOT_TILES)

            def attention_step(i):
                b = i - 1
                if live(b, BATCHES):
                    pe.wait_ge(at["x2"], b + 1)
                    wait(pe, at["x2T"], b)
                    wait(pe, at["x3_lo"], b - 3)
                    for t in range(TILES):
                        last = transpose(ps[:, 0, t * P:(t + 1) * P], x2[:, t * D:(t + 1) * D], ident)
                    last.then_inc(at["tr"], 1)
                b = i - 3
                if live(b, BATCHES):
                    pe.wait_ge(at["kv"], b + 1)
                    wait(pe, at["kvT"], b)
                    for a in range(2):
                        last = transpose(ps[:, 6, (2 + a) * P:(3 + a) * P], kv[:, a, :], ident)
                    last.then_inc(at["kv_tr"], 1)
                b = i - 2
                if live(b, BATCHES):
                    pe.wait_ge(at["st_lo"], b + 1)
                    wait(pe, at["qp"], b)
                    for t in range(TILES):
                        cols = slice(t * P, (t + 1) * P)
                        for s in range(2):
                            last = mm3(ps[:, 4 + t, s * 256:(s + 1) * 256], (st_hi[:, 2 + s, cols], st_lo[:, 2 + s, cols]),
                                       (om_hi[:, :], om_lo[:, :]), True, True)
                    last.then_inc(at["kf"], 1)
                b = i - 4
                if live(b, BATCHES):
                    pe.wait_ge(at["x3"], b + 1)
                    if live(i - 1, BATCHES):
                        pe.wait_ge(at["x2T"], i)
                    for t in range(TILES):
                        last = transpose(ps[:, 0, SEQ + t * P:SEQ + (t + 1) * P], x3[:, t * D:(t + 1) * D], ident)
                    last.then_inc(at["tr3"], 1)
                b = i - 3
                if live(b, BATCHES):
                    pe.wait_ge(at["kvT"], b + 1)
                    pe.wait_ge(at["qp"], b + 1)
                    wait(pe, at["res3"], b)
                    for a in range(2):
                        for g in range(HEAD_GROUPS):
                            last = mm(ps[32 * g:32 * g + 32, 7, a * SEQ:(a + 1) * SEQ], kvT[:, a, 32 * g:32 * g + 32],
                                      qp[:, g, :], start=True, stop=True)
                    last.then_inc(at["nd"], 1)
                b = i - 2
                if live(b, BATCHES):
                    pe.wait_ge(at["kp"], b + 1)
                    for g in range(HEAD_GROUPS):
                        cols = slice((g % 2) * P, (g % 2 + 1) * P)
                        last = mm3(ps[:, 4 + g // 2, (g % 2) * SEQ:(g % 2 + 1) * SEQ], (om_hi[:, cols], om_lo[:, cols]),
                                   (st_hi[:, g // 2, :], st_lo[:, g // 2, :]), True, True)
                    last.then_inc(at["qf"], 1)
                b = i - 3
                if live(b, BATCHES):
                    pe.wait_ge(at["att"], b + 1)
                    for t in range(TILES):
                        last = mm(ps[:, 7, t * D:(t + 1) * D], att[:, t * P:(t + 1) * P], wout[:, :],
                                  start=True, stop=True)
                    last.then_inc(at["out"], 1)
                b = i - 1
                if live(b, BATCHES):
                    pe.wait_ge(at["lo"], b + 1)
                    wait(pe, at["st"], b)
                    for s in range(4):
                        last = mm3(ps[:, 1 + s // 2, (s % 2) * SEQ:(s % 2 + 1) * SEQ], (qk_hi[:, s, :], qk_lo[:, s, :]),
                                   (x2T_hi[:, :], x2T_lo[:, :]), True, True)
                    last.then_inc(at["qk"], 1)
                    wait(pe, at["v_tok"], b)
                    for t in range(TILES):
                        last = mm(ps[:, 3, t * D:(t + 1) * D], x2T[:, t * P:(t + 1) * P], wv[:, :], start=True, stop=True)
                    last.then_inc(at["v_mm"], 1)
                b = i - 2
                if live(b, BATCHES):
                    pe.wait_ge(at["kp"], b + 1)
                    pe.wait_ge(at["v_tok"], b + 1)
                    wait(pe, at["kv"], b)
                    wait(pe, at["kvT"], b)
                    for a in range(2):
                        for t in range(TILES):
                            for g in range(HEAD_GROUPS):
                                lhs = ones[:, 0:32] if a else v_tok[:, t, 32 * g:32 * g + 32]
                                last = mm(ps[32 * g:32 * g + 32, 6, a * P:(a + 1) * P], lhs, kp[:, t, g * P:(g + 1) * P],
                                          start=t == 0, stop=t == TILES - 1)
                    last.then_inc(at["kv_mm"], 1)
            steps(pe, BATCHES, 4, attention_step)

            pe.wait_ge(wt["ff_lo"], 2 * FF_TILES)
            pe.wait_ge(wt["fi_lo"], 1)
            pe.wait_ge(wt["ff_out"], 1)
            pe.wait_ge(at["x3_lo"], BATCHES)

            def mlp_step(c):
                if live(c, CHUNKS):
                    cols = BATCHES // CHUNKS
                    x_parts = [x.rearrange("p (c a) t -> p c (a t)", a=cols)[:, c, :] for x in (x3T_hi, x3T_lo)]
                    for m in range(FF_TILES):
                        n = FF_TILES * c + m
                        wait(pe, ff["act"], n - 1)
                        if m == 0:
                            wait(pe, ff["g2"], n)
                        for w in range(2):
                            rows = slice(m * P, (m + 1) * P)
                            last = mm3(ps[:, 2 * (m % 2) + w, :], (fi_hi[:, w, rows], fi_lo[:, w, rows]), x_parts, True, True)
                        last.then_inc(ff["in_mm"], 1)
                b = c - 1
                if live(b, CHUNKS):
                    pe.wait_ge(ff["g2"], FF_TILES * (b + 1))
                    wait(pe, ff["res"], b)
                    for t in range(CHUNK_TILES):
                        for k in range(FF_TILES):
                            last = mm(ps[:, 4, t * D:(t + 1) * D], f_last[:, k, t * P:(t + 1) * P], ff_out_w[:, k, :],
                                      start=k == 0, stop=k == FF_TILES - 1)
                    last.then_inc(ff["out_mm"], 1)
                if live(c, CHUNKS):
                    for layer, bank, sem in ((0, 4, ff["h1_mm"]), (1, 0, ff["h2_mm"])):
                        for k in range(FF_TILES):
                            pe.wait_ge(ff["lo"], FF_TILES * (2 * c + layer) + k + 1)
                            if k == 0 and layer == 0:
                                wait(pe, ff["res"], c)
                                wait(pe, ff["g1"], FF_TILES * c)
                            for m in range(FF_TILES):
                                rows = slice(m * P, (m + 1) * P)
                                last = mm3(ps[:, bank + m, :], (fh_hi[:, layer * FF_TILES + k, rows], fh_lo[:, layer * FF_TILES + k, rows]),
                                           (f_hi[:, k, :], f_lo[:, k, :]), k == 0, k == FF_TILES - 1)
                                if k == FF_TILES - 1:
                                    last.then_inc(sem, 1)
            steps(pe, CHUNKS, 1, mlp_step)


def layouts(a):
    f = np.float32
    tiled = lambda w: np.ascontiguousarray(w.reshape(-1, P, w.shape[-1]).transpose(1, 0, 2))
    cols = lambda v: np.ascontiguousarray(v.reshape(-1, P).T)
    rows = lambda v: np.ascontiguousarray(np.broadcast_to(v[None, :], (P, v.shape[0])))
    A = {}
    x = a["L0_attn_hidden_states"]
    A["x_tok"] = np.ascontiguousarray(x.reshape(BATCHES, TILES, P, D).transpose(2, 0, 1, 3).reshape(P, BATCHES, TILES * D))
    xT = np.zeros((D, BATCHES, PAD + SEQ), f)
    xT[:, :, PAD:] = x.transpose(2, 0, 1)
    A["xT"] = xT
    w = a["L0_attn_in_proj_w"]
    A["w_h"] = tiled(w[:INNER])
    A["w_gate"] = np.ascontiguousarray(w[INNER:].T)
    width = INNER // GROUPS
    bd = np.zeros((2, P, TAPS, P), f)
    for o in range(INNER):
        t, g = o // P, o % P // width
        bd[t, g * width:(g + 1) * width, :, o % P] = a["L0_attn_conv_w"][o]
    A["conv_bd"] = np.ascontiguousarray(bd.reshape(2, P, TAPS * P).transpose(1, 0, 2))
    A["conv_b"] = rows(a["L0_attn_conv_b"])
    A["fc_wT"] = tiled(np.ascontiguousarray(a["L0_attn_fc_w"].T))
    A["ln_gb"] = np.ascontiguousarray(np.concatenate([cols(a["L0_attn_ln_g"]), cols(a["L0_attn_ln_b"])], 1))
    A["fc_b"] = cols(a["L0_attn_fc_b"])
    A["cproj"] = tiled(a["L0_attn_cproj_w"])
    A["cproj_b"] = cols(a["L0_attn_cproj_b"])
    A["out_wT"] = tiled(np.ascontiguousarray(a["L0_attn_out_w"].T))
    A["gate_wT"] = np.ascontiguousarray(a["L0_ffn_gate_w"].T)
    A["w13"] = np.ascontiguousarray(np.concatenate([a["L0_ffn_w1"], a["L0_ffn_w3"]], 2).transpose(1, 0, 2))
    w2 = np.zeros((EXPERTS, HIDDEN_TILES * P, D), f)
    w2[:, :HIDDEN] = a["L0_ffn_w2"]
    A["w2"] = np.ascontiguousarray(w2.reshape(EXPERTS, HIDDEN_TILES, P, D).transpose(2, 0, 1, 3))
    wq, bq = a["L1_attn_Wqkv"], a["L1_attn_bqkv"]
    half = D // 2
    starts = [0, half, D, D + half]
    A["qk_w"] = np.ascontiguousarray(np.stack([np.tile(wq[:, s:s + half], (1, 2)) for s in starts], 1))
    A["qk_b"] = np.ascontiguousarray(np.stack([np.tile(bq[s:s + half], 2) for s in starts], 1))
    A["wv"] = np.ascontiguousarray(wq[:, 2 * D:])
    A["bv"] = rows(bq[2 * D:])
    om = np.zeros((P, 2 * P), f)
    for n in range(HEADS // 2):
        om[n * HEAD_DIM:(n + 1) * HEAD_DIM, n * FEATS:(n + 1) * FEATS] = a["L1_attn_omega"]
        om[half + n * HEAD_DIM:half + (n + 1) * HEAD_DIM, n * FEATS:(n + 1) * FEATS] = -0.5
    A["omega"] = om
    A["wout"] = np.ascontiguousarray(a["L1_attn_Wout"])
    A["bout"] = rows(a["L1_attn_bout"])
    A["ff_in"] = np.ascontiguousarray(np.stack([a["L1_ffn_w1_w"].T, a["L1_ffn_w2_w"].T], 1))
    A["ff_h"] = np.ascontiguousarray(np.concatenate([tiled(np.ascontiguousarray(a[n].T)) for n in ("L1_ffn_h1_w", "L1_ffn_h2_w")], 1))
    A["ff_s"] = np.ascontiguousarray(np.stack([cols(a[f"L1_ffn_{n}_s"]) for n in ("w1", "w2", "h1", "h2")], 1))
    A["ff_out"] = tiled(np.ascontiguousarray(a["L1_ffn_w3_w"].T))
    A["ff_out_s"] = rows(a["L1_ffn_w3_s"])
    c = np.zeros((P, C_ALL), f)
    c[:, C_IDENT:C_IDENT + P] = np.eye(P)
    c[:, C_BEFORE:C_BEFORE + P] = np.triu(np.ones((P, P)), 1)
    own = np.arange(P) % 32 // HEAD_DIM
    c[:, C_KVMASK:C_KVMASK + P] = own[:, None] == np.arange(P)[None, :] // FEATS
    c[:, C_IOTA:C_IOTA + EXPERTS] = np.arange(EXPERTS)
    c[:, C_BASE:C_BASE + EXPERTS] = np.arange(EXPERTS) * REGION
    c[:, C_UPTO:C_TILE] = np.tril(np.ones((EXPERTS, EXPERTS))).reshape(-1)
    c[:, C_TILE:C_ROW] = np.arange(SLOT_TILES)
    c[:, C_ROW:C_ALL] = np.arange(SLOT_TILES) * P
    A["const"] = c
    return A


def kernel(**inputs):
    import concourse.bacc as bacc
    from concourse.bass_utils import run_bass_kernel_spmd

    nc = bacc.Bacc("TRN2", target_bir_lowering=False, num_devices=1)
    laid = layouts({n: np.asarray(v) for n, v in inputs.items()})
    arrays, A = {}, {}
    for name, a in laid.items():
        arrays[f"in_{name}"] = a
        A[name] = nc.dram_tensor(f"in_{name}", a.shape, mybir.dt.from_np(a.dtype), kind="ExternalInput").ap()
    out = nc.dram_tensor("out", [TOKENS, D], mybir.dt.float32, kind="ExternalOutput").ap()
    build(nc, A, out)
    r = run_bass_kernel_spmd(nc, [arrays], core_ids=[0])
    return r.results[0]["out"].reshape(BATCHES, SEQ, D)
```

```python
import numpy as np
import concourse.bass as bass
from concourse import mybir
from contextlib import ExitStack

P = 128
BATCHES, SEQ, D = 8, 256, 128
TOKENS = BATCHES * SEQ
TILES = SEQ // P
INNER, TAPS, GROUPS = 256, 4, 8
PAD = TAPS - 1
EXPERTS, TOP_K, HIDDEN = 8, 2, 352
HIDDEN_TILES = -(-HIDDEN // P)
SLOT_TILES = TOKENS * TOP_K // P + EXPERTS - 1
DUMMY_TILES = EXPERTS - 1
REGION = TOKENS + P
ROWS = EXPERTS * REGION + DUMMY_TILES * P
HEADS, FEATS = 16, 32
HEAD_DIM = D // HEADS
GROUP_HEADS = P // FEATS
HEAD_GROUPS = HEADS // GROUP_HEADS
FF = 512
FF_TILES = FF // P
FLY = 3
EPS = 1e-5

C_IDENT, C_BEFORE, C_KVMASK = 0, P, 2 * P
C_IOTA = 3 * P
C_BASE = C_IOTA + EXPERTS
C_UPTO = C_BASE + EXPERTS
C_TILE = C_UPTO + EXPERTS * EXPERTS
C_ROW = C_TILE + SLOT_TILES
MEMSETS = 5
C_FIRST = C_ROW + SLOT_TILES
C_ALL = C_FIRST + P


def steps(engine, count, lag, step, ahead=0):
    for i in range(lag + 1):
        step(i)
    with engine.Fori(lag + 1, count - ahead) as i:
        step(i)
    for i in range(count - ahead, count + lag):
        step(i)


def alone(engine, carrier):
    engine.sem_inc(carrier, 1)


def live(n, count):
    return not isinstance(n, int) or 0 <= n < count


def wait(engine, semaphore, value):
    if not isinstance(value, int) or value > 0:
        engine.wait_ge(semaphore, value)


def build(nc, A, out):
    fp32, f32r, bf16 = mybir.dt.float32, mybir.dt.float32r, mybir.dt.bfloat16
    u32, i32 = mybir.dt.uint32, mybir.dt.int32
    ALU, ACT, AX = mybir.AluOpType, mybir.ActivationFunctionType, mybir.AxisListType

    ctx = ExitStack()
    with ctx:
        def sb(name, shape, dt=fp32):
            return ctx.enter_context(nc.sbuf_tensor("sb_" + name, shape, dt))

        def sems(prefix, names):
            return {n: ctx.enter_context(nc.semaphore(f"{prefix}_{n}")) for n in names.split()}

        routed = nc.dram_tensor("routed", [ROWS, D], fp32).ap()
        answers = nc.dram_tensor("answers", [SLOT_TILES * P, D], fp32).ap()

        const = sb("const", [P, C_ALL])
        ident = const[:, C_IDENT:C_IDENT + P]
        first_row = const[:, C_FIRST:C_FIRST + P]
        x_kept = sb("x_kept", [P, BATCHES, TILES * D])
        x_in = sb("x_in", [P, BATCHES, TILES * D])
        xT_in = sb("xT_in", [P, BATCHES, PAD + SEQ])
        w_h = sb("w_h", [P, 2, D])
        w_gate = sb("w_gate", [P, INNER])
        conv_bd = sb("conv_bd", [P, 2, TAPS * P])
        conv_b = sb("conv_b", [P, INNER])
        fc_wT = sb("fc_wT", [P, 2, D])
        ln_gb = sb("ln_gb", [P, 4])
        fc_b = sb("fc_b", [P, 1])
        cproj = sb("cproj", [P, 2, D])
        cproj_b = sb("cproj_b", [P, 2])
        out_wT = sb("out_wT", [P, 2, D])
        gate_wT = sb("gate_wT", [P, EXPERTS])
        w2 = sb("w2", [P, EXPERTS, HIDDEN_TILES, D])
        qk_w = sb("qk_w", [P, 4, P])
        qk_b = sb("qk_b", [P, 4])
        wv = sb("wv", [P, D])
        bv = sb("bv", [P, D])
        omega = sb("omega", [P, 2 * P])
        wout = sb("wout", [P, D])
        bout = sb("bout", [P, D])
        ff_in = conv_bd[:, :, :]
        ff_s = sb("ff_s", [P, 4, FF_TILES])
        ff_out_s = sb("ff_out_s", [P, D])

        def room(tile):
            flat = tile[:, :, :].rearrange("p b t -> p (b t)")
            return flat[:, 0:FF_TILES * FF].rearrange("p (k o) -> p k o", o=FF)
        ff_h = [room(x_in), room(xT_in)]

        before = sb("before", [P, P], bf16)
        ones_bf = sb("ones_bf", [P, P], bf16)
        ones = sb("ones", [P, FEATS])
        zeros = sb("zeros", [P, D])
        minus_half = sb("minus_half", [P, TILES])
        eps = sb("eps", [P, TILES])
        front_hi = sb("front_hi", [P, TAPS + 1, INNER], f32r)
        front_lo = sb("front_lo", [P, TAPS + 1, INNER], f32r)
        fc_g = sb("fc_g", [P, 2, D])
        fc_bias = sb("fc_bias", [P, 1])
        cproj_bb = sb("cproj_bb", [P, 2, P])
        mid_out = sb("mid_out", [P, D])
        out_bias = sb("out_bias", [P, D])
        w13_hi = sb("w13_hi", [P, EXPERTS, 2 * HIDDEN], f32r)
        w13_lo = sb("w13_lo", [P, EXPERTS, 2 * HIDDEN], f32r)
        qk_hi, qk_lo = sb("qk_hi", [P, 4, P], f32r), sb("qk_lo", [P, 4, P], f32r)
        om_hi, om_lo = sb("om_hi", [P, 2 * P], f32r), sb("om_lo", [P, 2 * P], f32r)
        fh_hi, fh_lo = sb("fh_hi", [P, 2 * FF_TILES, FF], f32r), sb("fh_lo", [P, 2 * FF_TILES, FF], f32r)
        ff_out_w = sb("ff_out_w", [P, FF_TILES, D])

        xT_hi, xT_lo = sb("xT_hi", [P, PAD + SEQ], f32r), sb("xT_lo", [P, PAD + SEQ], f32r)
        work = sb("work", [P, 4, TILES * INNER])
        gate, conv, h, hn = (work[:, n, :].rearrange("p (t f) -> p t f", f=INNER) for n in range(4))
        hT = sb("hT", [P, TILES, 2 * P])
        hnT = sb("hnT", [P, 2, SEQ])
        mid = sb("mid", [P, SEQ])
        res = sb("res", [P, TILES * D])
        x1 = sb("x1", [P, TILES * D])
        x1T = sb("x1T", [P, SEQ])
        stats = sb("stats", [P, TILES, 6])
        mv = sb("mv", [P, TILES, 2])
        veps = sb("veps", [P, TILES])
        rstd = sb("rstd", [P, TILES])
        stats_h = sb("stats_h", [P, TILES, 6])
        mv_h = sb("mv_h", [P, TILES, 2])
        veps_h = sb("veps_h", [P, TILES])
        rstd_h = sb("rstd_h", [P, TILES])
        top = sb("top", [P, TILES, EXPERTS])
        top_at = sb("top_at", [P, TILES, EXPERTS], u32)
        below = sb("below", [P, TILES, EXPERTS])
        exps = sb("exps", [P, TILES, EXPERTS])
        denom = sb("denom", [P, TILES])
        rdenom = sb("rdenom", [P, TILES])
        score = sb("score", [P, TILES, TOP_K])
        chosen_at = sb("chosen_at", [P, TILES, TOP_K])
        chosen = sb("chosen", [P, BATCHES, TILES * TOP_K, EXPERTS])
        either = sb("either", [P, TILES, EXPERTS], bf16)
        earlier = sb("earlier", [P, TILES, EXPERTS], bf16)
        rank = sb("rank", [P, TILES, EXPERTS])
        rank_of = sb("rank_of", [P, TILES * TOP_K, EXPERTS])
        row_f = sb("row_f", [P, TILES * TOP_K])
        rows_f = sb("rows_f", [P, BATCHES, TILES * TOP_K])
        row = sb("row", [P, TILES * TOP_K], u32)
        row_all = sb("row_all", [P, BATCHES, TILES * TOP_K], u32)
        xs = sb("xs", [P, TILES * TOP_K, D])

        n_tiles_f = sb("n_tiles_f", [P, EXPERTS])
        n_tiles_i = sb("n_tiles_i", [P, EXPERTS], i32)
        n_tiles_s = sb("n_tiles_s", [P, EXPERTS], i32)
        n_tiles = sb("n_tiles", [P, EXPERTS])
        upto_p = sb("upto_p", [P, EXPERTS, EXPERTS])
        upto = sb("upto", [P, EXPERTS])
        skip_rows = sb("skip_rows", [P, EXPERTS])
        past = sb("past", [P, SLOT_TILES, EXPERTS])
        past_rows = sb("past_rows", [P, SLOT_TILES, EXPERTS])
        ends = sb("ends", [P, EXPERTS], i32)
        shift_r = sb("shift_r", [P, EXPERTS])
        shift = sb("shift", [P, EXPERTS])
        shift_of = sb("shift_of", [P, BATCHES * TILES * TOP_K])
        expert_f = sb("expert_f", [P, SLOT_TILES])
        start_f = sb("start_f", [P, SLOT_TILES])
        start_f2 = sb("start_f2", [P, SLOT_TILES])
        expert_t = sb("expert_t", [P, SLOT_TILES], i32)
        start_t = sb("start_t", [P, SLOT_TILES], i32)

        fly = (HIDDEN_TILES * P,) * 3 + (D, D)
        stage = sb("stage", [P, max(EXPERTS * 2 * HIDDEN, FLY * sum(fly) + 2 * FF)])
        w13 = stage[:, 0:EXPERTS * 2 * HIDDEN].rearrange("p (e c) -> p e c", e=EXPERTS)
        starts = [FLY * sum(fly[:n]) for n in range(len(fly) + 1)]
        hid_room, hidT_room, act1_room, rows_in, rows_out = (stage[:, a:b] for a, b in zip(starts, starts[1:]))
        rows_in, rows_out = (r.rearrange("p (j d) -> p j d", d=D) for r in (rows_in, rows_out))
        f_res = stage[:, starts[-1]:starts[-1] + TILES * D]
        ff_out = stage[:, starts[-1] + FF:starts[-1] + 2 * FF].rearrange("p (k d) -> p k d", d=D)
        rT_hi, rT_lo = sb("rT_hi", [P, FLY, P], f32r), sb("rT_lo", [P, FLY, P], f32r)
        hid, hidT = (r.rearrange("p (j f) -> p j f", j=FLY) for r in (hid_room, hidT_room))
        act1 = act1_room[:, 0:FLY * HIDDEN].rearrange("p (j f) -> p j f", j=FLY)

        row_now = sb("row_now", [P, TILES * TOP_K], u32)
        got = hT[:, :, :].rearrange("p t (k d) -> p t k d", d=D)
        kv, kvT = (hnT[:, n, :].rearrange("p (a f) -> p a f", f=P) for n in range(2))
        sum1, v_tok = (work[:, n, 0:SEQ].rearrange("p (t d) -> p t d", d=D) for n in range(2))
        v_use = mid[:, :].rearrange("p (t d) -> p t d", d=D)
        x2, x2T = work[:, 0, SEQ:], work[:, 1, SEQ:]
        den, rden = work[:, 2, 0:SEQ], work[:, 2, SEQ:]
        att, x3 = work[:, 3, 0:SEQ], work[:, 3, SEQ:]
        x2T_hi, x2T_lo = xT_hi[:, 0:SEQ], xT_lo[:, 0:SEQ]
        st = hid_room[:, 0:4 * SEQ].rearrange("p (s t) -> p s t", t=SEQ)
        kp = hidT_room[:, 0:TILES * HEADS * FEATS].rearrange("p (t f) -> p t f", t=TILES)
        qp = act1_room[:, 0:HEAD_GROUPS * SEQ].rearrange("p (g t) -> p g t", t=SEQ)
        def over(parts, first, n, k):
            return parts[:, :, :].rearrange("p e c -> p (e c)")[:, first:first + n * k].rearrange("p (n k) -> p n k", k=k)
        x3T_hi, x3T_lo = (over(w, 0, BATCHES, SEQ) for w in (w13_hi, w13_lo))
        a_hi, a_lo = (over(w, TOKENS, FF_TILES, SEQ) for w in (w13_hi, w13_lo))
        g_hi, g_lo = (over(w, TOKENS + FF_TILES * SEQ, FF_TILES, SEQ) for w in (w13_hi, w13_lo))
        st_hi, st_lo = (over(w, TOKENS + 2 * FF_TILES * SEQ, 4, SEQ) for w in (w13_hi, w13_lo))
        fi_hi, fi_lo = (over(w, 0, 2, FF) for w in (front_hi, front_lo))

        f_silu = work[:, 0, :].rearrange("p (m t) -> p m t", t=SEQ)
        f_a, f_g = room(x_in)[:, :, 0:SEQ], room(x_in)[:, :, SEQ:]
        f_last = room(xT_in)[:, :, 0:SEQ]
        f_out = work[:, 2, 0:TILES * D]
        odd = sb("odd", [P, 2])
        odd_any = sb("odd_any", [P, 2])
        odd_i = sb("odd_i", [FEATS, 1], i32)

        ps = ctx.enter_context(nc.psum_tensor("ps", [P, 8, 512], fp32))

        in_bank = (0, 1, 7, 0)

        def half_bank(bank, m):
            return ps[:, bank + m % 2, m // 2 * SEQ:(m // 2 + 1) * SEQ]

        ld = sems("ld", "const front x_first x conv w13_a w13_b w2 att ff")
        wt = sems("wt", "before memset hid_zero conv_mm front_hi front_lo fc_g cproj_bb small_mm small x_bias zero_rows moe_hi moe_lo att_hi att_lo ff_hi ff_lo fi_hi fi_lo ff_out odd_any odd_mm odd_i")
        g0 = sems("g0", "x_hi x_lo front gate conv h mv rstd hn tr hT hnT fc mid out res"
                  " mv1 rstd1 x1 kept x1_tr x1T logits choose top_at below exps weigh score"
                  " rank_mm added rank place row carry xs sent")
        carrier = sems("carrier", "dve pool")
        tb = sems("tb", "count ends step ready place placed")
        mo = sems("mo", "tr hi lo up act1 hid hid_tr hidT down out")
        mo_out = [ctx.enter_context(nc.semaphore(f"mo_stored{j}")) for j in range(FLY)]
        mo_in = [ctx.enter_context(nc.semaphore(f"mo_loaded{j}")) for j in range(FLY)]
        at = sems("at", "row got sum1 res mv rstd x2 kept tr x2T lo qk st st_hi st_lo v_mm v_tok v_use"
                  " kf kp qf qp kv_mm kv kv_tr kvT nd den rden att out"
                  " res3 mv3 rstd3 x3 kept3 tr3 x3_hi x3_lo")
        ff = sems("ff", "in_mm silu act a_hi a_lo g1 g_hi g_lo g2 h1_mm h2_mm out_mm res mv rstd out stored")

        block = ctx.enter_context(nc.Block())

        def loaded(engine, table, first, count, most):
            return nc.values_load_multi_w_load_instructions(table[0:1, bass.ds(first, count)], engines=(engine,),
                                                            min_val=0, max_val=most, skip_runtime_bounds_check_because="the table is built within these bounds")[1]

        @block.sync
        def _(sp):
            for tile, src in ((w_h, "w_h"), (conv_bd, "conv_bd")):
                sp.dma_start(tile[:, :, :], A[src]).then_inc(ld["front"], 16)
            sp.dma_start(xT_in[:, 0, :], A["xT"][:, 0, :]).then_inc(ld["x_first"], 16)
            for tile, src in ((fc_wT, "fc_wT"), (cproj, "cproj"), (out_wT, "out_wT")):
                sp.dma_start(tile[:, :, :], A[src]).then_inc(ld["conv"], 16)
            sp.dma_start(xT_in[:, 1:, :], A["xT"][:, 1:, :]).then_inc(ld["x"], 16)
            sp.dma_start(x_in[:, :, :], A["x_tok"]).then_inc(ld["x"], 16)
            for half, sem in enumerate((ld["w13_a"], ld["w13_b"])):
                part = slice(half * EXPERTS // 2, (half + 1) * EXPERTS // 2)
                sp.dma_start(w13[:, part, :], A["w13"][:, part, :]).then_inc(sem, 16)
            sp.dma_start(w2[:, :, :, :], A["w2"]).then_inc(ld["w2"], 16)
            sp.wait_ge(wt["memset"], MEMSETS)
            sp.dma_start(routed[EXPERTS * REGION:ROWS, :].rearrange("(t p) d -> p t d", p=P),
                         zeros[:, :].unsqueeze(1).to_broadcast([P, DUMMY_TILES, D])).then_inc(wt["zero_rows"], 16)
            for tile, src in ((qk_w, "qk_w"),):
                sp.dma_start(tile[:, :, :], A[src]).then_inc(ld["att"], 16)
            for tile, src in ((qk_b, "qk_b"), (wv, "wv"), (bv, "bv"), (omega, "omega"), (wout, "wout"), (bout, "bout")):
                sp.dma_start(tile[:, :], A[src]).then_inc(ld["att"], 16)
            sp.dma_start(ff_s[:, :, :], A["ff_s"]).then_inc(ld["ff"], 16)
            sp.dma_start(ff_out_s[:, :], A["ff_out_s"]).then_inc(ld["ff"], 16)
            sp.wait_ge(wt["conv_mm"], 2)
            sp.dma_start(ff_in[:, :, :], A["ff_in"]).then_inc(ld["ff"], 16)

            sp.wait_ge(tb["ends"], 1)
            for e in range(0, EXPERTS, 2):
                end = sp.value_load(ends[0:1, e:e + 1], min_val=0, max_val=EXPERTS * REGION)
                sp.dma_start(routed[bass.ds(end, P), :], zeros[:, :]).then_inc(wt["zero_rows"], 16)
            sp.wait_ge(tb["ready"], 1)
            sp.wait_ge(g0["sent"], 64 * BATCHES)
            sp.wait_ge(wt["zero_rows"], 16 * (EXPERTS + 1))

            def rows_step(i):
                start = loaded(mybir.EngineType.SP, start_t, FLY * i, FLY, ROWS - P)
                for j in range(FLY):
                    t = FLY * i + j
                    wait(sp, mo["tr"], t - FLY + 1)
                    sp.dma_start(rows_in[:, j, :], routed[bass.ds(start[j], P), :]).then_inc(mo_in[j], 16)
            steps(sp, SLOT_TILES // FLY, 0, rows_step)

            def store(b):
                sp.wait_ge(ff["out"], b + 1)
                sp.dma_start(out.rearrange("(b t p) d -> b p t d", t=TILES, p=P)[b],
                             f_out.rearrange("p (t d) -> p t d", d=D)).then_inc(ff["stored"], 16)
            steps(sp, BATCHES, 0, store)
            sp.wait_ge(ff["stored"], 16 * BATCHES)

        @block.gpsimd
        def _(pool):
            pool.memset(zeros[:, :], 0.0).then_inc(wt["memset"], 1)
            pool.memset(ones[:, :], 1.0).then_inc(wt["memset"], 1)
            pool.memset(ones_bf[:, :], 1.0).then_inc(wt["memset"], 1)
            pool.memset(minus_half[:, :], -0.5).then_inc(wt["memset"], 1)
            pool.memset(eps[:, :], EPS).then_inc(wt["memset"], 1)

            def inverse_root(sem_mv, sem, n, mv_, veps_, rstd_, tiles):
                pool.wait_ge(sem_mv, 2 * n)
                nc.gpsimd.tensor_tensor(veps_[:, 0:tiles], mv_[:, 0:tiles, 1], eps[:, 0:tiles], ALU.add).then_inc(sem, 1)
                pool.wait_ge(sem, 2 * n - 1)
                for t in range(0, tiles, TILES):
                    last = nc.gpsimd.tensor_tensor(rstd_[:, t:t + TILES], veps_[:, t:t + TILES], minus_half[:, :], ALU.pow)
                last.then_inc(sem, 1)

            pool.wait_ge(wt["memset"], MEMSETS)
            def route_step(i):
                b = i - 4
                if live(b, BATCHES):
                    pool.wait_ge(g0["xs"], b + 1)
                    pool.wait_ge(g0["row"], b + 1)
                    alone(pool, carrier["pool"])

                def scatter(r):
                    nc.gpsimd.indirect_dma_start(
                        routed[:, :], bass.IndirectOffsetOnAxis(ap=row[:, r:r + 1], axis=0),
                        xs[:, r, :], None).then_inc(g0["sent"], 16)
                if live(b, BATCHES):
                    for r in range(TOP_K):
                        scatter(r)
                b = i - 2
                if live(b, BATCHES):
                    inverse_root(g0["mv1"], g0["rstd1"], b + 1, mv, veps, rstd, TILES)
                b = i - 4
                if live(b, BATCHES):
                    for r in range(TOP_K, TILES * TOP_K):
                        scatter(r)
                if live(i, BATCHES):
                    inverse_root(g0["mv"], g0["rstd"], i + 1, mv_h, veps_h, rstd_h, TILES)
                    if isinstance(i, int) and i == 0:
                        pool.wait_ge(ld["x"], 32)
                        pool.wait_ge(wt["small"], 3)
                        x_tiles = x_in[:, :, :].rearrange("p b (t d) -> p (b t) d", d=D)
                        nc.gpsimd.tensor_tensor(x_tiles, x_tiles, out_bias[:, :].unsqueeze(1).to_broadcast([P, BATCHES * TILES, D]),
                                                ALU.add).then_inc(wt["x_bias"], 1)
                    pool.wait_ge(wt["moe_hi"], i + 1)
                    nc.gpsimd.tensor_tensor(w13_lo[:, i, :], w13[:, i, :], w13_hi[:, i, :].bitcast(fp32),
                                            ALU.subtract).then_inc(wt["moe_lo"], 1)
            steps(pool, BATCHES, 4, route_step)
            pool.wait_ge(wt["moe_lo"], EXPERTS)
            pool.memset(hid[:, :, :], 0.0).then_inc(wt["hid_zero"], 1)

            pool.wait_ge(ld["att"], 16 * 7)
            nc.gpsimd.tensor_copy(qk_hi[:, :, :], qk_w[:, :, :]).then_inc(wt["att_hi"], 1)
            nc.gpsimd.tensor_copy(om_hi[:, :], omega[:, :]).then_inc(wt["att_hi"], 1)
            pool.wait_ge(wt["att_hi"], 2)
            nc.gpsimd.tensor_tensor(qk_lo[:, :, :], qk_w[:, :, :], qk_hi[:, :, :].bitcast(fp32), ALU.subtract).then_inc(wt["att_lo"], 1)
            nc.gpsimd.tensor_tensor(om_lo[:, :], omega[:, :], om_hi[:, :].bitcast(fp32), ALU.subtract).then_inc(wt["att_lo"], 1)
            pool.wait_ge(ld["ff"], 16 * 6)
            for half, whole in enumerate(ff_h):
                with pool.Fori(0, FF_TILES) as k:
                    r = half * FF_TILES + k
                    nc.gpsimd.tensor_copy(fh_hi[:, r, :], whole[:, k, :]).then_inc(wt["ff_hi"], 1)
                    pool.wait_ge(wt["ff_hi"], r + 1)
                    nc.gpsimd.tensor_tensor(fh_lo[:, r, :], whole[:, k, :], fh_hi[:, r, :].bitcast(fp32), ALU.subtract).then_inc(wt["ff_lo"], 1)
            nc.gpsimd.tensor_copy(fi_hi, ff_in).then_inc(wt["fi_hi"], 1)
            pool.wait_ge(wt["fi_hi"], 1)
            nc.gpsimd.tensor_tensor(fi_lo, ff_in, fi_hi.bitcast(fp32), ALU.subtract).then_inc(wt["fi_lo"], 1)
            nc.gpsimd.tensor_tensor(ff_out_w[:, :, :], ff_out[:, :, :],
                                    ff_out_s[:, :].unsqueeze(1).to_broadcast([P, FF_TILES, D]), ALU.mult).then_inc(wt["ff_out"], 1)

            pool.wait_ge(tb["placed"], 1)
            for j in range(FLY):
                pool.wait_ge(mo_out[j], 16 * (SLOT_TILES // FLY))
            def attention_step(i):
                def gather(ks):
                    for r in ks:
                        nc.gpsimd.indirect_dma_start(
                            got[:, r // TOP_K, r % TOP_K, :], None,
                            answers[:, :], bass.IndirectOffsetOnAxis(ap=row_now[:, r:r + 1], axis=0)).then_inc(at["got"], 16)
                if live(i, BATCHES):
                    wait(pool, at["got"], 64 * i)
                    nc.gpsimd.tensor_copy(row_now[:, :], row_all[:, i, :]).then_inc(at["row"], 1)
                    pool.wait_ge(at["row"], i + 1)
                    wait(pool, at["sum1"], i)
                    alone(pool, carrier["pool"])
                    gather(range(TOP_K))
                b = i - 1
                if live(b, BATCHES):
                    inverse_root(at["mv"], at["rstd"], b + 1, mv, veps, rstd, TILES)
                b = i - 6
                if live(b, BATCHES):
                    inverse_root(at["mv3"], at["rstd3"], b + 1, mv_h, veps_h, rstd_h, TILES)
                if live(i, BATCHES):
                    gather(range(TOP_K, TILES * TOP_K))
                b = i - 3
                if live(b, BATCHES):
                    pool.wait_ge(at["st_hi"], b + 1)
                    wait(pool, at["qf"], b)
                    nc.gpsimd.tensor_tensor(st_lo[:, :, :], st[:, :, :], st_hi[:, :, :].bitcast(fp32), ALU.subtract).then_inc(at["st_lo"], 1)
            steps(pool, BATCHES, 6, attention_step)

            def mlp_step(i):
                b = i - 3
                if live(b, BATCHES):
                    inverse_root(ff["mv"], ff["rstd"], b + 1, mv, veps, rstd, TILES)
                if live(i, BATCHES):
                    for m in range(FF_TILES):
                        pool.wait_ge(ff["a_hi"], FF_TILES * i + m + 1)
                        nc.gpsimd.tensor_tensor(a_lo[:, m, :], f_a[:, m, :], a_hi[:, m, :].bitcast(fp32), ALU.subtract).then_inc(ff["a_lo"], 1)
            steps(pool, BATCHES, 3, mlp_step)

        @block.scalar
        def _(act):
            act.dma_start(w_gate[:, :], A["w_gate"]).then_inc(ld["front"], 16)
            act.dma_start(const[:, :], A["const"]).then_inc(ld["const"], 16)
            for tile, src in ((conv_b, "conv_b"), (ln_gb, "ln_gb"), (fc_b, "fc_b"),
                              (cproj_b, "cproj_b"), (gate_wT, "gate_wT")):
                act.dma_start(tile[:, :], A[src]).then_inc(ld["conv"], 16)

            act.wait_ge(ld["front"], 16 * 3)
            nc.scalar.activation(front_hi[:, TAPS, :], w_gate[:, :], ACT.Copy).then_inc(wt["front_hi"], 1)
            for t in range(2):
                act.wait_ge(wt["conv_mm"], t + 1)
                nc.scalar.activation(front_hi[:, 0:TAPS, t * P:(t + 1) * P],
                                     ps[:, t, :].rearrange("p (k o) -> p k o", o=P), ACT.Copy).then_inc(wt["front_hi"], 1)

            def high_part(b):
                if isinstance(b, int) and b <= 1:
                    act.wait_ge(ld["x"] if b else ld["x_first"], 16 * (b + 1))
                wait(act, g0["front"], b)
                nc.scalar.activation(xT_hi[:, :], xT_in[:, b, :], ACT.Copy).then_inc(g0["x_hi"], 1)
            high_part(0)

            def conv_step(i):
                if live(i, BATCHES):
                    act.wait_ge(g0["front"], i + 1)
                    wait(act, g0["h"], i)
                    nc.scalar.activation(gate[:, :, :], ps[:, 0:2, INNER:], ACT.Silu).then_inc(g0["gate"], 1)
                if live(i + 1, BATCHES):
                    high_part(i + 1)
                b = i - 1
                if live(b, BATCHES):
                    act.wait_ge(g0["tr"], b + 1)
                    wait(act, g0["out"], b)
                    nc.scalar.activation(hT[:, :, :].rearrange("p t f -> p (t f)"), ps[:, 2, :], ACT.Copy).then_inc(g0["hT"], 1)
                b = i - 3
                if live(b, BATCHES):
                    act.wait_ge(g0["below"], b + 1)
                    nc.scalar.activation(exps[:, :, :], below[:, :, :], ACT.Exp).then_inc(g0["exps"], 1)
                b = i - 2
                if live(b, BATCHES):
                    act.wait_ge(g0["x1_tr"], b + 1)
                    wait(act, g0["logits"], b)
                    nc.scalar.activation(x1T[:, :], ps[:, 6, 0:SEQ], ACT.Copy).then_inc(g0["x1T"], 1)
                b = i - 1
                if live(b, BATCHES):
                    act.wait_ge(g0["fc"], b + 1)
                    act.wait_ge(wt["small"], 2)
                    nc.scalar.activation(mid[:, :], ps[:, 4, 0:SEQ], ACT.Silu, bias=fc_bias[:, 0:1]).then_inc(g0["mid"], 1)
                b = i - 2
                if live(b, BATCHES):
                    act.wait_ge(g0["x1"], b + 1)
                    nc.scalar.activation(x_kept[:, b, :], x1[:, :], ACT.Copy).then_inc(g0["kept"], 1)
                b = i - 3
                if live(b, BATCHES):
                    act.wait_ge(g0["score"], b + 1)
                    act.wait_ge(g0["kept"], b + 1)
                    wait(act, g0["sent"], 64 * b)
                    for t in range(TILES):
                        for k in range(TOP_K):
                            last = nc.scalar.activation(xs[:, TOP_K * t + k, :], x_kept[:, b, t * D:(t + 1) * D],
                                                        ACT.Copy, scale=score[:, t, k:k + 1])
                    last.then_inc(g0["xs"], 1)
                if live(i, BATCHES):
                    first = isinstance(i, int) and i < EXPERTS // 2
                    act.wait_ge(ld["w13_a"] if first else ld["w13_b"], 16)
                    nc.scalar.activation(w13_hi[:, i, :], w13[:, i, :], ACT.Copy).then_inc(wt["moe_hi"], 1)
            steps(act, BATCHES, 3, conv_step, ahead=1)

            act.wait_ge(tb["ends"], 1)
            for e in range(1, EXPERTS, 2):
                end = act.value_load(ends[0:1, e:e + 1], min_val=0, max_val=EXPERTS * REGION)
                act.dma_start(routed[bass.ds(end, P), :], zeros[:, :]).then_inc(wt["zero_rows"], 16)

            def expert_step(i):
                if isinstance(i, int) and i == 1:
                    act.wait_ge(wt["moe_lo"], EXPERTS)
                    act.dma_start(ff_out[:, :, :], A["ff_out"]).then_inc(ld["ff"], 16)
                    act.wait_ge(g0["res"], BATCHES)
                    act.wait_ge(g0["front"], BATCHES)
                    for k, tile in enumerate(ff_h):
                        act.dma_start(tile, A["ff_h"][:, k * FF_TILES:(k + 1) * FF_TILES, :]).then_inc(ld["ff"], 16)
                for j in range(FLY):
                    t = FLY * i + j
                    if live(i, SLOT_TILES // FLY):
                        act.wait_ge(mo["tr"], t + 1)
                        wait(act, mo["up"], t - FLY + 1)
                        nc.scalar.activation(rT_hi[:, j, :], ps[:, 0, 0:P], ACT.Copy).then_inc(mo["hi"], 1)
                    u, ju = t - 1, (j - 1) % FLY
                    if live(u, SLOT_TILES):
                        act.wait_ge(mo["up"], u + 1)
                        wait(act, mo["hid"], u - FLY + 1)
                        nc.scalar.activation(act1[:, ju, :], ps[:, 2, 0:HIDDEN], ACT.Silu).then_inc(mo["act1"], 1)
                    u, ju = t - 5, (j - 5) % FLY
                    if live(u, SLOT_TILES):
                        act.wait_ge(mo["out"], u + 1)
                        act.dma_start(answers.rearrange("(t p) d -> t p d", p=P)[u], rows_out[:, ju, :]).then_inc(mo_out[ju], 16)
                    u, ju = t - 4, (j - 4) % FLY
                    if live(u, SLOT_TILES):
                        act.wait_ge(mo["down"], u + 1)
                        wait(act, mo_out[ju], 16 * (i + (j - 4) // FLY))
                        nc.scalar.activation(rows_out[:, ju, :], ps[:, 6, 0:D], ACT.Copy).then_inc(mo["out"], 1)
            steps(act, SLOT_TILES // FLY, 2, expert_step)

            def attention_step(i):
                b = i - 5
                if live(b, BATCHES):
                    act.wait_ge(at["kv_tr"], b + 1)
                    wait(act, at["nd"], b)
                    nc.scalar.activation(kvT[:, :, :].rearrange("p a f -> p (a f)"), ps[:, 6, 256:512], ACT.Copy).then_inc(at["kvT"], 1)
                b = i - 3
                if live(b, BATCHES):
                    act.wait_ge(at["qk"], b + 1)
                    wait(act, at["st_lo"], b)
                    for n in range(4):
                        nc.scalar.activation(st[0:64, n, :], ps[0:64, 1 + n // 2, n % 2 * SEQ:(n % 2 + 1) * SEQ],
                                             ACT.Identity, bias=qk_b[0:64, n:n + 1])
                b = i - 4
                if live(b, BATCHES):
                    act.wait_ge(at["kf"], b + 1)
                    wait(act, at["kv_mm"], b)
                    nc.scalar.activation(kp[:, :, :], ps[:, 4:6, :], ACT.Exp).then_inc(at["kp"], 1)
                b = i - 3
                if live(b, BATCHES):
                    for n in range(4):
                        last = nc.scalar.activation(st[64:128, n, :], ps[64:128, 1 + n // 2, n % 2 * SEQ:(n % 2 + 1) * SEQ],
                                                    ACT.Square, bias=qk_b[64:128, n:n + 1])
                    last.then_inc(at["st"], 1)
                b = i - 5
                if live(b, BATCHES):
                    act.wait_ge(at["nd"], b + 1)
                    wait(act, at["rden"], b)
                    nc.scalar.activation(den[:, :], ps[:, 7, SEQ:], ACT.Copy, bias=1e-6).then_inc(at["den"], 1)
                b = i - 4
                if live(b, BATCHES):
                    act.wait_ge(at["qf"], b + 1)
                    wait(act, at["nd"], b)
                    nc.scalar.activation(qp[:, :, :].rearrange("p g t -> p (g t)"),
                                         ps[:, 4:6, :].rearrange("p a t -> p (a t)"), ACT.Exp).then_inc(at["qp"], 1)
                b = i - 1
                if live(b, BATCHES):
                    act.wait_ge(at["tr"], b + 1)
                    wait(act, at["v_mm"], b)
                    wait(act, at["lo"], b)
                    nc.scalar.activation(x2T[:, :], ps[:, 0, 0:SEQ], ACT.Copy)
                    wait(act, at["qk"], b)
                    nc.scalar.activation(x2T_hi[:, :], ps[:, 0, 0:SEQ], ACT.Copy).then_inc(at["x2T"], 1)
                    act.wait_ge(at["x2"], b + 1)
                    nc.scalar.activation(x_kept[:, b, :], x2, ACT.Copy).then_inc(at["kept"], 1)
                b = i - 6
                if live(b, BATCHES):
                    act.wait_ge(at["tr3"], b + 1)
                    nc.scalar.activation(x3T_hi[:, b, :], ps[:, 0, SEQ:], ACT.Copy).then_inc(at["x3_hi"], 1)
                    act.wait_ge(at["x3"], b + 1)
                    nc.scalar.activation(x_kept[:, b, :], x3, ACT.Copy).then_inc(at["kept3"], 1)
            steps(act, BATCHES, 6, attention_step)

            def mlp_step(i):
                for m in range(FF_TILES):
                    if live(i, BATCHES):
                        n = FF_TILES * i + m
                        act.wait_ge(ff["in_mm"], n + 1)
                        wait(act, ff["act"], n - 1)
                        nc.scalar.activation(f_silu[:, m % 2, :], ps[:, in_bank[m], 0:SEQ], ACT.Silu,
                                             scale=ff_s[:, 0, m:m + 1]).then_inc(ff["silu"], 1)
                b = i - 2
                for m in range(FF_TILES):
                    if live(b, BATCHES):
                        act.wait_ge(ff["h2_mm"], FF_TILES * b + m + 1)
                        wait(act, ff["out_mm"], b)
                        nc.scalar.activation(f_last[:, m, :], half_bank(4, m), ACT.Gelu,
                                             scale=ff_s[:, 3, m:m + 1]).then_inc(ff["g2"], 1)
                b = i - 1
                for m in range(FF_TILES):
                    if live(b, BATCHES):
                        n = FF_TILES * b + m
                        act.wait_ge(ff["h1_mm"], n + 1)
                        wait(act, ff["g_lo"], n - FF_TILES + 1)
                        nc.scalar.activation(f_g[:, m, :], half_bank(2, m), ACT.Gelu,
                                             scale=ff_s[:, 2, m:m + 1]).then_inc(ff["g1"], 1)
            act.wait_ge(ld["ff"], 16 * 6)
            act.wait_ge(wt["ff_lo"], 2 * FF_TILES)
            steps(act, BATCHES, 3, mlp_step)

        @block.vector
        def _(dve):
            V = nc.vector

            def split(hi, lo, src, sem_hi, sem_lo, n):
                V.tensor_copy(hi, src).then_inc(sem_hi, 1)
                dve.wait_ge(sem_hi, n)
                V.tensor_tensor(lo, src, hi.bitcast(fp32), ALU.subtract).then_inc(sem_lo, 1)

            def moments(src, stats_, mv_, tiles, width, sem, n):
                for t in range(tiles):
                    last = V.bn_stats(stats_[:, t, :], src[:, t * width:(t + 1) * width])
                last.then_inc(sem, 1)
                dve.wait_ge(sem, 2 * n - 1)
                alone(dve, carrier["dve"])
                for t in range(tiles):
                    last = V.bn_aggr(mv_[:, t, :], stats_[:, t, :])
                last.then_inc(sem, 1)

            def normalise(dst, src, mv_, rstd_, tiles, width, sem):
                for t in range(tiles):
                    cols = slice(t * width, (t + 1) * width)
                    last = V.tensor_scalar(dst[:, cols], src[:, cols], mv_[:, t, 0:1], rstd_[:, t:t + 1],
                                           ALU.subtract, ALU.mult)
                last.then_inc(sem, 1)

            V.memset(earlier[:, :, :], 0.0).then_inc(wt["before"], 1)
            dve.wait_ge(ld["const"], 16)
            V.tensor_copy(before[:, :], const[:, C_BEFORE:C_BEFORE + P]).then_inc(wt["before"], 1)
            dve.wait_ge(wt["front_hi"], 1)
            V.tensor_tensor(front_lo[:, TAPS, :], w_gate[:, :], front_hi[:, TAPS, :].bitcast(fp32), ALU.subtract).then_inc(wt["front_lo"], 1)
            for t in range(2):
                dve.wait_ge(wt["front_hi"], t + 2)
                V.tensor_tensor(front_lo[:, 0:TAPS, t * P:(t + 1) * P], ps[:, t, :].rearrange("p (k o) -> p k o", o=P),
                                front_hi[:, 0:TAPS, t * P:(t + 1) * P].bitcast(fp32), ALU.subtract).then_inc(wt["front_lo"], 1)

            def small_weights():
                dve.wait_ge(wt["small_mm"], 1)
                V.tensor_copy(mid_out[:, :], ps[:, 4, 0:D]).then_inc(wt["small"], 1)
                dve.wait_ge(wt["small_mm"], 2)
                V.tensor_tensor(fc_bias[:, :], ps[:, 6, 0:1], fc_b[:, :], ALU.add).then_inc(wt["small"], 1)
                dve.wait_ge(wt["small_mm"], 3)
                V.tensor_copy(out_bias[:, :], ps[:, 5, 0:D]).then_inc(wt["small"], 1)

            iota = const[:, C_IOTA:C_IOTA + EXPERTS]
            base = const[:, C_BASE:C_BASE + EXPERTS]
            logits = ps[:, 6, SEQ:SEQ + TILES * EXPERTS].rearrange("p (t e) -> p t e", e=EXPERTS)
            rank_ps = ps[:, 7, 32:32 + TILES * EXPERTS].rearrange("p (t e) -> p t e", e=EXPERTS)

            def choose(b):
                dve.wait_ge(g0["logits"], b + 1)
                alone(dve, carrier["dve"])
                for t in range(TILES):
                    last = V.max(top[:, t, :], logits[:, t, :])
                last.then_inc(g0["choose"], 1)
                dve.wait_ge(g0["choose"], 4 * b + 1)
                alone(dve, carrier["dve"])
                for t in range(TILES):
                    last = V.max_index(top_at[:, t, :], top[:, t, :], logits[:, t, :])
                last.then_inc(g0["top_at"], 1)
                V.tensor_tensor(below[:, :, :], top[:, :, :], top[:, :, 0:1].to_broadcast([P, TILES, EXPERTS]),
                                ALU.subtract).then_inc(g0["below"], 1)
                dve.wait_ge(g0["top_at"], b + 1)
                V.tensor_copy(chosen_at[:, :, :], top_at[:, :, 0:TOP_K]).then_inc(g0["choose"], 1)
                dve.wait_ge(g0["choose"], 4 * b + 2)
                V.tensor_tensor(chosen[:, b, :, :].rearrange("p (t k) e -> p t k e", k=TOP_K),
                                iota.unsqueeze(1).unsqueeze(1).to_broadcast([P, TILES, TOP_K, EXPERTS]),
                                chosen_at[:, :, :].unsqueeze(3).to_broadcast([P, TILES, TOP_K, EXPERTS]),
                                ALU.is_equal).then_inc(g0["choose"], 1)
                dve.wait_ge(g0["choose"], 4 * b + 3)
                wait(dve, g0["rank_mm"], b)
                of_tile = chosen[:, b, :, :].rearrange("p (t k) e -> p t k e", k=TOP_K)
                V.tensor_tensor(either[:, :, :], of_tile[:, :, 0, :], of_tile[:, :, 1, :], ALU.add).then_inc(g0["choose"], 1)
                dve.wait_ge(g0["choose"], 4 * b + 4)
                V.tensor_tensor(earlier[:, 1, :], earlier[:, 0, :], either[:, 0, :], ALU.add).then_inc(g0["added"], 1)

            def weigh(b):
                dve.wait_ge(g0["exps"], b + 1)
                V.reduce_sum(denom[:, :], exps[:, :, :], axis=AX.X).then_inc(g0["weigh"], 1)
                dve.wait_ge(g0["weigh"], 2 * b + 1)
                V.reciprocal(rdenom[:, :], denom[:, :]).then_inc(g0["weigh"], 1)
                dve.wait_ge(g0["weigh"], 2 * b + 2)
                wait(dve, g0["xs"], b)
                V.tensor_tensor(score[:, :, :], exps[:, :, 0:TOP_K],
                                rdenom[:, :].unsqueeze(2).to_broadcast([P, TILES, TOP_K]), ALU.mult).then_inc(g0["score"], 1)

            def place(b):
                dve.wait_ge(g0["rank_mm"], b + 1)
                V.tensor_tensor(rank[:, :, :], rank_ps, base.unsqueeze(1).to_broadcast([P, TILES, EXPERTS]),
                                ALU.add).then_inc(g0["rank"], 1)
                V.tensor_tensor(earlier[:, 0, :], earlier[:, 1, :], either[:, 1, :], ALU.add).then_inc(g0["carry"], 1)
                dve.wait_ge(g0["rank"], b + 1)
                V.tensor_tensor(rank_of[:, :, :].rearrange("p (t k) e -> p t k e", k=TOP_K),
                                chosen[:, b, :, :].rearrange("p (t k) e -> p t k e", k=TOP_K),
                                rank[:, :, :].unsqueeze(2).to_broadcast([P, TILES, TOP_K, EXPERTS]),
                                ALU.mult).then_inc(g0["place"], 1)
                dve.wait_ge(g0["place"], 2 * b + 1)
                V.reduce_sum(row_f[:, :], rank_of[:, :, :], axis=AX.X).then_inc(g0["place"], 1)
                dve.wait_ge(g0["place"], 2 * b + 2)
                wait(dve, g0["sent"], 64 * b)
                V.tensor_copy(row[:, :], row_f[:, :])
                V.tensor_copy(rows_f[:, b, :], row_f[:, :]).then_inc(g0["row"], 1)

            h_flat, hn_flat = (x[:, :, :].rearrange("p t f -> p (t f)") for x in (h, hn))

            def low_part(b):
                dve.wait_ge(g0["x_hi"], b + 1)
                V.tensor_tensor(xT_lo[:, :], xT_in[:, b, :], xT_hi[:, :].bitcast(fp32), ALU.subtract).then_inc(g0["x_lo"], 1)
            low_part(0)
            dve.wait_ge(ld["conv"], 16 * 8)
            for t in range(2):
                V.tensor_copy(cproj_bb[:, t, :], cproj_b[:, t:t + 1].to_broadcast([P, P])).then_inc(wt["cproj_bb"], 1)
                V.tensor_scalar(fc_g[:, t, :], fc_wT[:, t, :], ln_gb[:, t:t + 1], None, ALU.mult).then_inc(wt["fc_g"], 1)

            def conv_step(i):
                if live(i - 3, BATCHES):
                    choose(i - 3)
                b = i - 1
                if live(b, BATCHES):
                    dve.wait_ge(g0["rstd"], 2 * b + 2)
                    wait(dve, g0["tr"], b)
                    normalise(hn_flat, h_flat, mv_h, rstd_h, TILES, INNER, g0["hn"])
                b = i - 2
                if live(b, BATCHES):
                    dve.wait_ge(g0["out"], b + 1)
                    wait(dve, g0["x1"], b)
                    if isinstance(b, int) and b == 0:
                        dve.wait_ge(wt["x_bias"], 1)
                    V.tensor_tensor(res[:, :], ps[:, 5, 0:SEQ], x_in[:, b, :], ALU.add).then_inc(g0["res"], 1)
                    dve.wait_ge(g0["res"], b + 1)
                    moments(res, stats, mv, TILES, D, g0["mv1"], b + 1)
                b = i - 2
                if live(b, BATCHES):
                    dve.wait_ge(g0["rstd1"], 2 * b + 2)
                    wait(dve, g0["kept"], b)
                    wait(dve, g0["x1_tr"], b)
                    normalise(x1, res, mv, rstd, TILES, D, g0["x1"])
                b = i - 1
                if live(b, BATCHES):
                    dve.wait_ge(g0["tr"], b + 1)
                    wait(dve, g0["fc"], b)
                    V.tensor_copy(hnT[:, :, :].rearrange("p k (t q) -> p t k q", q=P),
                                  ps[:, 3, :].rearrange("p (t k q) -> p t k q", k=2, q=P)).then_inc(g0["hnT"], 1)
                if live(i, BATCHES):
                    dve.wait_ge(g0["gate"], i + 1)
                    V.tensor_tensor(conv[:, :, :], ps[:, 0:2, 0:INNER],
                                    conv_b[:, :].unsqueeze(1).to_broadcast([P, TILES, INNER]), ALU.add).then_inc(g0["conv"], 1)
                if live(i + 1, BATCHES):
                    low_part(i + 1)
                if live(i, BATCHES):
                    dve.wait_ge(g0["conv"], i + 1)
                    wait(dve, g0["tr"], i)
                    V.tensor_tensor(h[:, :, :], conv[:, :, :], gate[:, :, :], ALU.mult).then_inc(g0["h"], 1)
                    dve.wait_ge(g0["h"], i + 1)
                    moments(h_flat, stats_h, mv_h, TILES, INNER, g0["mv"], i + 1)
                if isinstance(i, int) and i == 0:
                    small_weights()
                if live(i - 3, BATCHES):
                    weigh(i - 3)
                    place(i - 3)
            steps(dve, BATCHES, 3, conv_step, ahead=1)

            dve.wait_ge(tb["count"], 1)
            V.tensor_tensor(ends[:, :], ps[:, 7, 64:64 + EXPERTS], base, ALU.add).then_inc(tb["ends"], 1)
            V.tensor_scalar(n_tiles_f[:, :], ps[:, 7, 64:64 + EXPERTS], float(P - 1), None, ALU.add).then_inc(tb["step"], 1)
            dve.wait_ge(tb["step"], 1)
            V.tensor_copy(n_tiles_i[:, :], n_tiles_f[:, :]).then_inc(tb["step"], 1)
            dve.wait_ge(tb["step"], 2)
            V.tensor_scalar(n_tiles_s[:, :], n_tiles_i[:, :], P.bit_length() - 1, None, ALU.logical_shift_right).then_inc(tb["step"], 1)
            dve.wait_ge(tb["step"], 3)
            V.tensor_copy(n_tiles[:, :], n_tiles_s[:, :]).then_inc(tb["step"], 1)
            dve.wait_ge(tb["step"], 4)
            V.tensor_tensor(upto_p[:, :, :], const[:, C_UPTO:C_UPTO + EXPERTS * EXPERTS].rearrange("p (a b) -> p a b", b=EXPERTS),
                            n_tiles[:, :].unsqueeze(1).to_broadcast([P, EXPERTS, EXPERTS]), ALU.mult).then_inc(tb["step"], 1)
            V.tensor_scalar(skip_rows[:, :], n_tiles[:, :], -float(P), float(REGION), ALU.mult, ALU.add).then_inc(tb["step"], 1)
            dve.wait_ge(tb["step"], 5)
            V.reduce_sum(upto[:, :], upto_p[:, :, :], axis=AX.X).then_inc(tb["step"], 1)
            dve.wait_ge(tb["step"], 7)
            V.tensor_tensor(past[:, :, :], upto[:, :].unsqueeze(1).to_broadcast([P, SLOT_TILES, EXPERTS]),
                            const[:, C_TILE:C_TILE + SLOT_TILES].unsqueeze(2).to_broadcast([P, SLOT_TILES, EXPERTS]),
                            ALU.is_le).then_inc(tb["step"], 1)
            dve.wait_ge(tb["step"], 8)
            dve.wait_ge(tb["step"], 6)
            V.tensor_tensor(past_rows[:, :, :], past[:, :, :],
                            skip_rows[:, :].unsqueeze(1).to_broadcast([P, SLOT_TILES, EXPERTS]), ALU.mult).then_inc(tb["step"], 1)
            V.reduce_sum(expert_f[:, :], past[:, :, :], axis=AX.X).then_inc(tb["step"], 1)
            dve.wait_ge(tb["step"], 9)
            V.reduce_sum(start_f[:, :], past_rows[:, :, :], axis=AX.X).then_inc(tb["step"], 1)
            dve.wait_ge(tb["step"], 11)
            V.tensor_tensor(start_f2[:, :], start_f[:, :], const[:, C_ROW:C_ROW + SLOT_TILES], ALU.add).then_inc(tb["step"], 1)
            dve.wait_ge(tb["step"], 10)
            V.tensor_scalar(expert_t[:, :], expert_f[:, :], float(EXPERTS - 1), None, ALU.min)
            dve.wait_ge(tb["step"], 12)
            V.tensor_copy(start_t[:, :], start_f2[:, :]).then_inc(tb["ready"], 1)
            V.scalar_tensor_tensor(shift_r[:, :], upto[:, :], float(P), skip_rows[:, :], ALU.mult, ALU.add).then_inc(tb["place"], 1)
            dve.wait_ge(tb["place"], 1)
            V.scalar_tensor_tensor(shift[:, :], shift_r[:, :], float(REGION), base, ALU.subtract, ALU.subtract).then_inc(tb["place"], 1)
            dve.wait_ge(tb["place"], 2)
            chosen_rows = chosen[:, :, :, :].rearrange("p b r e -> p (b r) e")
            V.tensor_tensor(chosen_rows, chosen_rows, shift[:, :].unsqueeze(1).to_broadcast([P, BATCHES * TILES * TOP_K, EXPERTS]),
                            ALU.mult).then_inc(tb["place"], 1)
            dve.wait_ge(tb["place"], 3)
            V.reduce_sum(shift_of[:, :], chosen_rows, axis=AX.X).then_inc(tb["place"], 1)
            dve.wait_ge(tb["place"], 4)
            V.tensor_tensor(row_all[:, :, :].rearrange("p b r -> p (b r)"), rows_f[:, :, :].rearrange("p b r -> p (b r)"),
                            shift_of[:, :], ALU.add).then_inc(tb["placed"], 1)

            dve.wait_ge(wt["hid_zero"], 1)
            def expert_step(i):
                for j in range(FLY):
                    t = FLY * i + j
                    if live(i, SLOT_TILES // FLY):
                        dve.wait_ge(mo["hi"], t + 1)
                        wait(dve, mo["up"], t - FLY + 1)
                        V.tensor_tensor(rT_lo[:, j, :], ps[:, 0, 0:P], rT_hi[:, j, :].bitcast(fp32),
                                        ALU.subtract).then_inc(mo["lo"], 1)
                    u, ju = t - 1, (j - 1) % FLY
                    if live(u, SLOT_TILES):
                        dve.wait_ge(mo["act1"], u + 1)
                        wait(dve, mo["hid_tr"], u - FLY + 1)
                        V.tensor_tensor(hid[:, ju, 0:HIDDEN], act1[:, ju, :], ps[:, 3 + ju, 0:HIDDEN],
                                        ALU.mult).then_inc(mo["hid"], 1)
                    u, ju = t - 3, j
                    if live(u, SLOT_TILES):
                        dve.wait_ge(mo["hid_tr"], u + 1)
                        wait(dve, mo["down"], u - FLY + 1)
                        V.tensor_copy(hidT[:, ju, :], ps[:, 1, 0:HIDDEN_TILES * P]).then_inc(mo["hidT"], 1)
            steps(dve, SLOT_TILES // FLY, 2, expert_step)

            dve.wait_ge(wt["ff_lo"], 2 * FF_TILES)
            dve.wait_ge(wt["fi_lo"], 1)
            for n, lo in enumerate((fh_lo[:, :, :], fi_lo)):
                last = V.reduce_max(odd[:, n:n + 1], lo.rearrange("p k o -> p (k o)").bitcast(u32), axis=AX.X)
            last.then_inc(wt["odd_any"], 1)
            dve.wait_ge(wt["odd_any"], 1)
            V.tensor_scalar(odd_any[:, :], odd[:, :], 0.0, None, ALU.not_equal).then_inc(wt["odd_any"], 1)
            dve.wait_ge(wt["odd_mm"], 1)
            V.tensor_reduce(odd_i[:, :], ps[0:FEATS, 7, 0:2], axis=AX.X, op=ALU.max).then_inc(wt["odd_i"], 1)

            def attention_step(i):
                b = i - 5
                if live(b, BATCHES):
                    dve.wait_ge(at["kv_mm"], b + 1)
                    wait(dve, at["kv_tr"], b)
                    V.tensor_tensor(kv[:, :, :], ps[:, 6, 0:2 * P].rearrange("p (a f) -> p a f", f=P),
                                    const[:, C_KVMASK:C_KVMASK + P].unsqueeze(1).to_broadcast([P, 2, P]), ALU.mult).then_inc(at["kv"], 1)
                b = i - 1
                if live(b, BATCHES):
                    dve.wait_ge(at["got"], 64 * (b + 1))
                    wait(dve, at["res"], b)
                    V.tensor_tensor(sum1[:, :, :], got[:, :, 0, :], got[:, :, 1, :], ALU.add).then_inc(at["sum1"], 1)
                b = i - 6
                if live(b, BATCHES):
                    dve.wait_ge(at["out"], b + 1)
                    dve.wait_ge(at["kept"], b + 1)
                    wait(dve, at["x3"], b)
                    V.tensor_tensor(f_res, ps[:, 7, 0:SEQ], x_kept[:, b, :], ALU.add).then_inc(at["res3"], 1)
                b = i - 1
                if live(b, BATCHES):
                    dve.wait_ge(at["sum1"], b + 1)
                    wait(dve, at["x2"], b)
                    V.tensor_tensor(res[:, :], sum1[:, :, :].rearrange("p t d -> p (t d)"), x_kept[:, b, :], ALU.add).then_inc(at["res"], 1)
                    dve.wait_ge(at["res"], b + 1)
                    moments(res, stats, mv, TILES, D, at["mv"], b + 1)
                b = i - 6
                if live(b, BATCHES):
                    dve.wait_ge(at["res3"], b + 1)
                    moments(f_res, stats_h, mv_h, TILES, D, at["mv3"], b + 1)
                b = i - 2
                if live(b, BATCHES):
                    dve.wait_ge(at["x2T"], b + 1)
                    wait(dve, at["qk"], b)
                    V.tensor_tensor(x2T_lo[:, :], x2T[:, :], x2T_hi[:, :].bitcast(fp32), ALU.subtract).then_inc(at["lo"], 1)
                b = i - 1
                if live(b, BATCHES):
                    dve.wait_ge(at["rstd"], 2 * b + 2)
                    wait(dve, at["kept"], b)
                    wait(dve, at["tr"], b)
                    normalise(x2, res, mv, rstd, TILES, D, at["x2"])
                b = i - 3
                if live(b, BATCHES):
                    dve.wait_ge(at["st"], b + 1)
                    wait(dve, at["qf"], b)
                    V.tensor_copy(st_hi[:, :, :], st[:, :, :]).then_inc(at["st_hi"], 1)
                b = i - 5
                if live(b, BATCHES):
                    dve.wait_ge(at["den"], b + 1)
                    wait(dve, at["att"], b)
                    V.reciprocal(rden[:, :], den[:, :]).then_inc(at["rden"], 1)
                    dve.wait_ge(at["rden"], b + 1)
                    wait(dve, at["out"], b)
                    V.tensor_tensor(att[:, :], ps[:, 7, 0:SEQ], rden[:, :], ALU.mult).then_inc(at["att"], 1)
                b = i - 6
                if live(b, BATCHES):
                    dve.wait_ge(at["rstd3"], 2 * b + 2)
                    wait(dve, at["kept3"], b)
                    wait(dve, at["tr3"], b)
                    normalise(x3, f_res, mv_h, rstd_h, TILES, D, at["x3"])
                b = i - 3
                if live(b, BATCHES):
                    dve.wait_ge(at["v_tok"], b + 1)
                    wait(dve, at["kv_mm"], b)
                    V.tensor_copy(v_use[:, :, :], v_tok[:, :, :]).then_inc(at["v_use"], 1)
                b = i - 2
                if live(b, BATCHES):
                    dve.wait_ge(at["v_mm"], b + 1)
                    wait(dve, at["v_use"], b)
                    V.tensor_tensor(v_tok[:, :, :], ps[:, 3, 0:SEQ].rearrange("p (t d) -> p t d", d=D),
                                    bv[:, :].unsqueeze(1).to_broadcast([P, TILES, D]), ALU.add).then_inc(at["v_tok"], 1)
                b = i - 6
                if live(b, BATCHES):
                    dve.wait_ge(at["x3_hi"], b + 1)
                    V.tensor_tensor(x3T_lo[:, b, :], ps[:, 0, SEQ:], x3T_hi[:, b, :].bitcast(fp32), ALU.subtract).then_inc(at["x3_lo"], 1)
            steps(dve, BATCHES, 6, attention_step)


            def mlp_step(i):
                for m in range(FF_TILES):
                    if live(i, BATCHES):
                        n = FF_TILES * i + m
                        dve.wait_ge(ff["silu"], n + 1)
                        wait(dve, ff["a_lo"], n - FF_TILES + 1)
                        V.scalar_tensor_tensor(f_a[:, m, :], ps[:, in_bank[m], SEQ:], ff_s[:, 1, m:m + 1],
                                               f_silu[:, m % 2, :], ALU.mult, ALU.mult).then_inc(ff["act"], 1)
                b = i - 3
                if live(b, BATCHES):
                    dve.wait_ge(ff["out_mm"], b + 1)
                    wait(dve, ff["out"], b)
                    V.tensor_tensor(f_res, ps[:, 6, 0:TILES * D], x_kept[:, b, :], ALU.add).then_inc(ff["res"], 1)
                    dve.wait_ge(ff["res"], b + 1)
                    moments(f_res, stats, mv, TILES, D, ff["mv"], b + 1)
                    dve.wait_ge(ff["rstd"], 2 * b + 2)
                    wait(dve, ff["stored"], 16 * b)
                    normalise(f_out, f_res, mv, rstd, TILES, D, ff["out"])
                b = i - 1
                for m in range(FF_TILES):
                    if live(b, BATCHES):
                        n = FF_TILES * b + m
                        dve.wait_ge(ff["g1"], n + 1)
                        wait(dve, ff["h2_mm"], FF_TILES * b)
                        split(g_hi[:, m, :], g_lo[:, m, :], f_g[:, m, :], ff["g_hi"], ff["g_lo"], n + 1)
                for m in range(FF_TILES):
                    if live(i, BATCHES):
                        n = FF_TILES * i + m
                        dve.wait_ge(ff["act"], n + 1)
                        wait(dve, ff["h1_mm"], FF_TILES * i)
                        V.tensor_copy(a_hi[:, m, :], f_a[:, m, :]).then_inc(ff["a_hi"], 1)
            steps(dve, BATCHES, 3, mlp_step)

        @block.tensor
        def _(pe):
            mm, transpose = nc.tensor.matmul, nc.tensor.transpose

            def mm3(dst, lhs, rhs, start, stop):
                mm(dst, lhs[0], rhs[0], start=start, stop=False)
                mm(dst, lhs[0], rhs[1], start=False, stop=False)
                return mm(dst, lhs[1], rhs[0], start=False, stop=stop)

            pe.wait_ge(ld["front"], 16 * 3)
            for t in range(2):
                mm(ps[:, t, :], w_h[:, t, :], conv_bd[:, t, :], start=True, stop=True).then_inc(wt["conv_mm"], 1)
            pe.wait_ge(wt["front_hi"], 3)
            pe.wait_ge(wt["front_lo"], 3)

            def small_weights():
                pe.wait_ge(ld["conv"], 16 * 8)
                for t in range(2):
                    last = mm(ps[:, 4, 0:D], cproj[:, t, :], out_wT[:, t, :], start=t == 0, stop=t == 1)
                last.then_inc(wt["small_mm"], 1)
                for t in range(2):
                    last = mm(ps[:, 6, 0:1], fc_wT[:, t, :], ln_gb[:, 2 + t:3 + t], start=t == 0, stop=t == 1)
                last.then_inc(wt["small_mm"], 1)
                pe.wait_ge(wt["cproj_bb"], 2)
                for t in range(2):
                    last = mm(ps[:, 5, 0:D], cproj_bb[:, t, :], out_wT[:, t, :], start=t == 0, stop=t == 1)
                last.then_inc(wt["small_mm"], 1)
                pe.wait_ge(ld["const"], 16)
                pe.wait_ge(wt["before"], 2)
                pe.wait_ge(wt["memset"], MEMSETS)
                pe.wait_ge(wt["small"], 3)
                pe.wait_ge(wt["fc_g"], 2)

            def conv_step(i):
                if live(i, BATCHES):
                    pe.wait_ge(g0["x_lo"], i + 1)
                    wait(pe, g0["gate"], i)
                    wait(pe, g0["conv"], i)
                    for t in range(TILES):
                        def x_at(tap):
                            cols = slice(t * P + tap, t * P + tap + P)
                            return xT_hi[:, cols], xT_lo[:, cols]
                        both = [w[:, PAD:, :].rearrange("p k o -> p (k o)") for w in (front_hi, front_lo)]
                        mm3(ps[:, t, :], x_at(PAD), both, True, False)
                        for tap in range(PAD):
                            last = mm3(ps[:, t, 0:INNER], x_at(tap), (front_hi[:, tap, :], front_lo[:, tap, :]),
                                       False, tap == PAD - 1)
                    last.then_inc(g0["front"], 1)
                if isinstance(i, int) and i == 0:
                    small_weights()
                b = i - 3
                if live(b, BATCHES):
                    pe.wait_ge(g0["added"], b + 1)
                    wait(pe, g0["rank"], b)
                    dst = ps[:, 7, 32:32 + TILES * EXPERTS]
                    mm(dst, before[:, :], either[:, :, :].rearrange("p t e -> p (t e)"), start=True, stop=False)
                    mm(dst, ones_bf[:, :], earlier[:, :, :].rearrange("p t e -> p (t e)"), start=False, stop=True)\
                        .then_inc(g0["rank_mm"], 1)
                b = i - 1
                if live(b, BATCHES):
                    pe.wait_ge(g0["hn"], b + 1)
                    wait(pe, g0["hT"], b)
                    wait(pe, g0["hnT"], b)
                    for t in range(TILES):
                        for k in range(2):
                            cols = slice((2 * t + k) * P, (2 * t + k + 1) * P)
                            transpose(ps[:, 2, cols], h[:, t, k * P:(k + 1) * P], ident)
                            last = transpose(ps[:, 3, cols], hn[:, t, k * P:(k + 1) * P], ident)
                    last.then_inc(g0["tr"], 1)
                b = i - 2
                if live(b, BATCHES):
                    pe.wait_ge(g0["x1"], b + 1)
                    wait(pe, g0["x1T"], b)
                    wait(pe, g0["top_at"], b)
                    for t in range(TILES):
                        last = transpose(ps[:, 6, t * P:(t + 1) * P], x1[:, t * D:(t + 1) * D], ident)
                    last.then_inc(g0["x1_tr"], 1)
                b = i - 1
                if live(b, BATCHES):
                    pe.wait_ge(g0["hnT"], b + 1)
                    wait(pe, g0["mid"], b)
                    for k in range(2):
                        last = mm(ps[:, 4, 0:SEQ], fc_g[:, k, :], hnT[:, k, :], start=k == 0, stop=k == 1)
                    last.then_inc(g0["fc"], 1)
                b = i - 2
                if live(b, BATCHES):
                    pe.wait_ge(g0["x1T"], b + 1)
                    for t in range(TILES):
                        last = mm(ps[:, 6, SEQ + t * EXPERTS:SEQ + (t + 1) * EXPERTS], x1T[:, t * P:(t + 1) * P], gate_wT[:, :],
                                  start=True, stop=True)
                    last.then_inc(g0["logits"], 1)
                b = i - 1
                if live(b, BATCHES):
                    pe.wait_ge(g0["mid"], b + 1)
                    pe.wait_ge(g0["hT"], b + 1)
                    wait(pe, g0["res"], b)
                    for t in range(TILES):
                        dst = ps[:, 5, t * D:(t + 1) * D]
                        mm(dst, mid[:, t * P:(t + 1) * P], mid_out[:, :], start=True, stop=False)
                        for k in range(2):
                            last = mm(dst, hT[:, t, k * P:(k + 1) * P], out_wT[:, k, :], start=False, stop=k == 1)
                    last.then_inc(g0["out"], 1)
            steps(pe, BATCHES, 3, conv_step)

            pe.wait_ge(g0["carry"], BATCHES)
            mm(ps[:, 7, 64:64 + EXPERTS], ones_bf[:, :], earlier[:, 0, :], start=True, stop=True).then_inc(tb["count"], 1)

            pe.wait_ge(tb["ready"], 1)
            pe.wait_ge(wt["moe_lo"], EXPERTS)
            pe.wait_ge(ld["w2"], 16)

            def expert_step(i):
                for j in range(FLY):
                    t = FLY * i + j
                    if live(t - 1, SLOT_TILES):
                        e_up = loaded(mybir.EngineType.PE, expert_t, t - 1, 1, EXPERTS - 1)[0]
                    if live(i, SLOT_TILES // FLY):
                        pe.wait_ge(mo_in[j], 16 * (i + 1))
                        wait(pe, mo["lo"], t)
                        transpose(ps[:, 0, 0:P], rows_in[:, j, :], ident).then_inc(mo["tr"], 1)
                    u, ju = t - 1, (j - 1) % FLY
                    if live(u, SLOT_TILES):
                        pe.wait_ge(mo["lo"], u + 1)
                        wait(pe, mo["act1"], u)
                        wait(pe, mo["hid"], u - FLY + 1)
                        for w in range(2):
                            cols = slice(w * HIDDEN, (w + 1) * HIDDEN)
                            last = mm3(ps[:, 3 + ju if w else 2, 0:HIDDEN], (rT_hi[:, ju, :], rT_lo[:, ju, :]),
                                       (w13_hi[:, e_up, cols], w13_lo[:, e_up, cols]), True, True)
                        last.then_inc(mo["up"], 1)
                    if live(t - 4, SLOT_TILES):
                        e_down = loaded(mybir.EngineType.PE, expert_t, t - 4, 1, EXPERTS - 1)[0]
                    u, ju = t - 3, j
                    if live(u, SLOT_TILES):
                        pe.wait_ge(mo["hid"], u + 1)
                        wait(pe, mo["hidT"], u)
                        for k in range(HIDDEN_TILES):
                            last = transpose(ps[:, 1, k * P:(k + 1) * P], hid[:, ju, k * P:(k + 1) * P], ident)
                        last.then_inc(mo["hid_tr"], 1)
                    u, ju = t - 4, (j - 4) % FLY
                    if live(u, SLOT_TILES):
                        pe.wait_ge(mo["hidT"], u + 1)
                        wait(pe, mo["out"], u)
                        for k in range(HIDDEN_TILES):
                            last = mm(ps[:, 6, 0:D], hidT[:, ju, k * P:(k + 1) * P], w2[:, e_down, k, :],
                                      start=k == 0, stop=k == HIDDEN_TILES - 1)
                        last.then_inc(mo["down"], 1)
            steps(pe, SLOT_TILES // FLY, 2, expert_step)

            pe.wait_ge(wt["att_lo"], 2)
            pe.wait_ge(mo["out"], SLOT_TILES)
            pe.wait_ge(wt["odd_any"], 2)
            mm(ps[0:FEATS, 7, 0:2], ones[:, :], odd_any[:, :], start=True, stop=True).then_inc(wt["odd_mm"], 1)
            pe.wait_ge(wt["odd_i"], 1)
            n_odd = pe.value_load(odd_i[0:1, 0:1], min_val=0, max_val=P)

            def attention_step(i):
                b = i - 5
                if live(b, BATCHES):
                    pe.wait_ge(at["kv"], b + 1)
                    wait(pe, at["kvT"], b)
                    for a in range(2):
                        last = transpose(ps[:, 6, (2 + a) * P:(3 + a) * P], kv[:, a, :], ident)
                    last.then_inc(at["kv_tr"], 1)
                b = i - 4
                if live(b, BATCHES):
                    pe.wait_ge(at["st_lo"], b + 1)
                    wait(pe, at["qp"], b)
                    for t in range(TILES):
                        cols = slice(t * P, (t + 1) * P)
                        for n in range(2):
                            last = mm3(ps[:, 4 + t, n * 256:(n + 1) * 256], (st_hi[:, 2 + n, cols], st_lo[:, 2 + n, cols]),
                                       (om_hi[:, :], om_lo[:, :]), True, True)
                    last.then_inc(at["kf"], 1)
                b = i - 2
                if live(b, BATCHES):
                    pe.wait_ge(at["x2T"], b + 1)
                    wait(pe, at["v_tok"], b)
                    for t in range(TILES):
                        last = mm(ps[:, 3, t * D:(t + 1) * D], x2T[:, t * P:(t + 1) * P], wv[:, :], start=True, stop=True)
                    last.then_inc(at["v_mm"], 1)
                b = i - 5
                if live(b, BATCHES):
                    pe.wait_ge(at["kvT"], b + 1)
                    pe.wait_ge(at["qp"], b + 1)
                    wait(pe, at["res3"], b)
                    for a in range(2):
                        for g in range(HEAD_GROUPS):
                            last = mm(ps[32 * g:32 * g + 32, 7, a * SEQ:(a + 1) * SEQ], kvT[:, a, 32 * g:32 * g + 32],
                                      qp[:, g, :], start=True, stop=True)
                    last.then_inc(at["nd"], 1)
                b = i - 4
                if live(b, BATCHES):
                    pe.wait_ge(at["kp"], b + 1)
                    for g in range(HEAD_GROUPS):
                        cols = slice((g % 2) * P, (g % 2 + 1) * P)
                        last = mm3(ps[:, 4 + g // 2, (g % 2) * SEQ:(g % 2 + 1) * SEQ], (om_hi[:, cols], om_lo[:, cols]),
                                   (st_hi[:, g // 2, :], st_lo[:, g // 2, :]), True, True)
                    last.then_inc(at["qf"], 1)
                b = i - 4
                if live(b, BATCHES):
                    pe.wait_ge(at["kp"], b + 1)
                    pe.wait_ge(at["v_use"], b + 1)
                    wait(pe, at["kv"], b)
                    wait(pe, at["kvT"], b)
                    for a in range(2):
                        for t in range(TILES):
                            for g in range(HEAD_GROUPS):
                                lhs = ones[:, 0:32] if a else v_use[:, t, 32 * g:32 * g + 32]
                                last = mm(ps[32 * g:32 * g + 32, 6, a * P:(a + 1) * P], lhs, kp[:, t, g * P:(g + 1) * P],
                                          start=t == 0, stop=t == TILES - 1)
                    last.then_inc(at["kv_mm"], 1)
                b = i - 1
                if live(b, BATCHES):
                    pe.wait_ge(at["x2"], b + 1)
                    wait(pe, at["x2T"], b)
                    wait(pe, at["x3_lo"], b - 5)
                    for t in range(TILES):
                        last = transpose(ps[:, 0, t * P:(t + 1) * P], x2[:, t * D:(t + 1) * D], ident)
                    last.then_inc(at["tr"], 1)
                b = i - 2
                if live(b, BATCHES):
                    pe.wait_ge(at["lo"], b + 1)
                    wait(pe, at["st"], b)
                    for n in range(4):
                        last = mm3(ps[:, 1 + n // 2, (n % 2) * SEQ:(n % 2 + 1) * SEQ], (qk_hi[:, n, :], qk_lo[:, n, :]),
                                   (x2T_hi[:, :], x2T_lo[:, :]), True, True)
                    last.then_inc(at["qk"], 1)
                b = i - 5
                if live(b, BATCHES):
                    pe.wait_ge(at["att"], b + 1)
                    for t in range(TILES):
                        dst = ps[:, 7, t * D:(t + 1) * D]
                        mm(dst, first_row, bout[:, :], start=True, stop=False)
                        last = mm(dst, att[:, t * P:(t + 1) * P], wout[:, :], start=False, stop=True)
                    last.then_inc(at["out"], 1)
                b = i - 6
                if live(b, BATCHES):
                    pe.wait_ge(at["x3"], b + 1)
                    if live(i - 1, BATCHES):
                        pe.wait_ge(at["x2T"], i)
                    for t in range(TILES):
                        last = transpose(ps[:, 0, SEQ + t * P:SEQ + (t + 1) * P], x3[:, t * D:(t + 1) * D], ident)
                    last.then_inc(at["tr3"], 1)
            steps(pe, BATCHES, 6, attention_step)

            pe.wait_ge(wt["ff_lo"], 2 * FF_TILES)
            pe.wait_ge(wt["fi_lo"], 1)
            pe.wait_ge(wt["ff_out"], 1)
            pe.wait_ge(at["x3_lo"], BATCHES)

            def mlp_product(dst, w_hi, w_lo, x_hi, x_lo, start, stop, exact):
                mm(dst, w_hi, x_hi, start=start, stop=False)
                last = mm(dst, w_hi, x_lo, start=False, stop=stop and exact)
                return last if exact else mm(dst, w_lo, x_hi, start=False, stop=stop)

            def mlp_step(i, exact):
                def first_layer(m):
                    n = FF_TILES * i + m
                    wait(pe, ff["act"], (n, n - 3, n - 3, n - 2)[m])
                    for w in range(2):
                        rows = slice(m * P, (m + 1) * P)
                        last = mlp_product(ps[:, in_bank[m], w * SEQ:(w + 1) * SEQ], fi_hi[:, w, rows], fi_lo[:, w, rows],
                                           x3T_hi[:, i, :], x3T_lo[:, i, :], True, True, exact)
                    last.then_inc(ff["in_mm"], 1)

                def square_layer(layer, b, bank, x_hi, x_lo, ready, read, done):
                    pe.wait_ge(ready, FF_TILES * (b + 1))
                    for m in range(FF_TILES):
                        rows = slice(m * P, (m + 1) * P)
                        wait(pe, read, FF_TILES * b + (m - 1 if m >= 2 else 0))
                        for k in range(FF_TILES):
                            row = layer * FF_TILES + k
                            last = mlp_product(half_bank(bank, m), fh_hi[:, row, rows], fh_lo[:, row, rows],
                                               x_hi[:, k, :], x_lo[:, k, :], k == 0, k == FF_TILES - 1, exact)
                        last.then_inc(done, 1)

                if live(i, BATCHES):
                    for m in range(FF_TILES - 1):
                        first_layer(m)
                b = i - 3
                if live(b, BATCHES):
                    pe.wait_ge(ff["g2"], FF_TILES * (b + 1))
                    wait(pe, ff["res"], b)
                    for t in range(TILES):
                        for k in range(FF_TILES):
                            last = mm(ps[:, 6, t * D:(t + 1) * D], f_last[:, k, t * P:(t + 1) * P], ff_out_w[:, k, :],
                                      start=k == 0, stop=k == FF_TILES - 1)
                    last.then_inc(ff["out_mm"], 1)
                if live(i, BATCHES):
                    first_layer(FF_TILES - 1)
                if live(i - 2, BATCHES):
                    square_layer(1, i - 2, 4, g_hi, g_lo, ff["g_lo"], ff["g2"], ff["h2_mm"])
                if live(i - 1, BATCHES):
                    square_layer(0, i - 1, 2, a_hi, a_lo, ff["a_lo"], ff["g1"], ff["h1_mm"])

            with pe.If(n_odd == 0):
                steps(pe, BATCHES, 3, lambda i: mlp_step(i, True))
            with pe.Else():
                steps(pe, BATCHES, 3, lambda i: mlp_step(i, False))


def layouts(a):
    f = np.float32
    tiled = lambda w: np.ascontiguousarray(w.reshape(-1, P, w.shape[-1]).transpose(1, 0, 2))
    cols = lambda v: np.ascontiguousarray(v.reshape(-1, P).T)
    rows = lambda v: np.ascontiguousarray(np.broadcast_to(v[None, :], (P, v.shape[0])))
    A = {}
    x = a["L0_attn_hidden_states"]
    A["x_tok"] = np.ascontiguousarray(x.reshape(BATCHES, TILES, P, D).transpose(2, 0, 1, 3).reshape(P, BATCHES, TILES * D))
    xT = np.zeros((D, BATCHES, PAD + SEQ), f)
    xT[:, :, PAD:] = x.transpose(2, 0, 1)
    A["xT"] = xT
    w = a["L0_attn_in_proj_w"]
    A["w_h"] = tiled(w[:INNER])
    A["w_gate"] = np.ascontiguousarray(w[INNER:].T)
    width = INNER // GROUPS
    bd = np.zeros((2, P, TAPS, P), f)
    for o in range(INNER):
        t, g = o // P, o % P // width
        bd[t, g * width:(g + 1) * width, :, o % P] = a["L0_attn_conv_w"][o]
    A["conv_bd"] = np.ascontiguousarray(bd.reshape(2, P, TAPS * P).transpose(1, 0, 2))
    A["conv_b"] = rows(a["L0_attn_conv_b"])
    A["fc_wT"] = tiled(np.ascontiguousarray(a["L0_attn_fc_w"].T))
    A["ln_gb"] = np.ascontiguousarray(np.concatenate([cols(a["L0_attn_ln_g"]), cols(a["L0_attn_ln_b"])], 1))
    A["fc_b"] = cols(a["L0_attn_fc_b"])
    A["cproj"] = tiled(a["L0_attn_cproj_w"])
    A["cproj_b"] = cols(a["L0_attn_cproj_b"])
    A["out_wT"] = tiled(np.ascontiguousarray(a["L0_attn_out_w"].T))
    A["gate_wT"] = np.ascontiguousarray(a["L0_ffn_gate_w"].T)
    A["w13"] = np.ascontiguousarray(np.concatenate([a["L0_ffn_w1"], a["L0_ffn_w3"]], 2).transpose(1, 0, 2))
    w2 = np.zeros((EXPERTS, HIDDEN_TILES * P, D), f)
    w2[:, :HIDDEN] = a["L0_ffn_w2"]
    A["w2"] = np.ascontiguousarray(w2.reshape(EXPERTS, HIDDEN_TILES, P, D).transpose(2, 0, 1, 3))
    wq, bq = a["L1_attn_Wqkv"], a["L1_attn_bqkv"]
    half = D // 2
    starts = [0, half, D, D + half]
    A["qk_w"] = np.ascontiguousarray(np.stack([np.tile(wq[:, s:s + half], (1, 2)) for s in starts], 1))
    A["qk_b"] = np.ascontiguousarray(np.stack([np.tile(bq[s:s + half], 2) for s in starts], 1))
    A["wv"] = np.ascontiguousarray(wq[:, 2 * D:])
    A["bv"] = rows(bq[2 * D:])
    om = np.zeros((P, 2 * P), f)
    for n in range(HEADS // 2):
        om[n * HEAD_DIM:(n + 1) * HEAD_DIM, n * FEATS:(n + 1) * FEATS] = a["L1_attn_omega"]
        om[half + n * HEAD_DIM:half + (n + 1) * HEAD_DIM, n * FEATS:(n + 1) * FEATS] = -0.5
    A["omega"] = om
    A["wout"] = np.ascontiguousarray(a["L1_attn_Wout"])
    A["bout"] = rows(a["L1_attn_bout"])
    A["ff_in"] = np.ascontiguousarray(np.stack([a["L1_ffn_w1_w"].T, a["L1_ffn_w2_w"].T], 1))
    A["ff_h"] = np.ascontiguousarray(np.concatenate([tiled(np.ascontiguousarray(a[n].T)) for n in ("L1_ffn_h1_w", "L1_ffn_h2_w")], 1))
    A["ff_s"] = np.ascontiguousarray(np.stack([cols(a[f"L1_ffn_{n}_s"]) for n in ("w1", "w2", "h1", "h2")], 1))
    A["ff_out"] = tiled(np.ascontiguousarray(a["L1_ffn_w3_w"].T))
    A["ff_out_s"] = rows(a["L1_ffn_w3_s"])
    c = np.zeros((P, C_ALL), f)
    c[:, C_IDENT:C_IDENT + P] = np.eye(P)
    c[:, C_BEFORE:C_BEFORE + P] = np.triu(np.ones((P, P)), 1)
    own = np.arange(P) % 32 // HEAD_DIM
    c[:, C_KVMASK:C_KVMASK + P] = own[:, None] == np.arange(P)[None, :] // FEATS
    c[:, C_IOTA:C_IOTA + EXPERTS] = np.arange(EXPERTS)
    c[:, C_BASE:C_BASE + EXPERTS] = np.arange(EXPERTS) * REGION
    c[:, C_UPTO:C_TILE] = np.tril(np.ones((EXPERTS, EXPERTS))).reshape(-1)
    c[:, C_TILE:C_ROW] = np.arange(SLOT_TILES)
    c[:, C_ROW:C_FIRST] = np.arange(SLOT_TILES) * P
    c[0, C_FIRST:] = 1
    A["const"] = c
    return A


def kernel(**inputs):
    import concourse.bacc as bacc
    from concourse.bass_utils import run_bass_kernel_spmd

    nc = bacc.Bacc("TRN2", target_bir_lowering=False, num_devices=1)
    laid = layouts({n: np.asarray(v) for n, v in inputs.items()})
    arrays, A = {}, {}
    for name, a in laid.items():
        arrays[f"in_{name}"] = a
        A[name] = nc.dram_tensor(f"in_{name}", a.shape, mybir.dt.from_np(a.dtype), kind="ExternalInput").ap()
    out = nc.dram_tensor("out", [TOKENS, D], mybir.dt.float32, kind="ExternalOutput").ap()
    build(nc, A, out)
    r = run_bass_kernel_spmd(nc, [arrays], core_ids=[0])
    return r.results[0]["out"].reshape(BATCHES, SEQ, D)
```

```python
import numpy as np
import concourse.bass as bass
from concourse import mybir
from contextlib import ExitStack

P = 128
BATCHES, SEQ, D = 8, 256, 128
TOKENS = BATCHES * SEQ
TILES = SEQ // P
INNER, TAPS, GROUPS = 256, 4, 8
PAD = TAPS - 1
EXPERTS, TOP_K, HIDDEN = 8, 2, 352
HIDDEN_TILES = -(-HIDDEN // P)
SLOT_TILES = TOKENS * TOP_K // P + EXPERTS - 1
DUMMY_TILES = EXPERTS - 1
REGION = TOKENS + P
ROWS = EXPERTS * REGION + DUMMY_TILES * P
HEADS, FEATS = 16, 32
HEAD_DIM = D // HEADS
GROUP_HEADS = P // FEATS
HEAD_GROUPS = HEADS // GROUP_HEADS
FF = 512
FF_TILES = FF // P
ATTENTION_LAG, MLP_LAG = 6, 3
EARLY = 2
FLY = 3
EPS = 1e-5

C_IDENT, C_BEFORE, C_KVMASK = 0, P, 2 * P
C_IOTA = 3 * P
C_BASE = C_IOTA + EXPERTS
C_UPTO = C_BASE + EXPERTS
C_TILE = C_UPTO + EXPERTS * EXPERTS
C_ROW = C_TILE + SLOT_TILES
MEMSETS = 5
C_FIRST = C_ROW + SLOT_TILES
C_ALL = C_FIRST + P


def steps(engine, count, lag, step, ahead=0, first=0, left=0):
    for i in range(first, lag + 1):
        step(i)
    with engine.Fori(lag + 1, count - ahead) as i:
        step(i)
    for i in range(count - ahead, count + lag - left):
        step(i)


def attention_then_mlp(engine, attention_step, mlp_first, mlp_rest):
    steps(engine, BATCHES, ATTENTION_LAG, attention_step, left=3)
    last = BATCHES + ATTENTION_LAG - 1

    def first_step():
        mlp_first(0)
        mlp_rest(0)
    attention_step(last - 2, first_step)
    attention_step(last - 1, lambda: mlp_first(1))
    attention_step(last, lambda: mlp_rest(1))


def alone(engine, carrier):
    engine.sem_inc(carrier, 1)


def live(n, count):
    return not isinstance(n, int) or 0 <= n < count


def wait(engine, semaphore, value):
    if not isinstance(value, int) or value > 0:
        engine.wait_ge(semaphore, value)


def build(nc, A, out):
    fp32, f32r, bf16 = mybir.dt.float32, mybir.dt.float32r, mybir.dt.bfloat16
    u32, i32 = mybir.dt.uint32, mybir.dt.int32
    ALU, ACT, AX = mybir.AluOpType, mybir.ActivationFunctionType, mybir.AxisListType

    ctx = ExitStack()
    with ctx:
        def sb(name, shape, dt=fp32):
            return ctx.enter_context(nc.sbuf_tensor("sb_" + name, shape, dt))

        def sems(prefix, names):
            return {n: ctx.enter_context(nc.semaphore(f"{prefix}_{n}")) for n in names.split()}

        routed = nc.dram_tensor("routed", [ROWS, D], fp32).ap()
        answers = nc.dram_tensor("answers", [SLOT_TILES * P, D], fp32).ap()

        const = sb("const", [P, C_ALL])
        ident = const[:, C_IDENT:C_IDENT + P]
        first_row = const[:, C_FIRST:C_FIRST + P]
        x_kept = sb("x_kept", [P, BATCHES, TILES * D])
        x_in = sb("x_in", [P, BATCHES, TILES * D])
        xT_in = sb("xT_in", [P, BATCHES, PAD + SEQ])
        w_h = sb("w_h", [P, 2, D])
        w_gate = sb("w_gate", [P, INNER])
        conv_bd = sb("conv_bd", [P, 2, TAPS * P])
        conv_b = sb("conv_b", [P, INNER])
        fc_wT = sb("fc_wT", [P, 2, D])
        ln_gb = sb("ln_gb", [P, 4])
        fc_b = sb("fc_b", [P, 1])
        cproj = sb("cproj", [P, 2, D])
        cproj_b = sb("cproj_b", [P, 2])
        out_wT = sb("out_wT", [P, 2, D])
        gate_wT = sb("gate_wT", [P, EXPERTS])
        w2 = sb("w2", [P, EXPERTS, HIDDEN_TILES, D])
        qk_w = sb("qk_w", [P, 4, P])
        qk_b = sb("qk_b", [P, 4])
        wv = sb("wv", [P, D])
        bv = sb("bv", [P, D])
        omega = sb("omega", [P, 2 * P])
        wout = sb("wout", [P, D])
        bout = sb("bout", [P, D])
        ff_in = conv_bd[:, :, :]
        ff_s = sb("ff_s", [P, 4, FF_TILES])
        ff_out_s = sb("ff_out_s", [P, D])

        def room(tile):
            flat = tile[:, :, :].rearrange("p b t -> p (b t)")
            return flat[:, 0:FF_TILES * FF].rearrange("p (k o) -> p k o", o=FF)
        ff_h = [room(x_in), room(xT_in)]

        before = sb("before", [P, P], bf16)
        ones_bf = sb("ones_bf", [P, P], bf16)
        ones = sb("ones", [P, FEATS])
        zeros = sb("zeros", [P, D])
        minus_half = sb("minus_half", [P, TILES])
        eps = sb("eps", [P, TILES])
        front_hi = sb("front_hi", [P, TAPS + 1, INNER], f32r)
        front_lo = sb("front_lo", [P, TAPS + 1, INNER], f32r)
        fc_g = sb("fc_g", [P, 2, D])
        fc_bias = sb("fc_bias", [P, 1])
        cproj_bb = sb("cproj_bb", [P, 2, P])
        mid_out = sb("mid_out", [P, D])
        out_bias = sb("out_bias", [P, D])
        w13_hi = sb("w13_hi", [P, EXPERTS, 2 * HIDDEN], f32r)
        w13_lo = sb("w13_lo", [P, EXPERTS, 2 * HIDDEN], f32r)
        qk_hi, qk_lo = sb("qk_hi", [P, 4, P], f32r), sb("qk_lo", [P, 4, P], f32r)
        om_hi, om_lo = sb("om_hi", [P, 2 * P], f32r), sb("om_lo", [P, 2 * P], f32r)
        fh_hi, fh_lo = sb("fh_hi", [P, 2 * FF_TILES, FF], f32r), sb("fh_lo", [P, 2 * FF_TILES, FF], f32r)
        ff_out_w = sb("ff_out_w", [P, FF_TILES, D])

        xT_hi, xT_lo = sb("xT_hi", [P, PAD + SEQ], f32r), sb("xT_lo", [P, PAD + SEQ], f32r)
        work = sb("work", [P, 4, TILES * INNER])
        gate, conv, h, hn = (work[:, n, :].rearrange("p (t f) -> p t f", f=INNER) for n in range(4))
        hT = sb("hT", [P, TILES, 2 * P])
        hnT = sb("hnT", [P, 2, SEQ])
        mid = sb("mid", [P, SEQ])
        res = sb("res", [P, TILES * D])
        x1 = sb("x1", [P, TILES * D])
        x1T = sb("x1T", [P, SEQ])
        stats = sb("stats", [P, TILES, 6])
        mv = sb("mv", [P, TILES, 2])
        veps = sb("veps", [P, TILES])
        rstd = sb("rstd", [P, TILES])
        stats_h = sb("stats_h", [P, TILES, 6])
        mv_h = sb("mv_h", [P, TILES, 2])
        veps_h = sb("veps_h", [P, TILES])
        rstd_h = sb("rstd_h", [P, TILES])
        top = sb("top", [P, TILES, EXPERTS])
        top_at = sb("top_at", [P, TILES, EXPERTS], u32)
        below = sb("below", [P, TILES, EXPERTS])
        exps = sb("exps", [P, TILES, EXPERTS])
        denom = sb("denom", [P, TILES])
        rdenom = sb("rdenom", [P, TILES])
        score = sb("score", [P, TILES, TOP_K])
        chosen_at = sb("chosen_at", [P, TILES, TOP_K])
        chosen = sb("chosen", [P, BATCHES, TILES * TOP_K, EXPERTS])
        either = sb("either", [P, TILES, EXPERTS], bf16)
        earlier = sb("earlier", [P, TILES, EXPERTS], bf16)
        rank = sb("rank", [P, TILES, EXPERTS])
        rank_of = sb("rank_of", [P, TILES * TOP_K, EXPERTS])
        row_f = sb("row_f", [P, TILES * TOP_K])
        rows_f = sb("rows_f", [P, BATCHES, TILES * TOP_K])
        row = sb("row", [P, 2, TILES * TOP_K], u32)
        row_all = sb("row_all", [P, BATCHES, TILES * TOP_K], u32)
        xs = sb("xs", [P, 2, TILES * TOP_K, D])

        n_tiles_f = sb("n_tiles_f", [P, EXPERTS])
        n_tiles_i = sb("n_tiles_i", [P, EXPERTS], i32)
        n_tiles_s = sb("n_tiles_s", [P, EXPERTS], i32)
        n_tiles = sb("n_tiles", [P, EXPERTS])
        upto_p = sb("upto_p", [P, EXPERTS, EXPERTS])
        upto = sb("upto", [P, EXPERTS])
        skip_rows = sb("skip_rows", [P, EXPERTS])
        past = sb("past", [P, SLOT_TILES, EXPERTS])
        past_rows = sb("past_rows", [P, SLOT_TILES, EXPERTS])
        ends = sb("ends", [P, EXPERTS], i32)
        shift_r = sb("shift_r", [P, EXPERTS])
        shift = sb("shift", [P, EXPERTS])
        shift_of = sb("shift_of", [P, BATCHES * TILES * TOP_K])
        expert_f = sb("expert_f", [P, SLOT_TILES])
        start_f = sb("start_f", [P, SLOT_TILES])
        start_f2 = sb("start_f2", [P, SLOT_TILES])
        expert_t = sb("expert_t", [P, SLOT_TILES], i32)
        start_t = sb("start_t", [P, SLOT_TILES], i32)

        fly = (HIDDEN_TILES * P,) * 3 + (D, D)
        stage = sb("stage", [P, max(EXPERTS * 2 * HIDDEN, FLY * sum(fly) + 2 * FF)])
        w13 = stage[:, 0:EXPERTS * 2 * HIDDEN].rearrange("p (e c) -> p e c", e=EXPERTS)
        starts = [FLY * sum(fly[:n]) for n in range(len(fly) + 1)]
        hid_room, hidT_room, act1_room, rows_in, rows_out = (stage[:, a:b] for a, b in zip(starts, starts[1:]))
        rows_in, rows_out = (r.rearrange("p (j d) -> p j d", d=D) for r in (rows_in, rows_out))
        f_res = stage[:, starts[-1]:starts[-1] + TILES * D]
        ff_out = stage[:, starts[-1] + FF:starts[-1] + 2 * FF].rearrange("p (k d) -> p k d", d=D)
        rT_hi, rT_lo = sb("rT_hi", [P, FLY, P], f32r), sb("rT_lo", [P, FLY, P], f32r)
        hid, hidT = (r.rearrange("p (j f) -> p j f", j=FLY) for r in (hid_room, hidT_room))
        act1 = act1_room[:, 0:FLY * HIDDEN].rearrange("p (j f) -> p j f", j=FLY)

        row_now = sb("row_now", [P, TILES * TOP_K], u32)
        got = hT[:, :, :].rearrange("p t (k d) -> p t k d", d=D)
        kv, kvT = (hnT[:, n, :].rearrange("p (a f) -> p a f", f=P) for n in range(2))
        sum1, v_tok = (work[:, n, 0:SEQ].rearrange("p (t d) -> p t d", d=D) for n in range(2))
        v_use = mid[:, :].rearrange("p (t d) -> p t d", d=D)
        x2, x2T = work[:, 0, SEQ:], work[:, 1, SEQ:]
        den, rden = work[:, 2, 0:SEQ], work[:, 2, SEQ:]
        att, x3 = work[:, 3, 0:SEQ], work[:, 3, SEQ:]
        x2T_hi, x2T_lo = xT_hi[:, 0:SEQ], xT_lo[:, 0:SEQ]
        st = hid_room[:, 0:4 * SEQ].rearrange("p (s t) -> p s t", t=SEQ)
        kp = hidT_room[:, 0:TILES * HEADS * FEATS].rearrange("p (t f) -> p t f", t=TILES)
        qp = act1_room[:, 0:HEAD_GROUPS * SEQ].rearrange("p (g t) -> p g t", t=SEQ)
        def over(parts, first, n, k):
            return parts[:, :, :].rearrange("p e c -> p (e c)")[:, first:first + n * k].rearrange("p (n k) -> p n k", k=k)
        x3T_hi, x3T_lo = (over(w, 0, BATCHES, SEQ) for w in (w13_hi, w13_lo))
        a_hi, a_lo = (over(w, TOKENS, FF_TILES, SEQ) for w in (w13_hi, w13_lo))
        g_hi, g_lo = (over(w, TOKENS + FF_TILES * SEQ, FF_TILES, SEQ) for w in (w13_hi, w13_lo))
        st_hi, st_lo = (over(w, TOKENS + 2 * FF_TILES * SEQ, 4, SEQ) for w in (w13_hi, w13_lo))
        fi_hi, fi_lo = (over(w, 0, 2, FF) for w in (front_hi, front_lo))

        f_silu = work[:, 0, :].rearrange("p (m t) -> p m t", t=SEQ)
        f_a, f_g = room(x_in)[:, :, 0:SEQ], room(x_in)[:, :, SEQ:]
        f_last = room(xT_in)[:, :, 0:SEQ]
        f_out = work[:, 2, 0:TILES * D]
        odd = sb("odd", [P, 2])
        odd_any = sb("odd_any", [P, 2])
        odd_i = sb("odd_i", [FEATS, 1], i32)

        ps = ctx.enter_context(nc.psum_tensor("ps", [P, 8, 512], fp32))

        in_bank = (1, 2, 3, 1)

        def half_bank(bank, m):
            return ps[:, bank + m % 2, m // 2 * SEQ:(m // 2 + 1) * SEQ]

        ld = sems("ld", "const front x_first x conv w13_a w13_b w2 att ff")
        wt = sems("wt", "before memset hid_zero conv_mm front_hi front_lo fc_g cproj_bb small_mm small x_bias zero_rows moe_hi moe_lo att_hi att_lo ff_hi ff_lo fi_hi fi_lo ff_out odd_any odd_mm odd_i")
        g0 = sems("g0", "x_hi x_lo front gate conv h mv rstd hn tr hT hnT fc mid out res"
                  " mv1 rstd1 x1 kept x1_tr x1T logits choose top_at below exps weigh score"
                  " rank_mm added rank place row carry xs sent sent_last")
        carrier = sems("carrier", "dve pool")
        tb = sems("tb", "count ends step ready place placed")
        mo = sems("mo", "tr hi lo up act1 hid hid_tr hidT down out")
        mo_out = [ctx.enter_context(nc.semaphore(f"mo_stored{j}")) for j in range(FLY)]
        mo_in = [ctx.enter_context(nc.semaphore(f"mo_loaded{j}")) for j in range(FLY)]
        at = sems("at", "row got sum1 res mv rstd x2 kept tr x2T lo qk st st_hi st_lo v_mm v_tok v_use"
                  " kf kp qf qp kv_mm kv kv_tr kvT nd den rden att out"
                  " res3 mv3 rstd3 x3 kept3 tr3 x3_hi x3_lo")
        ff = sems("ff", "in_mm silu act a_hi a_lo g1 g_hi g_lo g2 h1_mm h2_mm out_mm res mv rstd out stored")

        block = ctx.enter_context(nc.Block())

        def slot(b):
            return 1 if isinstance(b, int) and b in (BATCHES - 3, BATCHES - 1) else 0

        def sent_before(engine, b):
            if slot(b):
                wait(engine, g0["sent_last"], 64 if b == BATCHES - 1 else 0)
            else:
                wait(engine, g0["sent"], 64 * (b - 1 if isinstance(b, int) and b == BATCHES - 2 else b))

        def loaded(engine, table, first, count, most):
            return nc.values_load_multi_w_load_instructions(table[0:1, bass.ds(first, count)], engines=(engine,),
                                                            min_val=0, max_val=most, skip_runtime_bounds_check_because="the table is built within these bounds")[1]

        @block.sync
        def _(sp):
            for tile, src in ((w_h, "w_h"), (conv_bd, "conv_bd")):
                sp.dma_start(tile[:, :, :], A[src]).then_inc(ld["front"], 16)
            sp.dma_start(xT_in[:, 0, :], A["xT"][:, 0, :]).then_inc(ld["x_first"], 16)
            for tile, src in ((fc_wT, "fc_wT"), (cproj, "cproj"), (out_wT, "out_wT")):
                sp.dma_start(tile[:, :, :], A[src]).then_inc(ld["conv"], 16)
            sp.dma_start(xT_in[:, 1:, :], A["xT"][:, 1:, :]).then_inc(ld["x"], 16)
            sp.dma_start(x_in[:, :, :], A["x_tok"]).then_inc(ld["x"], 16)
            for half, sem in enumerate((ld["w13_a"], ld["w13_b"])):
                part = slice(half * EXPERTS // 2, (half + 1) * EXPERTS // 2)
                sp.dma_start(w13[:, part, :], A["w13"][:, part, :]).then_inc(sem, 16)
            sp.dma_start(w2[:, :, :, :], A["w2"]).then_inc(ld["w2"], 16)
            sp.wait_ge(wt["memset"], MEMSETS)
            sp.dma_start(routed[EXPERTS * REGION:ROWS, :].rearrange("(t p) d -> p t d", p=P),
                         zeros[:, :].unsqueeze(1).to_broadcast([P, DUMMY_TILES, D])).then_inc(wt["zero_rows"], 16)
            for tile, src in ((qk_w, "qk_w"),):
                sp.dma_start(tile[:, :, :], A[src]).then_inc(ld["att"], 16)
            for tile, src in ((qk_b, "qk_b"), (wv, "wv"), (bv, "bv"), (omega, "omega"), (wout, "wout"), (bout, "bout")):
                sp.dma_start(tile[:, :], A[src]).then_inc(ld["att"], 16)
            sp.dma_start(ff_s[:, :, :], A["ff_s"]).then_inc(ld["ff"], 16)
            sp.dma_start(ff_out_s[:, :], A["ff_out_s"]).then_inc(ld["ff"], 16)
            sp.wait_ge(wt["conv_mm"], 2)
            sp.dma_start(ff_in[:, :, :], A["ff_in"]).then_inc(ld["ff"], 16)

            sp.wait_ge(tb["ends"], 1)
            for e in range(0, EXPERTS, 2):
                end = sp.value_load(ends[0:1, e:e + 1], min_val=0, max_val=EXPERTS * REGION)
                sp.dma_start(routed[bass.ds(end, P), :], zeros[:, :]).then_inc(wt["zero_rows"], 16)
            sp.wait_ge(tb["ready"], 1)
            sp.wait_ge(g0["sent"], 64 * (BATCHES - 2))
            sp.wait_ge(g0["sent_last"], 64 * 2)
            sp.wait_ge(wt["zero_rows"], 16 * (EXPERTS + 1))

            def rows_step(i):
                if live(i, SLOT_TILES // FLY):
                    start = loaded(mybir.EngineType.SP, start_t, FLY * i, FLY, ROWS - P)
                    for j in range(FLY):
                        t = FLY * i + j
                        wait(sp, mo["tr"], t - FLY + 1)
                        sp.dma_start(rows_in[:, j, :], routed[bass.ds(start[j], P), :]).then_inc(mo_in[j], 16)
                if isinstance(i, int) and i == 1:
                    sp.wait_ge(wt["moe_lo"], EXPERTS)
                    sp.dma_start(ff_out[:, :, :], A["ff_out"]).then_inc(ld["ff"], 16)
                    sp.wait_ge(g0["res"], BATCHES)
                    sp.wait_ge(g0["front"], BATCHES)
                    for k, tile in enumerate(ff_h):
                        sp.dma_start(tile, A["ff_h"][:, k * FF_TILES:(k + 1) * FF_TILES, :]).then_inc(ld["ff"], 16)
            steps(sp, SLOT_TILES // FLY, 1, rows_step)

            def store(b):
                sp.wait_ge(ff["out"], b + 1)
                sp.dma_start(out.rearrange("(b t p) d -> b p t d", t=TILES, p=P)[b],
                             f_out.rearrange("p (t d) -> p t d", d=D)).then_inc(ff["stored"], 16)
            steps(sp, BATCHES, 0, store)
            sp.wait_ge(ff["stored"], 16 * BATCHES)

        @block.gpsimd
        def _(pool):
            pool.memset(zeros[:, :], 0.0).then_inc(wt["memset"], 1)
            pool.memset(ones[:, :], 1.0).then_inc(wt["memset"], 1)
            pool.memset(ones_bf[:, :], 1.0).then_inc(wt["memset"], 1)
            pool.memset(minus_half[:, :], -0.5).then_inc(wt["memset"], 1)
            pool.memset(eps[:, :], EPS).then_inc(wt["memset"], 1)

            def inverse_root(sem_mv, sem, n, mv_, veps_, rstd_, tiles):
                pool.wait_ge(sem_mv, 2 * n)
                nc.gpsimd.tensor_tensor(veps_[:, 0:tiles], mv_[:, 0:tiles, 1], eps[:, 0:tiles], ALU.add).then_inc(sem, 1)
                pool.wait_ge(sem, 2 * n - 1)
                for t in range(0, tiles, TILES):
                    last = nc.gpsimd.tensor_tensor(rstd_[:, t:t + TILES], veps_[:, t:t + TILES], minus_half[:, :], ALU.pow)
                last.then_inc(sem, 1)

            pool.wait_ge(wt["memset"], MEMSETS)
            def route_step(i):
                b = i - 4
                if live(b, BATCHES):
                    pool.wait_ge(g0["xs"], b + 1)
                    pool.wait_ge(g0["row"], b + 1)
                    alone(pool, carrier["pool"])

                def scatter(b, r):
                    nc.gpsimd.indirect_dma_start(
                        routed[:, :], bass.IndirectOffsetOnAxis(ap=row[:, slot(b), r:r + 1], axis=0),
                        xs[:, slot(b), r, :], None).then_inc(g0["sent_last" if slot(b) else "sent"], 16)
                early = TOP_K if isinstance(i, int) and i >= BATCHES else 4
                if live(b, BATCHES):
                    for r in range(early):
                        scatter(b, r)
                if live(i - 2, BATCHES):
                    inverse_root(g0["mv1"], g0["rstd1"], i - 1, mv, veps, rstd, TILES)
                if live(b, BATCHES):
                    for r in range(early, TILES * TOP_K):
                        scatter(b, r)
                if live(i, BATCHES):
                    inverse_root(g0["mv"], g0["rstd"], i + 1, mv_h, veps_h, rstd_h, TILES)
                if isinstance(i, int) and i == 0:
                    pool.wait_ge(ld["x"], 32)
                    pool.wait_ge(wt["small"], 3)
                    x_tiles = x_in[:, :, :].rearrange("p b (t d) -> p (b t) d", d=D)
                    nc.gpsimd.tensor_tensor(x_tiles, x_tiles, out_bias[:, :].unsqueeze(1).to_broadcast([P, BATCHES * TILES, D]),
                                            ALU.add).then_inc(wt["x_bias"], 1)
                e = i - 1
                if live(e, EXPERTS):
                    pool.wait_ge(wt["moe_hi"], e + 1)
                    nc.gpsimd.tensor_tensor(w13_lo[:, e, :], w13[:, e, :], w13_hi[:, e, :].bitcast(fp32),
                                            ALU.subtract).then_inc(wt["moe_lo"], 1)
            steps(pool, BATCHES, 4, route_step)
            pool.wait_ge(wt["moe_lo"], EXPERTS)
            pool.memset(hid[:, :, :], 0.0).then_inc(wt["hid_zero"], 1)

            pool.wait_ge(ld["att"], 16 * 7)
            nc.gpsimd.tensor_copy(qk_hi[:, :, :], qk_w[:, :, :]).then_inc(wt["att_hi"], 1)
            nc.gpsimd.tensor_copy(om_hi[:, :], omega[:, :]).then_inc(wt["att_hi"], 1)
            pool.wait_ge(wt["att_hi"], 2)
            nc.gpsimd.tensor_tensor(qk_lo[:, :, :], qk_w[:, :, :], qk_hi[:, :, :].bitcast(fp32), ALU.subtract).then_inc(wt["att_lo"], 1)
            nc.gpsimd.tensor_tensor(om_lo[:, :], omega[:, :], om_hi[:, :].bitcast(fp32), ALU.subtract).then_inc(wt["att_lo"], 1)
            pool.wait_ge(ld["ff"], 16 * 6)
            for half, whole in enumerate(ff_h):
                with pool.Fori(0, FF_TILES) as k:
                    r = half * FF_TILES + k
                    nc.gpsimd.tensor_copy(fh_hi[:, r, :], whole[:, k, :]).then_inc(wt["ff_hi"], 1)
                    pool.wait_ge(wt["ff_hi"], r + 1)
                    nc.gpsimd.tensor_tensor(fh_lo[:, r, :], whole[:, k, :], fh_hi[:, r, :].bitcast(fp32), ALU.subtract).then_inc(wt["ff_lo"], 1)
            nc.gpsimd.tensor_copy(fi_hi, ff_in).then_inc(wt["fi_hi"], 1)
            pool.wait_ge(wt["fi_hi"], 1)
            nc.gpsimd.tensor_tensor(fi_lo, ff_in, fi_hi.bitcast(fp32), ALU.subtract).then_inc(wt["fi_lo"], 1)
            nc.gpsimd.tensor_tensor(ff_out_w[:, :, :], ff_out[:, :, :],
                                    ff_out_s[:, :].unsqueeze(1).to_broadcast([P, FF_TILES, D]), ALU.mult).then_inc(wt["ff_out"], 1)

            pool.wait_ge(tb["placed"], 1)
            for j in range(FLY):
                pool.wait_ge(mo_out[j], 16 * (SLOT_TILES // FLY))
            def attention_step(i, meanwhile=None):
                def gather(ks):
                    for r in ks:
                        nc.gpsimd.indirect_dma_start(
                            got[:, r // TOP_K, r % TOP_K, :], None,
                            answers[:, :], bass.IndirectOffsetOnAxis(ap=row_now[:, r:r + 1], axis=0)).then_inc(at["got"], 16)
                if live(i, BATCHES):
                    wait(pool, at["got"], 64 * i)
                    nc.gpsimd.tensor_copy(row_now[:, :], row_all[:, i, :]).then_inc(at["row"], 1)
                    pool.wait_ge(at["row"], i + 1)
                    wait(pool, at["sum1"], i)
                    alone(pool, carrier["pool"])
                    gather(range(1))
                b = i - 1
                if live(b, BATCHES):
                    inverse_root(at["mv"], at["rstd"], b + 1, mv, veps, rstd, TILES)
                if live(i, BATCHES):
                    gather(range(1, TOP_K))
                b = i - 6
                if live(b, BATCHES):
                    inverse_root(at["mv3"], at["rstd3"], b + 1, mv_h, veps_h, rstd_h, TILES)
                if live(i, BATCHES):
                    gather(range(TOP_K, TILES * TOP_K))
                b = i - 3
                if live(b, BATCHES):
                    for part, (n, used) in enumerate(((slice(2, 4), at["kf"]), (slice(0, 2), at["qf"]))):
                        pool.wait_ge(at["st_hi"], 2 * b + part + 1)
                        wait(pool, used, b)
                        nc.gpsimd.tensor_tensor(st_lo[:, n, :], st[:, n, :], st_hi[:, n, :].bitcast(fp32), ALU.subtract).then_inc(at["st_lo"], 1)
                if meanwhile:
                    meanwhile()

            def mlp_first(i):
                pass

            def mlp_rest(i):
                b = i - 3
                if live(b, BATCHES):
                    inverse_root(ff["mv"], ff["rstd"], b + 1, mv, veps, rstd, TILES)
                if live(i, BATCHES):
                    for m in range(FF_TILES):
                        pool.wait_ge(ff["a_hi"], FF_TILES * i + m + 1)
                        nc.gpsimd.tensor_tensor(a_lo[:, m, :], f_a[:, m, :], a_hi[:, m, :].bitcast(fp32), ALU.subtract).then_inc(ff["a_lo"], 1)
            attention_then_mlp(pool, attention_step, mlp_first, mlp_rest)
            steps(pool, BATCHES, MLP_LAG, mlp_rest, first=EARLY)

        @block.scalar
        def _(act):
            act.dma_start(w_gate[:, :], A["w_gate"]).then_inc(ld["front"], 16)
            act.dma_start(const[:, :], A["const"]).then_inc(ld["const"], 16)
            for tile, src in ((conv_b, "conv_b"), (ln_gb, "ln_gb"), (fc_b, "fc_b"),
                              (cproj_b, "cproj_b"), (gate_wT, "gate_wT")):
                act.dma_start(tile[:, :], A[src]).then_inc(ld["conv"], 16)

            act.wait_ge(ld["front"], 16 * 3)
            nc.scalar.activation(front_hi[:, TAPS, :], w_gate[:, :], ACT.Copy).then_inc(wt["front_hi"], 1)
            for t in range(2):
                act.wait_ge(wt["conv_mm"], t + 1)
                nc.scalar.activation(front_hi[:, 0:TAPS, t * P:(t + 1) * P],
                                     ps[:, t, :].rearrange("p (k o) -> p k o", o=P), ACT.Copy).then_inc(wt["front_hi"], 1)

            def high_part(b):
                if isinstance(b, int) and b <= 1:
                    act.wait_ge(ld["x"] if b else ld["x_first"], 16 * (b + 1))
                wait(act, g0["front"], b)
                nc.scalar.activation(xT_hi[:, :], xT_in[:, b, :], ACT.Copy).then_inc(g0["x_hi"], 1)

            def gate_of(b):
                act.wait_ge(g0["front"], b + 1)
                wait(act, g0["h"], b)
                nc.scalar.activation(gate[:, :, :], ps[:, 0:2, INNER:], ACT.Silu).then_inc(g0["gate"], 1)
            high_part(0)
            gate_of(0)
            high_part(1)

            def conv_step(i):
                b = i - 1
                if live(b, BATCHES):
                    act.wait_ge(g0["tr"], b + 1)
                    wait(act, g0["out"], b)
                    nc.scalar.activation(hT[:, :, :].rearrange("p t f -> p (t f)"), ps[:, 2, :], ACT.Copy).then_inc(g0["hT"], 1)
                b = i - 3
                if live(b, BATCHES):
                    act.wait_ge(g0["below"], b + 1)
                    nc.scalar.activation(exps[:, :, :], below[:, :, :], ACT.Exp).then_inc(g0["exps"], 1)
                if live(i + 1, BATCHES):
                    gate_of(i + 1)
                if live(i + 2, BATCHES):
                    high_part(i + 2)
                b = i - 2
                if live(b, BATCHES):
                    act.wait_ge(g0["x1_tr"], b + 1)
                    wait(act, g0["logits"], b)
                    nc.scalar.activation(x1T[:, :], ps[:, 6, 0:SEQ], ACT.Copy).then_inc(g0["x1T"], 1)
                b = i - 1
                if live(b, BATCHES):
                    act.wait_ge(g0["fc"], b + 1)
                    act.wait_ge(wt["small"], 2)
                    nc.scalar.activation(mid[:, :], ps[:, 4, 0:SEQ], ACT.Silu, bias=fc_bias[:, 0:1]).then_inc(g0["mid"], 1)
                b = i - 2
                if live(b, BATCHES):
                    act.wait_ge(g0["x1"], b + 1)
                    nc.scalar.activation(x_kept[:, b, :], x1[:, :], ACT.Copy).then_inc(g0["kept"], 1)
                b = i - 3
                if live(b, BATCHES):
                    act.wait_ge(g0["score"], b + 1)
                    act.wait_ge(g0["kept"], b + 1)
                    sent_before(act, b)
                    for t in range(TILES):
                        for k in range(TOP_K):
                            last = nc.scalar.activation(xs[:, slot(b), TOP_K * t + k, :], x_kept[:, b, t * D:(t + 1) * D],
                                                        ACT.Copy, scale=score[:, t, k:k + 1])
                    last.then_inc(g0["xs"], 1)
                if live(i, BATCHES):
                    first = isinstance(i, int) and i < EXPERTS // 2
                    act.wait_ge(ld["w13_a"] if first else ld["w13_b"], 16)
                    nc.scalar.activation(w13_hi[:, i, :], w13[:, i, :], ACT.Copy).then_inc(wt["moe_hi"], 1)
            steps(act, BATCHES, 3, conv_step, ahead=2)

            act.wait_ge(tb["ends"], 1)
            for e in range(1, EXPERTS, 2):
                end = act.value_load(ends[0:1, e:e + 1], min_val=0, max_val=EXPERTS * REGION)
                act.dma_start(routed[bass.ds(end, P), :], zeros[:, :]).then_inc(wt["zero_rows"], 16)

            def expert_step(i):
                for j in range(FLY):
                    t = FLY * i + j
                    if live(i, SLOT_TILES // FLY):
                        act.wait_ge(mo["tr"], t + 1)
                        wait(act, mo["up"], t - FLY + 1)
                        nc.scalar.activation(rT_hi[:, j, :], ps[:, 0, 0:P], ACT.Copy).then_inc(mo["hi"], 1)
                    u, ju = t - 1, (j - 1) % FLY
                    if live(u, SLOT_TILES):
                        act.wait_ge(mo["up"], u + 1)
                        wait(act, mo["hid"], u - FLY + 1)
                        nc.scalar.activation(act1[:, ju, :], ps[:, 2, 0:HIDDEN], ACT.Silu).then_inc(mo["act1"], 1)
                    u, ju = t - 5, (j - 5) % FLY
                    if live(u, SLOT_TILES):
                        act.wait_ge(mo["out"], u + 1)
                        act.dma_start(answers.rearrange("(t p) d -> t p d", p=P)[u], rows_out[:, ju, :]).then_inc(mo_out[ju], 16)
                    u, ju = t - 4, (j - 4) % FLY
                    if live(u, SLOT_TILES):
                        act.wait_ge(mo["down"], u + 1)
                        wait(act, mo_out[ju], 16 * (i + (j - 4) // FLY))
                        nc.scalar.activation(rows_out[:, ju, :], ps[:, 6, 0:D], ACT.Copy).then_inc(mo["out"], 1)
            steps(act, SLOT_TILES // FLY, 2, expert_step)

            def biased_and_squared(b, part):
                if part == 0:
                    act.wait_ge(at["qk"], b + 1)
                wait(act, at["st_lo"], 2 * b - 1 + part)
                tiles = (0, 1) if part else (2, 3)
                def products(rows, n):
                    return ps[rows, 1 + n // 2, n % 2 * SEQ:(n % 2 + 1) * SEQ]
                low, high = slice(0, 64), slice(64, 128)
                for n in tiles:
                    nc.scalar.activation(st[low, n, :], products(low, n), ACT.Identity, bias=qk_b[low, n:n + 1])
                for n in tiles:
                    last = nc.scalar.activation(st[high, n, :], products(high, n), ACT.Square, bias=qk_b[high, n:n + 1])
                last.then_inc(at["st"], 1)

            def attention_step(i, meanwhile=None):
                if live(i - 3, BATCHES):
                    biased_and_squared(i - 3, 0)
                b = i - 4
                if live(b, BATCHES):
                    act.wait_ge(at["kf"], b + 1)
                    wait(act, at["kv_mm"], b)
                    nc.scalar.activation(kp[:, :, :], ps[:, 4:6, :], ACT.Exp).then_inc(at["kp"], 1)
                b = i - 5
                if live(b, BATCHES):
                    act.wait_ge(at["nd"], b + 1)
                    wait(act, at["rden"], b)
                    nc.scalar.activation(den[:, :], ps[:, 7, SEQ:], ACT.Copy, bias=1e-6).then_inc(at["den"], 1)
                if live(i - 3, BATCHES):
                    biased_and_squared(i - 3, 1)
                b = i - 4
                if live(b, BATCHES):
                    act.wait_ge(at["qf"], b + 1)
                    wait(act, at["nd"], b)
                    nc.scalar.activation(qp[:, :, :].rearrange("p g t -> p (g t)"),
                                         ps[:, 4:6, :].rearrange("p a t -> p (a t)"), ACT.Exp).then_inc(at["qp"], 1)
                b = i - 1
                if live(b, BATCHES):
                    act.wait_ge(at["tr"], b + 1)
                    wait(act, at["v_mm"], b)
                    wait(act, at["lo"], b)
                    nc.scalar.activation(x2T[:, :], ps[:, 0, 0:SEQ], ACT.Copy)
                    wait(act, at["qk"], b)
                    nc.scalar.activation(x2T_hi[:, :], ps[:, 0, 0:SEQ], ACT.Copy).then_inc(at["x2T"], 1)
                    act.wait_ge(at["x2"], b + 1)
                    nc.scalar.activation(x_kept[:, b, :], x2, ACT.Copy).then_inc(at["kept"], 1)
                b = i - 4
                if live(b, BATCHES):
                    act.wait_ge(at["kv_tr"], b + 1)
                    wait(act, at["nd"], b)
                    nc.scalar.activation(kvT[:, :, :].rearrange("p a f -> p (a f)"), ps[:, 6, 256:512], ACT.Copy).then_inc(at["kvT"], 1)
                if meanwhile:
                    meanwhile()
                b = i - 6
                if live(b, BATCHES):
                    act.wait_ge(at["tr3"], b + 1)
                    nc.scalar.activation(x3T_hi[:, b, :], ps[:, 0, SEQ:], ACT.Copy).then_inc(at["x3_hi"], 1)
                    act.wait_ge(at["x3"], b + 1)
                    nc.scalar.activation(x_kept[:, b, :], x3, ACT.Copy).then_inc(at["kept3"], 1)

            def mlp_first(i):
                if isinstance(i, int) and i == 0:
                    act.wait_ge(ld["ff"], 16 * 6)
                    act.wait_ge(wt["ff_lo"], 2 * FF_TILES)
                    act.wait_ge(at["res"], BATCHES)
                    act.wait_ge(at["tr"], BATCHES)
                    act.wait_ge(at["kept"], BATCHES)
                for m in range(FF_TILES):
                    if live(i, BATCHES):
                        n = FF_TILES * i + m
                        act.wait_ge(ff["in_mm"], n + 1)
                        wait(act, ff["act"], n - 1)
                        nc.scalar.activation(f_silu[:, m % 2, :], ps[:, in_bank[m], 0:SEQ], ACT.Silu,
                                             scale=ff_s[:, 0, m:m + 1]).then_inc(ff["silu"], 1)

            def mlp_rest(i):
                for pair in range(0, FF_TILES, 2):
                    b = i - 2
                    if live(b, BATCHES):
                        for m in range(pair, pair + 2):
                            act.wait_ge(ff["h2_mm"], FF_TILES * b + m + 1)
                            wait(act, ff["out_mm"], b)
                            nc.scalar.activation(f_last[:, m, :], half_bank(6, m), ACT.Gelu,
                                                 scale=ff_s[:, 3, m:m + 1]).then_inc(ff["g2"], 1)
                    b = i - 1
                    if live(b, BATCHES):
                        for m in range(pair, pair + 2):
                            n = FF_TILES * b + m
                            act.wait_ge(ff["h1_mm"], n + 1)
                            wait(act, ff["g_lo"], n - FF_TILES + 1)
                            nc.scalar.activation(f_g[:, m, :], half_bank(4, m), ACT.Gelu,
                                                 scale=ff_s[:, 2, m:m + 1]).then_inc(ff["g1"], 1)

            def mlp_step(i):
                mlp_first(i)
                mlp_rest(i)
            attention_then_mlp(act, attention_step, mlp_first, mlp_rest)
            steps(act, BATCHES, MLP_LAG, mlp_step, first=EARLY)

        @block.vector
        def _(dve):
            V = nc.vector

            def split(hi, lo, src, sem_hi, sem_lo, n):
                V.tensor_copy(hi, src).then_inc(sem_hi, 1)
                dve.wait_ge(sem_hi, n)
                V.tensor_tensor(lo, src, hi.bitcast(fp32), ALU.subtract).then_inc(sem_lo, 1)

            def row_sums(src, stats_, tiles, width, sem):
                for t in range(tiles):
                    last = V.bn_stats(stats_[:, t, :], src[:, t * width:(t + 1) * width])
                last.then_inc(sem, 1)

            def row_moments(stats_, mv_, tiles, sem, n):
                dve.wait_ge(sem, 2 * n - 1)
                alone(dve, carrier["dve"])
                for t in range(tiles):
                    last = V.bn_aggr(mv_[:, t, :], stats_[:, t, :])
                last.then_inc(sem, 1)

            def moments(src, stats_, mv_, tiles, width, sem, n):
                row_sums(src, stats_, tiles, width, sem)
                row_moments(stats_, mv_, tiles, sem, n)

            def normalise(dst, src, mv_, rstd_, tiles, width, sem):
                for t in range(tiles):
                    cols = slice(t * width, (t + 1) * width)
                    last = V.tensor_scalar(dst[:, cols], src[:, cols], mv_[:, t, 0:1], rstd_[:, t:t + 1],
                                           ALU.subtract, ALU.mult)
                last.then_inc(sem, 1)

            V.memset(earlier[:, :, :], 0.0).then_inc(wt["before"], 1)
            dve.wait_ge(ld["const"], 16)
            V.tensor_copy(before[:, :], const[:, C_BEFORE:C_BEFORE + P]).then_inc(wt["before"], 1)
            dve.wait_ge(wt["front_hi"], 1)
            V.tensor_tensor(front_lo[:, TAPS, :], w_gate[:, :], front_hi[:, TAPS, :].bitcast(fp32), ALU.subtract).then_inc(wt["front_lo"], 1)
            for t in range(2):
                dve.wait_ge(wt["front_hi"], t + 2)
                V.tensor_tensor(front_lo[:, 0:TAPS, t * P:(t + 1) * P], ps[:, t, :].rearrange("p (k o) -> p k o", o=P),
                                front_hi[:, 0:TAPS, t * P:(t + 1) * P].bitcast(fp32), ALU.subtract).then_inc(wt["front_lo"], 1)

            def small_weights():
                dve.wait_ge(wt["small_mm"], 1)
                V.tensor_copy(mid_out[:, :], ps[:, 4, 0:D]).then_inc(wt["small"], 1)
                dve.wait_ge(wt["small_mm"], 2)
                V.tensor_tensor(fc_bias[:, :], ps[:, 6, 0:1], fc_b[:, :], ALU.add).then_inc(wt["small"], 1)
                dve.wait_ge(wt["small_mm"], 3)
                V.tensor_copy(out_bias[:, :], ps[:, 5, 0:D]).then_inc(wt["small"], 1)

            iota = const[:, C_IOTA:C_IOTA + EXPERTS]
            base = const[:, C_BASE:C_BASE + EXPERTS]
            logits = ps[:, 6, SEQ:SEQ + TILES * EXPERTS].rearrange("p (t e) -> p t e", e=EXPERTS)
            rank_ps = ps[:, 7, 32:32 + TILES * EXPERTS].rearrange("p (t e) -> p t e", e=EXPERTS)

            def best(b):
                dve.wait_ge(g0["logits"], b + 1)
                alone(dve, carrier["dve"])
                for t in range(TILES):
                    last = V.max(top[:, t, :], logits[:, t, :])
                last.then_inc(g0["choose"], 1)

            def best_at(b):
                dve.wait_ge(g0["choose"], 4 * b + 1)
                alone(dve, carrier["dve"])
                for t in range(TILES):
                    last = V.max_index(top_at[:, t, :], top[:, t, :], logits[:, t, :])
                last.then_inc(g0["top_at"], 1)
                V.tensor_tensor(below[:, :, :], top[:, :, :], top[:, :, 0:1].to_broadcast([P, TILES, EXPERTS]),
                                ALU.subtract).then_inc(g0["below"], 1)

            def best_numbers(b):
                dve.wait_ge(g0["top_at"], b + 1)
                V.tensor_copy(chosen_at[:, :, :], top_at[:, :, 0:TOP_K]).then_inc(g0["choose"], 1)

            def mark(b):
                dve.wait_ge(g0["choose"], 4 * b + 2)
                V.tensor_tensor(chosen[:, b, :, :].rearrange("p (t k) e -> p t k e", k=TOP_K),
                                iota.unsqueeze(1).unsqueeze(1).to_broadcast([P, TILES, TOP_K, EXPERTS]),
                                chosen_at[:, :, :].unsqueeze(3).to_broadcast([P, TILES, TOP_K, EXPERTS]),
                                ALU.is_equal).then_inc(g0["choose"], 1)

            def mark_both(b):
                dve.wait_ge(g0["choose"], 4 * b + 3)
                wait(dve, g0["rank_mm"], b)
                of_tile = chosen[:, b, :, :].rearrange("p (t k) e -> p t k e", k=TOP_K)
                V.tensor_tensor(either[:, :, :], of_tile[:, :, 0, :], of_tile[:, :, 1, :], ALU.add).then_inc(g0["choose"], 1)

            def add_first(b):
                dve.wait_ge(g0["choose"], 4 * b + 4)
                V.tensor_tensor(earlier[:, 1, :], earlier[:, 0, :], either[:, 0, :], ALU.add).then_inc(g0["added"], 1)

            def weigh_and_place(b):
                dve.wait_ge(g0["rank_mm"], b + 1)
                V.tensor_tensor(rank[:, :, :], rank_ps, base.unsqueeze(1).to_broadcast([P, TILES, EXPERTS]),
                                ALU.add).then_inc(g0["rank"], 1)
                dve.wait_ge(g0["exps"], b + 1)
                V.reduce_sum(denom[:, :], exps[:, :, :], axis=AX.X).then_inc(g0["weigh"], 1)
                dve.wait_ge(g0["rank"], b + 1)
                V.tensor_tensor(rank_of[:, :, :].rearrange("p (t k) e -> p t k e", k=TOP_K),
                                chosen[:, b, :, :].rearrange("p (t k) e -> p t k e", k=TOP_K),
                                rank[:, :, :].unsqueeze(2).to_broadcast([P, TILES, TOP_K, EXPERTS]),
                                ALU.mult).then_inc(g0["place"], 1)
                dve.wait_ge(g0["weigh"], 2 * b + 1)
                V.reciprocal(rdenom[:, :], denom[:, :]).then_inc(g0["weigh"], 1)
                dve.wait_ge(g0["place"], 2 * b + 1)
                V.reduce_sum(row_f[:, :], rank_of[:, :, :], axis=AX.X).then_inc(g0["place"], 1)
                dve.wait_ge(g0["weigh"], 2 * b + 2)
                wait(dve, g0["xs"], b)
                V.tensor_tensor(score[:, :, :], exps[:, :, 0:TOP_K],
                                rdenom[:, :].unsqueeze(2).to_broadcast([P, TILES, TOP_K]), ALU.mult).then_inc(g0["score"], 1)
                V.tensor_tensor(earlier[:, 0, :], earlier[:, 1, :], either[:, 1, :], ALU.add).then_inc(g0["carry"], 1)
                dve.wait_ge(g0["place"], 2 * b + 2)
                sent_before(dve, b)
                V.tensor_copy(row[:, slot(b), :], row_f[:, :])
                V.tensor_copy(rows_f[:, b, :], row_f[:, :]).then_inc(g0["row"], 1)

            h_flat, hn_flat = (x[:, :, :].rearrange("p t f -> p (t f)") for x in (h, hn))

            def low_part(b):
                dve.wait_ge(g0["x_hi"], b + 1)
                V.tensor_tensor(xT_lo[:, :], xT_in[:, b, :], xT_hi[:, :].bitcast(fp32), ALU.subtract).then_inc(g0["x_lo"], 1)
            low_part(0)
            dve.wait_ge(ld["conv"], 16 * 8)
            for t in range(2):
                V.tensor_copy(cproj_bb[:, t, :], cproj_b[:, t:t + 1].to_broadcast([P, P])).then_inc(wt["cproj_bb"], 1)
                V.tensor_scalar(fc_g[:, t, :], fc_wT[:, t, :], ln_gb[:, t:t + 1], None, ALU.mult).then_inc(wt["fc_g"], 1)

            def conv_step(i):
                chosen_now, summed, normed = live(i - 3, BATCHES), live(i - 2, BATCHES), live(i - 1, BATCHES)
                if normed:
                    dve.wait_ge(g0["rstd"], 2 * i)
                    wait(dve, g0["tr"], i - 1)
                    normalise(hn_flat, h_flat, mv_h, rstd_h, TILES, INNER, g0["hn"])
                if live(i, BATCHES):
                    dve.wait_ge(g0["gate"], i + 1)
                    V.tensor_tensor(conv[:, :, :], ps[:, 0:2, 0:INNER],
                                    conv_b[:, :].unsqueeze(1).to_broadcast([P, TILES, INNER]), ALU.add).then_inc(g0["conv"], 1)
                if live(i + 1, BATCHES):
                    low_part(i + 1)
                if chosen_now:
                    best(i - 3)
                if summed:
                    dve.wait_ge(g0["out"], i - 1)
                    wait(dve, g0["x1"], i - 2)
                    if isinstance(i, int) and i == 2:
                        dve.wait_ge(wt["x_bias"], 1)
                    V.tensor_tensor(res[:, :], ps[:, 5, 0:SEQ], x_in[:, i - 2, :], ALU.add).then_inc(g0["res"], 1)
                if chosen_now:
                    best_at(i - 3)
                if summed:
                    dve.wait_ge(g0["res"], i - 1)
                    row_sums(res, stats, TILES, D, g0["mv1"])
                if chosen_now:
                    best_numbers(i - 3)
                if live(i, BATCHES):
                    dve.wait_ge(g0["conv"], i + 1)
                    wait(dve, g0["tr"], i)
                    V.tensor_tensor(h[:, :, :], conv[:, :, :], gate[:, :, :], ALU.mult).then_inc(g0["h"], 1)
                if chosen_now:
                    mark(i - 3)
                if summed:
                    row_moments(stats, mv, TILES, g0["mv1"], i - 1)
                if chosen_now:
                    mark_both(i - 3)
                if live(i, BATCHES):
                    dve.wait_ge(g0["h"], i + 1)
                    row_sums(h_flat, stats_h, TILES, INNER, g0["mv"])
                if chosen_now:
                    add_first(i - 3)
                if normed:
                    dve.wait_ge(g0["tr"], i)
                    wait(dve, g0["fc"], i - 1)
                    V.tensor_copy(hnT[:, :, :].rearrange("p k (t q) -> p t k q", q=P),
                                  ps[:, 3, :].rearrange("p (t k q) -> p t k q", k=2, q=P)).then_inc(g0["hnT"], 1)
                if live(i, BATCHES):
                    row_moments(stats_h, mv_h, TILES, g0["mv"], i + 1)
                if summed:
                    dve.wait_ge(g0["rstd1"], 2 * (i - 1))
                    wait(dve, g0["kept"], i - 2)
                    wait(dve, g0["x1_tr"], i - 2)
                    normalise(x1, res, mv, rstd, TILES, D, g0["x1"])
                if isinstance(i, int) and i == 0:
                    small_weights()
                if chosen_now:
                    weigh_and_place(i - 3)
            steps(dve, BATCHES, 3, conv_step, ahead=1)

            dve.wait_ge(tb["count"], 1)
            V.tensor_tensor(ends[:, :], ps[:, 7, 64:64 + EXPERTS], base, ALU.add).then_inc(tb["ends"], 1)
            V.tensor_scalar(n_tiles_f[:, :], ps[:, 7, 64:64 + EXPERTS], float(P - 1), None, ALU.add).then_inc(tb["step"], 1)
            dve.wait_ge(tb["step"], 1)
            V.tensor_copy(n_tiles_i[:, :], n_tiles_f[:, :]).then_inc(tb["step"], 1)
            dve.wait_ge(tb["step"], 2)
            V.tensor_scalar(n_tiles_s[:, :], n_tiles_i[:, :], P.bit_length() - 1, None, ALU.logical_shift_right).then_inc(tb["step"], 1)
            dve.wait_ge(tb["step"], 3)
            V.tensor_copy(n_tiles[:, :], n_tiles_s[:, :]).then_inc(tb["step"], 1)
            dve.wait_ge(tb["step"], 4)
            V.tensor_tensor(upto_p[:, :, :], const[:, C_UPTO:C_UPTO + EXPERTS * EXPERTS].rearrange("p (a b) -> p a b", b=EXPERTS),
                            n_tiles[:, :].unsqueeze(1).to_broadcast([P, EXPERTS, EXPERTS]), ALU.mult).then_inc(tb["step"], 1)
            V.tensor_scalar(skip_rows[:, :], n_tiles[:, :], -float(P), float(REGION), ALU.mult, ALU.add).then_inc(tb["step"], 1)
            dve.wait_ge(tb["step"], 5)
            V.reduce_sum(upto[:, :], upto_p[:, :, :], axis=AX.X).then_inc(tb["step"], 1)
            dve.wait_ge(tb["step"], 7)
            V.tensor_tensor(past[:, :, :], upto[:, :].unsqueeze(1).to_broadcast([P, SLOT_TILES, EXPERTS]),
                            const[:, C_TILE:C_TILE + SLOT_TILES].unsqueeze(2).to_broadcast([P, SLOT_TILES, EXPERTS]),
                            ALU.is_le).then_inc(tb["step"], 1)
            dve.wait_ge(tb["step"], 8)
            dve.wait_ge(tb["step"], 6)
            V.tensor_tensor(past_rows[:, :, :], past[:, :, :],
                            skip_rows[:, :].unsqueeze(1).to_broadcast([P, SLOT_TILES, EXPERTS]), ALU.mult).then_inc(tb["step"], 1)
            V.reduce_sum(expert_f[:, :], past[:, :, :], axis=AX.X).then_inc(tb["step"], 1)
            dve.wait_ge(tb["step"], 9)
            V.reduce_sum(start_f[:, :], past_rows[:, :, :], axis=AX.X).then_inc(tb["step"], 1)
            dve.wait_ge(tb["step"], 11)
            V.tensor_tensor(start_f2[:, :], start_f[:, :], const[:, C_ROW:C_ROW + SLOT_TILES], ALU.add).then_inc(tb["step"], 1)
            dve.wait_ge(tb["step"], 10)
            V.tensor_scalar(expert_t[:, :], expert_f[:, :], float(EXPERTS - 1), None, ALU.min)
            dve.wait_ge(tb["step"], 12)
            V.tensor_copy(start_t[:, :], start_f2[:, :]).then_inc(tb["ready"], 1)
            V.scalar_tensor_tensor(shift_r[:, :], upto[:, :], float(P), skip_rows[:, :], ALU.mult, ALU.add).then_inc(tb["place"], 1)
            dve.wait_ge(tb["place"], 1)
            V.scalar_tensor_tensor(shift[:, :], shift_r[:, :], float(REGION), base, ALU.subtract, ALU.subtract).then_inc(tb["place"], 1)
            dve.wait_ge(tb["place"], 2)
            chosen_rows = chosen[:, :, :, :].rearrange("p b r e -> p (b r) e")
            V.tensor_tensor(chosen_rows, chosen_rows, shift[:, :].unsqueeze(1).to_broadcast([P, BATCHES * TILES * TOP_K, EXPERTS]),
                            ALU.mult).then_inc(tb["place"], 1)
            dve.wait_ge(tb["place"], 3)
            V.reduce_sum(shift_of[:, :], chosen_rows, axis=AX.X).then_inc(tb["place"], 1)
            dve.wait_ge(tb["place"], 4)
            V.tensor_tensor(row_all[:, :, :].rearrange("p b r -> p (b r)"), rows_f[:, :, :].rearrange("p b r -> p (b r)"),
                            shift_of[:, :], ALU.add).then_inc(tb["placed"], 1)

            dve.wait_ge(wt["hid_zero"], 1)
            def expert_step(i):
                for j in range(FLY):
                    t = FLY * i + j
                    if live(i, SLOT_TILES // FLY):
                        dve.wait_ge(mo["hi"], t + 1)
                        wait(dve, mo["up"], t - FLY + 1)
                        V.tensor_tensor(rT_lo[:, j, :], ps[:, 0, 0:P], rT_hi[:, j, :].bitcast(fp32),
                                        ALU.subtract).then_inc(mo["lo"], 1)
                    u, ju = t - 1, (j - 1) % FLY
                    if live(u, SLOT_TILES):
                        dve.wait_ge(mo["act1"], u + 1)
                        wait(dve, mo["hid_tr"], u - FLY + 1)
                        V.tensor_tensor(hid[:, ju, 0:HIDDEN], act1[:, ju, :], ps[:, 3 + ju, 0:HIDDEN],
                                        ALU.mult).then_inc(mo["hid"], 1)
                    u, ju = t - 3, j
                    if live(u, SLOT_TILES):
                        dve.wait_ge(mo["hid_tr"], u + 1)
                        wait(dve, mo["down"], u - FLY + 1)
                        V.tensor_copy(hidT[:, ju, :], ps[:, 1, 0:HIDDEN_TILES * P]).then_inc(mo["hidT"], 1)
            steps(dve, SLOT_TILES // FLY, 2, expert_step)

            dve.wait_ge(wt["ff_lo"], 2 * FF_TILES)
            dve.wait_ge(wt["fi_lo"], 1)
            for n, lo in enumerate((fh_lo[:, :, :], fi_lo)):
                last = V.reduce_max(odd[:, n:n + 1], lo.rearrange("p k o -> p (k o)").bitcast(u32), axis=AX.X)
            last.then_inc(wt["odd_any"], 1)
            dve.wait_ge(wt["odd_any"], 1)
            V.tensor_scalar(odd_any[:, :], odd[:, :], 0.0, None, ALU.not_equal).then_inc(wt["odd_any"], 1)
            dve.wait_ge(wt["odd_mm"], 1)
            V.tensor_reduce(odd_i[:, :], ps[0:FEATS, 7, 0:2], axis=AX.X, op=ALU.max).then_inc(wt["odd_i"], 1)

            def high_parts(b, part):
                dve.wait_ge(at["st"], 2 * b + part + 1)
                wait(dve, at["qf"] if part else at["kf"], b)
                n = slice(0, 2) if part else slice(2, 4)
                V.tensor_copy(st_hi[:, n, :], st[:, n, :]).then_inc(at["st_hi"], 1)

            def attention_step(i, meanwhile=None):
                b = i - 1
                if live(b, BATCHES):
                    dve.wait_ge(at["got"], 64 * (b + 1))
                    wait(dve, at["res"], b)
                    V.tensor_tensor(sum1[:, :, :], got[:, :, 0, :], got[:, :, 1, :], ALU.add).then_inc(at["sum1"], 1)
                b = i - 6
                if live(b, BATCHES):
                    dve.wait_ge(at["out"], b + 1)
                    dve.wait_ge(at["kept"], b + 1)
                    wait(dve, at["x3"], b)
                    V.tensor_tensor(f_res, ps[:, 7, 0:SEQ], x_kept[:, b, :], ALU.add).then_inc(at["res3"], 1)
                b = i - 1
                if live(b, BATCHES):
                    dve.wait_ge(at["sum1"], b + 1)
                    wait(dve, at["x2"], b)
                    V.tensor_tensor(res[:, :], sum1[:, :, :].rearrange("p t d -> p (t d)"), x_kept[:, b, :], ALU.add).then_inc(at["res"], 1)
                    dve.wait_ge(at["res"], b + 1)
                    moments(res, stats, mv, TILES, D, at["mv"], b + 1)
                b = i - 6
                if live(b, BATCHES):
                    dve.wait_ge(at["res3"], b + 1)
                    moments(f_res, stats_h, mv_h, TILES, D, at["mv3"], b + 1)
                b = i - 2
                if live(b, BATCHES):
                    dve.wait_ge(at["x2T"], b + 1)
                    wait(dve, at["qk"], b)
                    V.tensor_tensor(x2T_lo[:, :], x2T[:, :], x2T_hi[:, :].bitcast(fp32), ALU.subtract).then_inc(at["lo"], 1)
                if live(i - 3, BATCHES):
                    high_parts(i - 3, 0)
                b = i - 1
                if live(b, BATCHES):
                    dve.wait_ge(at["rstd"], 2 * b + 2)
                    wait(dve, at["kept"], b)
                    wait(dve, at["tr"], b)
                    normalise(x2, res, mv, rstd, TILES, D, at["x2"])
                b = i - 6
                if live(b, BATCHES):
                    dve.wait_ge(at["rstd3"], 2 * b + 2)
                    wait(dve, at["kept3"], b)
                    wait(dve, at["tr3"], b)
                    normalise(x3, f_res, mv_h, rstd_h, TILES, D, at["x3"])
                b = i - 5
                if live(b, BATCHES):
                    dve.wait_ge(at["den"], b + 1)
                    wait(dve, at["att"], b)
                    V.reciprocal(rden[:, :], den[:, :]).then_inc(at["rden"], 1)
                    dve.wait_ge(at["rden"], b + 1)
                    wait(dve, at["out"], b)
                    V.tensor_tensor(att[:, :], ps[:, 7, 0:SEQ], rden[:, :], ALU.mult).then_inc(at["att"], 1)
                if live(i - 3, BATCHES):
                    high_parts(i - 3, 1)
                b = i - 3
                if live(b, BATCHES):
                    dve.wait_ge(at["v_tok"], b + 1)
                    wait(dve, at["kv_mm"], b)
                    V.tensor_copy(v_use[:, :, :], v_tok[:, :, :]).then_inc(at["v_use"], 1)
                b = i - 4
                if live(b, BATCHES):
                    dve.wait_ge(at["kv_mm"], b + 1)
                    wait(dve, at["kv_tr"], b)
                    V.tensor_tensor(kv[:, :, :], ps[:, 6, 0:2 * P].rearrange("p (a f) -> p a f", f=P),
                                    const[:, C_KVMASK:C_KVMASK + P].unsqueeze(1).to_broadcast([P, 2, P]), ALU.mult).then_inc(at["kv"], 1)
                b = i - 2
                if live(b, BATCHES):
                    dve.wait_ge(at["v_mm"], b + 1)
                    wait(dve, at["v_use"], b)
                    V.tensor_tensor(v_tok[:, :, :], ps[:, 3, 0:SEQ].rearrange("p (t d) -> p t d", d=D),
                                    bv[:, :].unsqueeze(1).to_broadcast([P, TILES, D]), ALU.add).then_inc(at["v_tok"], 1)
                if meanwhile:
                    meanwhile()
                b = i - 6
                if live(b, BATCHES):
                    dve.wait_ge(at["x3_hi"], b + 1)
                    V.tensor_tensor(x3T_lo[:, b, :], ps[:, 0, SEQ:], x3T_hi[:, b, :].bitcast(fp32), ALU.subtract).then_inc(at["x3_lo"], 1)

            def mlp_first(i):
                for m in range(FF_TILES):
                    if live(i, BATCHES):
                        n = FF_TILES * i + m
                        dve.wait_ge(ff["silu"], n + 1)
                        wait(dve, ff["a_lo"], n - FF_TILES + 1)
                        V.scalar_tensor_tensor(f_a[:, m, :], ps[:, in_bank[m], SEQ:], ff_s[:, 1, m:m + 1],
                                               f_silu[:, m % 2, :], ALU.mult, ALU.mult).then_inc(ff["act"], 1)

            def mlp_rest(i):
                b = i - 3
                if live(b, BATCHES):
                    dve.wait_ge(ff["out_mm"], b + 1)
                    wait(dve, ff["out"], b)
                    V.tensor_tensor(f_res, ps[:, 0, 0:TILES * D], x_kept[:, b, :], ALU.add).then_inc(ff["res"], 1)
                    dve.wait_ge(ff["res"], b + 1)
                    moments(f_res, stats, mv, TILES, D, ff["mv"], b + 1)
                    dve.wait_ge(ff["rstd"], 2 * b + 2)
                    wait(dve, ff["stored"], 16 * b)
                    normalise(f_out, f_res, mv, rstd, TILES, D, ff["out"])
                b = i - 1
                for m in range(FF_TILES):
                    if live(b, BATCHES):
                        n = FF_TILES * b + m
                        dve.wait_ge(ff["g1"], n + 1)
                        wait(dve, ff["h2_mm"], FF_TILES * b)
                        split(g_hi[:, m, :], g_lo[:, m, :], f_g[:, m, :], ff["g_hi"], ff["g_lo"], n + 1)
                for m in range(FF_TILES):
                    if live(i, BATCHES):
                        n = FF_TILES * i + m
                        dve.wait_ge(ff["act"], n + 1)
                        wait(dve, ff["h1_mm"], FF_TILES * i)
                        V.tensor_copy(a_hi[:, m, :], f_a[:, m, :]).then_inc(ff["a_hi"], 1)

            def mlp_step(i):
                mlp_first(i)
                mlp_rest(i)
            attention_then_mlp(dve, attention_step, mlp_first, mlp_rest)
            steps(dve, BATCHES, MLP_LAG, mlp_step, first=EARLY)

        @block.tensor
        def _(pe):
            mm, transpose = nc.tensor.matmul, nc.tensor.transpose

            def mm3(dst, lhs, rhs, start, stop):
                mm(dst, lhs[0], rhs[0], start=start, stop=False)
                mm(dst, lhs[0], rhs[1], start=False, stop=False)
                return mm(dst, lhs[1], rhs[0], start=False, stop=stop)

            pe.wait_ge(ld["front"], 16 * 3)
            for t in range(2):
                mm(ps[:, t, :], w_h[:, t, :], conv_bd[:, t, :], start=True, stop=True).then_inc(wt["conv_mm"], 1)
            pe.wait_ge(wt["front_hi"], 3)
            pe.wait_ge(wt["front_lo"], 3)

            def small_weights():
                pe.wait_ge(ld["conv"], 16 * 8)
                for t in range(2):
                    last = mm(ps[:, 4, 0:D], cproj[:, t, :], out_wT[:, t, :], start=t == 0, stop=t == 1)
                last.then_inc(wt["small_mm"], 1)
                for t in range(2):
                    last = mm(ps[:, 6, 0:1], fc_wT[:, t, :], ln_gb[:, 2 + t:3 + t], start=t == 0, stop=t == 1)
                last.then_inc(wt["small_mm"], 1)
                pe.wait_ge(wt["cproj_bb"], 2)
                for t in range(2):
                    last = mm(ps[:, 5, 0:D], cproj_bb[:, t, :], out_wT[:, t, :], start=t == 0, stop=t == 1)
                last.then_inc(wt["small_mm"], 1)

            def front(b):
                pe.wait_ge(g0["x_lo"], b + 1)
                wait(pe, g0["gate"], b)
                wait(pe, g0["conv"], b)
                for t in range(TILES):
                    def x_at(tap):
                        cols = slice(t * P + tap, t * P + tap + P)
                        return xT_hi[:, cols], xT_lo[:, cols]
                    both = [w[:, PAD:, :].rearrange("p k o -> p (k o)") for w in (front_hi, front_lo)]
                    mm3(ps[:, t, :], x_at(PAD), both, True, False)
                    for tap in range(PAD):
                        last = mm3(ps[:, t, 0:INNER], x_at(tap), (front_hi[:, tap, :], front_lo[:, tap, :]),
                                   False, tap == PAD - 1)
                last.then_inc(g0["front"], 1)

            def transposes(b):
                pe.wait_ge(g0["hn"], b + 1)
                wait(pe, g0["hT"], b)
                wait(pe, g0["hnT"], b)
                for t in range(TILES):
                    for k in range(2):
                        cols = slice((2 * t + k) * P, (2 * t + k + 1) * P)
                        transpose(ps[:, 2, cols], h[:, t, k * P:(k + 1) * P], ident)
                        last = transpose(ps[:, 3, cols], hn[:, t, k * P:(k + 1) * P], ident)
                last.then_inc(g0["tr"], 1)

            def output(b):
                pe.wait_ge(g0["mid"], b + 1)
                pe.wait_ge(g0["hT"], b + 1)
                wait(pe, g0["res"], b)
                for t in range(TILES):
                    dst = ps[:, 5, t * D:(t + 1) * D]
                    mm(dst, mid[:, t * P:(t + 1) * P], mid_out[:, :], start=True, stop=False)
                    for k in range(2):
                        last = mm(dst, hT[:, t, k * P:(k + 1) * P], out_wT[:, k, :], start=False, stop=k == 1)
                last.then_inc(g0["out"], 1)

            front(0)
            small_weights()

            def conv_step(i):
                if isinstance(i, int) and i == 1:
                    pe.wait_ge(ld["const"], 16)
                    pe.wait_ge(wt["before"], 2)
                    pe.wait_ge(wt["memset"], MEMSETS)
                    pe.wait_ge(wt["small"], 3)
                    pe.wait_ge(wt["fc_g"], 2)
                order = ((transposes, i - 1), (output, i - 2)) if isinstance(i, int) and i >= BATCHES else ((output, i - 2), (transposes, i - 1))
                for stage, b in order:
                    if live(b, BATCHES):
                        stage(b)
                if live(i + 1, BATCHES):
                    front(i + 1)
                b = i - 3
                if live(b, BATCHES):
                    pe.wait_ge(g0["added"], b + 1)
                    wait(pe, g0["rank"], b)
                    dst = ps[:, 7, 32:32 + TILES * EXPERTS]
                    mm(dst, before[:, :], either[:, :, :].rearrange("p t e -> p (t e)"), start=True, stop=False)
                    mm(dst, ones_bf[:, :], earlier[:, :, :].rearrange("p t e -> p (t e)"), start=False, stop=True)\
                        .then_inc(g0["rank_mm"], 1)
                b = i - 2
                if live(b, BATCHES):
                    pe.wait_ge(g0["x1"], b + 1)
                    wait(pe, g0["x1T"], b)
                    wait(pe, g0["top_at"], b)
                    for t in range(TILES):
                        last = transpose(ps[:, 6, t * P:(t + 1) * P], x1[:, t * D:(t + 1) * D], ident)
                    last.then_inc(g0["x1_tr"], 1)
                b = i - 1
                if live(b, BATCHES):
                    pe.wait_ge(g0["hnT"], b + 1)
                    wait(pe, g0["mid"], b)
                    for k in range(2):
                        last = mm(ps[:, 4, 0:SEQ], fc_g[:, k, :], hnT[:, k, :], start=k == 0, stop=k == 1)
                    last.then_inc(g0["fc"], 1)
                b = i - 2
                if live(b, BATCHES):
                    pe.wait_ge(g0["x1T"], b + 1)
                    for t in range(TILES):
                        last = mm(ps[:, 6, SEQ + t * EXPERTS:SEQ + (t + 1) * EXPERTS], x1T[:, t * P:(t + 1) * P], gate_wT[:, :],
                                  start=True, stop=True)
                    last.then_inc(g0["logits"], 1)
            steps(pe, BATCHES, 3, conv_step, ahead=1)

            pe.wait_ge(g0["carry"], BATCHES)
            mm(ps[:, 7, 64:64 + EXPERTS], ones_bf[:, :], earlier[:, 0, :], start=True, stop=True).then_inc(tb["count"], 1)

            pe.wait_ge(tb["ready"], 1)
            pe.wait_ge(wt["moe_lo"], EXPERTS)
            pe.wait_ge(ld["w2"], 16)

            up_reg = [pe.alloc_register(f"expert_up{j}") for j in range(FLY)]

            def expert(reg):
                return pe.snap(reg).with_bounds(min_val=0, max_val=EXPERTS - 1)

            def expert_step(i):
                for j in range(FLY):
                    t = FLY * i + j
                    slot_reg = up_reg[(j - 1) % FLY]
                    if live(t - 4, SLOT_TILES):
                        e_down = expert(slot_reg)
                    if live(t - 1, SLOT_TILES):
                        pe.reg_load(slot_reg, expert_t[0:1, bass.ds(t - 1, 1)])
                        e_up = expert(slot_reg)
                    if live(i, SLOT_TILES // FLY):
                        pe.wait_ge(mo_in[j], 16 * (i + 1))
                        wait(pe, mo["lo"], t)
                        transpose(ps[:, 0, 0:P], rows_in[:, j, :], ident).then_inc(mo["tr"], 1)
                    u, ju = t - 1, (j - 1) % FLY
                    if live(u, SLOT_TILES):
                        pe.wait_ge(mo["lo"], u + 1)
                        wait(pe, mo["act1"], u)
                        wait(pe, mo["hid"], u - FLY + 1)
                        for w in range(2):
                            cols = slice(w * HIDDEN, (w + 1) * HIDDEN)
                            last = mm3(ps[:, 3 + ju if w else 2, 0:HIDDEN], (rT_hi[:, ju, :], rT_lo[:, ju, :]),
                                       (w13_hi[:, e_up, cols], w13_lo[:, e_up, cols]), True, True)
                        last.then_inc(mo["up"], 1)
                    u, ju = t - 3, j
                    if live(u, SLOT_TILES):
                        pe.wait_ge(mo["hid"], u + 1)
                        wait(pe, mo["hidT"], u)
                        for k in range(HIDDEN_TILES):
                            last = transpose(ps[:, 1, k * P:(k + 1) * P], hid[:, ju, k * P:(k + 1) * P], ident)
                        last.then_inc(mo["hid_tr"], 1)
                    u, ju = t - 4, (j - 4) % FLY
                    if live(u, SLOT_TILES):
                        pe.wait_ge(mo["hidT"], u + 1)
                        wait(pe, mo["out"], u)
                        for k in range(HIDDEN_TILES):
                            last = mm(ps[:, 6, 0:D], hidT[:, ju, k * P:(k + 1) * P], w2[:, e_down, k, :],
                                      start=k == 0, stop=k == HIDDEN_TILES - 1)
                        last.then_inc(mo["down"], 1)
            steps(pe, SLOT_TILES // FLY, 2, expert_step)

            pe.wait_ge(wt["att_lo"], 2)
            pe.wait_ge(mo["out"], SLOT_TILES)
            pe.wait_ge(wt["odd_any"], 2)
            mm(ps[0:FEATS, 7, 0:2], ones[:, :], odd_any[:, :], start=True, stop=True).then_inc(wt["odd_mm"], 1)
            pe.wait_ge(wt["odd_i"], 1)
            n_odd = pe.value_load(odd_i[0:1, 0:1], min_val=0, max_val=P)

            def attention_step(i, meanwhile=None):
                b = i - 4
                if live(b, BATCHES):
                    pe.wait_ge(at["st_lo"], 2 * b + 1)
                    wait(pe, at["qp"], b)
                    for t in range(TILES):
                        cols = slice(t * P, (t + 1) * P)
                        for n in range(2):
                            last = mm3(ps[:, 4 + t, n * 256:(n + 1) * 256], (st_hi[:, 2 + n, cols], st_lo[:, 2 + n, cols]),
                                       (om_hi[:, :], om_lo[:, :]), True, True)
                    last.then_inc(at["kf"], 1)
                b = i - 2
                if live(b, BATCHES):
                    pe.wait_ge(at["x2T"], b + 1)
                    wait(pe, at["v_tok"], b)
                    for t in range(TILES):
                        last = mm(ps[:, 3, t * D:(t + 1) * D], x2T[:, t * P:(t + 1) * P], wv[:, :], start=True, stop=True)
                    last.then_inc(at["v_mm"], 1)
                b = i - 5
                if live(b, BATCHES):
                    pe.wait_ge(at["kvT"], b + 1)
                    pe.wait_ge(at["qp"], b + 1)
                    wait(pe, at["res3"], b)
                    for a in range(2):
                        for g in range(HEAD_GROUPS):
                            last = mm(ps[32 * g:32 * g + 32, 7, a * SEQ:(a + 1) * SEQ], kvT[:, a, 32 * g:32 * g + 32],
                                      qp[:, g, :], start=True, stop=True)
                    last.then_inc(at["nd"], 1)
                b = i - 4
                if live(b, BATCHES):
                    pe.wait_ge(at["st_lo"], 2 * b + 2)
                    pe.wait_ge(at["kp"], b + 1)
                    for g in range(HEAD_GROUPS):
                        cols = slice((g % 2) * P, (g % 2 + 1) * P)
                        last = mm3(ps[:, 4 + g // 2, (g % 2) * SEQ:(g % 2 + 1) * SEQ], (om_hi[:, cols], om_lo[:, cols]),
                                   (st_hi[:, g // 2, :], st_lo[:, g // 2, :]), True, True)
                    last.then_inc(at["qf"], 1)
                b = i - 4
                if live(b, BATCHES):
                    pe.wait_ge(at["kp"], b + 1)
                    pe.wait_ge(at["v_use"], b + 1)
                    wait(pe, at["kv"], b)
                    wait(pe, at["kvT"], b)
                    for a in range(2):
                        for t in range(TILES):
                            for g in range(HEAD_GROUPS):
                                lhs = ones[:, 0:32] if a else v_use[:, t, 32 * g:32 * g + 32]
                                last = mm(ps[32 * g:32 * g + 32, 6, a * P:(a + 1) * P], lhs, kp[:, t, g * P:(g + 1) * P],
                                          start=t == 0, stop=t == TILES - 1)
                    last.then_inc(at["kv_mm"], 1)
                b = i - 1
                if live(b, BATCHES):
                    pe.wait_ge(at["x2"], b + 1)
                    wait(pe, at["x2T"], b)
                    wait(pe, at["x3_lo"], b - 5)
                    for t in range(TILES):
                        last = transpose(ps[:, 0, t * P:(t + 1) * P], x2[:, t * D:(t + 1) * D], ident)
                    last.then_inc(at["tr"], 1)
                b = i - 2
                if live(b, BATCHES):
                    pe.wait_ge(at["lo"], b + 1)
                    wait(pe, at["st"], 2 * b)
                    for n in range(4):
                        last = mm3(ps[:, 1 + n // 2, (n % 2) * SEQ:(n % 2 + 1) * SEQ], (qk_hi[:, n, :], qk_lo[:, n, :]),
                                   (x2T_hi[:, :], x2T_lo[:, :]), True, True)
                    last.then_inc(at["qk"], 1)
                b = i - 4
                if live(b, BATCHES):
                    pe.wait_ge(at["kv"], b + 1)
                    wait(pe, at["kvT"], b)
                    for a in range(2):
                        last = transpose(ps[:, 6, (2 + a) * P:(3 + a) * P], kv[:, a, :], ident)
                    last.then_inc(at["kv_tr"], 1)
                if meanwhile:
                    meanwhile()
                b = i - 6
                if live(b, BATCHES):
                    pe.wait_ge(at["x3"], b + 1)
                    if live(i - 1, BATCHES):
                        pe.wait_ge(at["x2T"], i)
                    for t in range(TILES):
                        last = transpose(ps[:, 0, SEQ + t * P:SEQ + (t + 1) * P], x3[:, t * D:(t + 1) * D], ident)
                    last.then_inc(at["tr3"], 1)
                b = i - 5
                if live(b, BATCHES):
                    pe.wait_ge(at["att"], b + 1)
                    for t in range(TILES):
                        dst = ps[:, 7, t * D:(t + 1) * D]
                        mm(dst, first_row, bout[:, :], start=True, stop=False)
                        last = mm(dst, att[:, t * P:(t + 1) * P], wout[:, :], start=False, stop=True)
                    last.then_inc(at["out"], 1)

            def mlp_product(dst, w_hi, w_lo, x_hi, x_lo, start, stop, exact):
                mm(dst, w_hi, x_hi, start=start, stop=False)
                last = mm(dst, w_hi, x_lo, start=False, stop=stop and exact)
                return last if exact else mm(dst, w_lo, x_hi, start=False, stop=stop)

            def first_layer(i, tiles, exact):
                pe.wait_ge(at["x3_lo"], i + 1)
                for m in tiles:
                    n = FF_TILES * i + m
                    wait(pe, ff["act"], (n, n - 3, n - 3, n - 2)[m])
                    for w in range(2):
                        rows = slice(m * P, (m + 1) * P)
                        last = mlp_product(ps[:, in_bank[m], w * SEQ:(w + 1) * SEQ], fi_hi[:, w, rows], fi_lo[:, w, rows],
                                           x3T_hi[:, i, :], x3T_lo[:, i, :], True, True, exact)
                    last.then_inc(ff["in_mm"], 1)

            def square_layer(layer, b, tiles, bank, x_hi, x_lo, ready, read, done, exact):
                if not live(b, BATCHES):
                    return
                pe.wait_ge(ready, FF_TILES * (b + 1))
                for m in tiles:
                    rows = slice(m * P, (m + 1) * P)
                    wait(pe, read, FF_TILES * b + (m - 1 if m >= 2 else 0))
                    for k in range(FF_TILES):
                        row = layer * FF_TILES + k
                        last = mlp_product(half_bank(bank, m), fh_hi[:, row, rows], fh_lo[:, row, rows],
                                           x_hi[:, k, :], x_lo[:, k, :], k == 0, k == FF_TILES - 1, exact)
                    last.then_inc(done, 1)

            def second_layer(b, tiles, exact):
                square_layer(0, b, tiles, 4, a_hi, a_lo, ff["a_lo"], ff["g1"], ff["h1_mm"], exact)

            def third_layer(b, tiles, exact):
                square_layer(1, b, tiles, 6, g_hi, g_lo, ff["g_lo"], ff["g2"], ff["h2_mm"], exact)

            def output_layer(b):
                pe.wait_ge(ff["g2"], FF_TILES * (b + 1))
                wait(pe, ff["res"], b)
                for t in range(TILES):
                    for k in range(FF_TILES):
                        last = mm(ps[:, 0, t * D:(t + 1) * D], f_last[:, k, t * P:(t + 1) * P], ff_out_w[:, k, :],
                                  start=k == 0, stop=k == FF_TILES - 1)
                last.then_inc(ff["out_mm"], 1)

            def mlp_first(i, exact=False):
                if isinstance(i, int) and i == 0:
                    pe.wait_ge(wt["ff_lo"], 2 * FF_TILES)
                    pe.wait_ge(wt["fi_lo"], 1)
                    pe.wait_ge(wt["ff_out"], 1)
                    pe.wait_ge(at["st"], 2 * BATCHES)
                    pe.wait_ge(at["v_tok"], BATCHES)
                if live(i, BATCHES):
                    first_layer(i, range(FF_TILES - 1), exact)

            def mlp_rest(i, exact=False):
                if isinstance(i, int) and i == 1:
                    pe.wait_ge(at["qp"], BATCHES)
                if isinstance(i, int) and i == 2:
                    pe.wait_ge(at["kvT"], BATCHES)
                    pe.wait_ge(at["res3"], BATCHES)
                if isinstance(i, int) and i == 3:
                    pe.wait_ge(at["x3_lo"], BATCHES)
                if live(i - 3, BATCHES):
                    output_layer(i - 3)
                third_layer(i - 2, (0,), exact)
                if live(i, BATCHES):
                    first_layer(i, (FF_TILES - 1,), exact)
                third_layer(i - 2, (1,), exact)
                second_layer(i - 1, (0, 1), exact)
                third_layer(i - 2, (2, 3), exact)
                second_layer(i - 1, (2, 3), exact)

            def mlp_step(i, exact):
                mlp_first(i, exact)
                mlp_rest(i, exact)

            attention_then_mlp(pe, attention_step, mlp_first, mlp_rest)
            with pe.If(n_odd == 0):
                steps(pe, BATCHES, MLP_LAG, lambda i: mlp_step(i, True), first=EARLY)
            with pe.Else():
                steps(pe, BATCHES, MLP_LAG, lambda i: mlp_step(i, False), first=EARLY)


def layouts(a):
    f = np.float32
    tiled = lambda w: np.ascontiguousarray(w.reshape(-1, P, w.shape[-1]).transpose(1, 0, 2))
    cols = lambda v: np.ascontiguousarray(v.reshape(-1, P).T)
    rows = lambda v: np.ascontiguousarray(np.broadcast_to(v[None, :], (P, v.shape[0])))
    A = {}
    x = a["L0_attn_hidden_states"]
    A["x_tok"] = np.ascontiguousarray(x.reshape(BATCHES, TILES, P, D).transpose(2, 0, 1, 3).reshape(P, BATCHES, TILES * D))
    xT = np.zeros((D, BATCHES, PAD + SEQ), f)
    xT[:, :, PAD:] = x.transpose(2, 0, 1)
    A["xT"] = xT
    w = a["L0_attn_in_proj_w"]
    A["w_h"] = tiled(w[:INNER])
    A["w_gate"] = np.ascontiguousarray(w[INNER:].T)
    width = INNER // GROUPS
    bd = np.zeros((2, P, TAPS, P), f)
    for o in range(INNER):
        t, g = o // P, o % P // width
        bd[t, g * width:(g + 1) * width, :, o % P] = a["L0_attn_conv_w"][o]
    A["conv_bd"] = np.ascontiguousarray(bd.reshape(2, P, TAPS * P).transpose(1, 0, 2))
    A["conv_b"] = rows(a["L0_attn_conv_b"])
    A["fc_wT"] = tiled(np.ascontiguousarray(a["L0_attn_fc_w"].T))
    A["ln_gb"] = np.ascontiguousarray(np.concatenate([cols(a["L0_attn_ln_g"]), cols(a["L0_attn_ln_b"])], 1))
    A["fc_b"] = cols(a["L0_attn_fc_b"])
    A["cproj"] = tiled(a["L0_attn_cproj_w"])
    A["cproj_b"] = cols(a["L0_attn_cproj_b"])
    A["out_wT"] = tiled(np.ascontiguousarray(a["L0_attn_out_w"].T))
    A["gate_wT"] = np.ascontiguousarray(a["L0_ffn_gate_w"].T)
    A["w13"] = np.ascontiguousarray(np.concatenate([a["L0_ffn_w1"], a["L0_ffn_w3"]], 2).transpose(1, 0, 2))
    w2 = np.zeros((EXPERTS, HIDDEN_TILES * P, D), f)
    w2[:, :HIDDEN] = a["L0_ffn_w2"]
    A["w2"] = np.ascontiguousarray(w2.reshape(EXPERTS, HIDDEN_TILES, P, D).transpose(2, 0, 1, 3))
    wq, bq = a["L1_attn_Wqkv"], a["L1_attn_bqkv"]
    half = D // 2
    starts = [0, half, D, D + half]
    A["qk_w"] = np.ascontiguousarray(np.stack([np.tile(wq[:, s:s + half], (1, 2)) for s in starts], 1))
    A["qk_b"] = np.ascontiguousarray(np.stack([np.tile(bq[s:s + half], 2) for s in starts], 1))
    A["wv"] = np.ascontiguousarray(wq[:, 2 * D:])
    A["bv"] = rows(bq[2 * D:])
    om = np.zeros((P, 2 * P), f)
    for n in range(HEADS // 2):
        om[n * HEAD_DIM:(n + 1) * HEAD_DIM, n * FEATS:(n + 1) * FEATS] = a["L1_attn_omega"]
        om[half + n * HEAD_DIM:half + (n + 1) * HEAD_DIM, n * FEATS:(n + 1) * FEATS] = -0.5
    A["omega"] = om
    A["wout"] = np.ascontiguousarray(a["L1_attn_Wout"])
    A["bout"] = rows(a["L1_attn_bout"])
    A["ff_in"] = np.ascontiguousarray(np.stack([a["L1_ffn_w1_w"].T, a["L1_ffn_w2_w"].T], 1))
    A["ff_h"] = np.ascontiguousarray(np.concatenate([tiled(np.ascontiguousarray(a[n].T)) for n in ("L1_ffn_h1_w", "L1_ffn_h2_w")], 1))
    A["ff_s"] = np.ascontiguousarray(np.stack([cols(a[f"L1_ffn_{n}_s"]) for n in ("w1", "w2", "h1", "h2")], 1))
    A["ff_out"] = tiled(np.ascontiguousarray(a["L1_ffn_w3_w"].T))
    A["ff_out_s"] = rows(a["L1_ffn_w3_s"])
    c = np.zeros((P, C_ALL), f)
    c[:, C_IDENT:C_IDENT + P] = np.eye(P)
    c[:, C_BEFORE:C_BEFORE + P] = np.triu(np.ones((P, P)), 1)
    own = np.arange(P) % 32 // HEAD_DIM
    c[:, C_KVMASK:C_KVMASK + P] = own[:, None] == np.arange(P)[None, :] // FEATS
    c[:, C_IOTA:C_IOTA + EXPERTS] = np.arange(EXPERTS)
    c[:, C_BASE:C_BASE + EXPERTS] = np.arange(EXPERTS) * REGION
    c[:, C_UPTO:C_TILE] = np.tril(np.ones((EXPERTS, EXPERTS))).reshape(-1)
    c[:, C_TILE:C_ROW] = np.arange(SLOT_TILES)
    c[:, C_ROW:C_FIRST] = np.arange(SLOT_TILES) * P
    c[0, C_FIRST:] = 1
    A["const"] = c
    return A


def kernel(**inputs):
    import concourse.bacc as bacc
    from concourse.bass_utils import run_bass_kernel_spmd

    nc = bacc.Bacc("TRN2", target_bir_lowering=False, num_devices=1)
    laid = layouts({n: np.asarray(v) for n, v in inputs.items()})
    arrays, A = {}, {}
    for name, a in laid.items():
        arrays[f"in_{name}"] = a
        A[name] = nc.dram_tensor(f"in_{name}", a.shape, mybir.dt.from_np(a.dtype), kind="ExternalInput").ap()
    out = nc.dram_tensor("out", [TOKENS, D], mybir.dt.float32, kind="ExternalOutput").ap()
    build(nc, A, out)
    r = run_bass_kernel_spmd(nc, [arrays], core_ids=[0])
    return r.results[0]["out"].reshape(BATCHES, SEQ, D)
```
